# Optimizing a Trainium2 kernel written in Bass

```python
import numpy as np
import jax
import jax.numpy as jnp

def _softmax(x, axis=-1):
    return jax.nn.softmax(x, axis=axis)

def _gelu(x):
    return jax.nn.gelu(x, approximate=True)

def _silu(x):
    return jax.nn.silu(x)

def _sigmoid(x):
    return jax.nn.sigmoid(x)

def _layernorm(x, axis=-1, eps=1e-05):
    m = jnp.mean(x, axis=axis, keepdims=True)
    v = jnp.var(x, axis=axis, keepdims=True)
    return (x - m) / jnp.sqrt(v + eps)

def _scatter_add(tgt, idx, src, axis=0):
    return tgt.at[idx].add(src)

def _segment_sum(src, seg, n):
    return jax.ops.segment_sum(src, seg, n)
kernel_name = 'mk_gnn_preln_d4_gnn_r32_f7287e'

def setup_inputs(seed: int=0):
    np.random.seed(seed)
    _w = jnp.asarray

    def _rec_inputs():
        import jax
        import jax.numpy as jnp
        _gk = jax.random.key(seed)
        x = -0.000202 + 1 * jax.random.normal(jax.random.fold_in(_gk, 1), (50000, 128), jnp.float32)
        src = jax.random.randint(jax.random.fold_in(_gk, 2), (25000,), 0, 50000, jnp.int32)
        dst = jnp.minimum((50000 * jax.random.uniform(jax.random.fold_in(_gk, 3), (25000,)) ** 2.0).astype(jnp.int32), 49999)
        _o = jnp.argsort(dst, stable=True)
        src = src[_o]
        dst = dst[_o]
        edge_attr_128 = -8.16379e-05 + 0.999858 * jax.random.normal(jax.random.fold_in(_gk, 12), (25000, 128), jnp.float32)
        return (x, src, dst, edge_attr_128)
    x, src, dst, edge_attr_128 = _rec_inputs()

    def _L0_gnn_setup():
        import jax, jax.numpy as jnp
        import numpy as np
        N = 50000
        E = 18750
        IN_CH = 128
        HEADS = 8
        HEAD_DIM = 16
        OUT_CH = 128
        NEG_SLOPE = 0.2
        LN_EPS = 1e-05
        key = jax.random.key(seed)
        ks = jax.random.split(key, 9)
        x = jax.random.normal(ks[0], (N, IN_CH), dtype=jnp.float32)
        edge_index = jax.random.randint(ks[1], (2, E), 0, N, dtype=jnp.int64)
        lin_w = jax.random.normal(ks[2], (HEADS * HEAD_DIM, IN_CH), dtype=jnp.float32) * 0.05
        att_src = jax.random.normal(ks[3], (1, HEADS, HEAD_DIM), dtype=jnp.float32) * 0.1
        att_dst = jax.random.normal(ks[4], (1, HEADS, HEAD_DIM), dtype=jnp.float32) * 0.1
        gat_bias = jnp.zeros((HEADS * HEAD_DIM,), dtype=jnp.float32)
        proj_w = jax.random.normal(ks[5], (OUT_CH, HEADS * HEAD_DIM), dtype=jnp.float32) * 0.05
        proj_b = jnp.zeros((OUT_CH,), dtype=jnp.float32)
        ln_gamma = jnp.ones((OUT_CH,), dtype=jnp.float32)
        ln_beta = jnp.zeros((OUT_CH,), dtype=jnp.float32)
        return {'x': x, 'edge_index': edge_index, 'lin_w': lin_w, 'att_src': att_src, 'att_dst': att_dst, 'gat_bias': gat_bias, 'proj_w': proj_w, 'proj_b': proj_b, 'ln_gamma': ln_gamma, 'ln_beta': ln_beta}
    _L0_gnn_all = _L0_gnn_setup()
    _L0_gnn_in = {k: v for k, v in _L0_gnn_all.items() if k in ('lin_w', 'att_src', 'att_dst', 'gat_bias', 'proj_w', 'proj_b', 'ln_gamma', 'ln_beta')}
    del _L0_gnn_all

    def _L1_gnn_setup():
        import jax, jax.numpy as jnp
        import numpy as np
        N_ATOMS = 10000
        N_EDGES = 20000
        IN_F = 128
        OUT_F = 128
        key = jax.random.key(seed)
        k1, k2, k3, k4, k5, k6 = jax.random.split(key, 6)
        atom_features = jax.random.normal(k1, (N_ATOMS, IN_F), dtype=jnp.float32)
        edge_indices = jax.random.randint(k2, (2, N_EDGES), 0, N_ATOMS, dtype=jnp.int64)
        bm_lim = 1.0 / np.sqrt(IN_F * 2)
        bu_lim = 1.0 / np.sqrt(IN_F + OUT_F)
        W_msg = jax.random.uniform(k3, (IN_F * 2, OUT_F), jnp.float32, -bm_lim, bm_lim)
        b_msg = jax.random.uniform(k4, (OUT_F,), jnp.float32, -bm_lim, bm_lim)
        W_upd = jax.random.uniform(k5, (IN_F + OUT_F, OUT_F), jnp.float32, -bu_lim, bu_lim)
        b_upd = jax.random.uniform(k6, (OUT_F,), jnp.float32, -bu_lim, bu_lim)
        return {'atom_features': atom_features, 'edge_indices': edge_indices, 'W_msg': W_msg, 'b_msg': b_msg, 'W_upd': W_upd, 'b_upd': b_upd}
    _L1_gnn_all = _L1_gnn_setup()
    _L1_gnn_in = {k: v for k, v in _L1_gnn_all.items() if k in ('W_msg', 'b_msg', 'W_upd', 'b_upd')}
    del _L1_gnn_all

    def _L2_gnn_setup():
        import jax, jax.numpy as jnp
        import numpy as np
        N_NODES = 50000
        N_EDGES = 25000
        D_FEAT = 128
        N_HEADS = 4
        HEAD_DIM = 32

        def mish(x):
            return x * jnp.tanh(jax.nn.softplus(x))
        key = jax.random.key(seed)
        ks = jax.random.split(key, 12)
        s = 1.0 / np.sqrt(D_FEAT)
        return {'nodes': jax.random.normal(ks[0], (N_NODES, D_FEAT), jnp.float32), 'edges': jax.random.normal(ks[1], (N_EDGES, D_FEAT), jnp.float32), 'Ws_k': jax.random.normal(ks[2], (D_FEAT, N_HEADS, HEAD_DIM), jnp.float32) * s, 'Ws_b': jnp.zeros((N_HEADS, HEAD_DIM), jnp.float32), 'Wr_k': jax.random.normal(ks[3], (D_FEAT, N_HEADS, HEAD_DIM), jnp.float32) * s, 'Wr_b': jnp.zeros((N_HEADS, HEAD_DIM), jnp.float32), 'We_k': jax.random.normal(ks[4], (D_FEAT, N_HEADS, HEAD_DIM), jnp.float32) * s, 'We_b': jnp.zeros((N_HEADS, HEAD_DIM), jnp.float32), 'attn_w': jax.random.normal(ks[5], (HEAD_DIM, 1), jnp.float32) / np.sqrt(HEAD_DIM), 'attn_b': jnp.zeros((1,), jnp.float32), 'senders': jax.random.randint(ks[6], (N_EDGES,), 0, N_NODES, jnp.int32), 'receivers': jax.random.randint(ks[7], (N_EDGES,), 0, N_NODES, jnp.int32)}
    _L2_gnn_all = _L2_gnn_setup()
    _L2_gnn_in = {k: v for k, v in _L2_gnn_all.items() if k in ('Ws_k', 'Ws_b', 'Wr_k', 'Wr_b', 'We_k', 'We_b', 'attn_w', 'attn_b')}
    del _L2_gnn_all

    def _L3_gnn_setup():
        import jax, jax.numpy as jnp
        import numpy as np
        N = 50000
        E = 25000
        F = 128
        COMP_RATIO = 4

        def _sage_mean(x, src, dst, w_self, w_neigh, b):
            n = x.shape[0]
            msg = x[src]
            summed = jax.ops.segment_sum(msg, dst, num_segments=n)
            deg = jax.ops.segment_sum(jnp.ones((src.shape[0],), x.dtype), dst, num_segments=n)
            mean = summed / jnp.maximum(deg, 1.0)[:, None]
            return x @ w_self + mean @ w_neigh + b
        key = jax.random.key(seed)
        ks = jax.random.split(key, 16)
        s = 1.0 / np.sqrt(F)
        inp = {'x': jax.random.normal(ks[0], (N, F), jnp.float32), 'src': jax.random.randint(ks[1], (E,), 0, N, jnp.int32), 'dst': jax.random.randint(ks[2], (E,), 0, N, jnp.int32), 'ws1': jax.random.normal(ks[3], (F, F), jnp.float32) * s, 'wn1': jax.random.normal(ks[4], (F, F), jnp.float32) * s, 'b1': jnp.zeros((F,), jnp.float32), 'ws2': jax.random.normal(ks[5], (F, F), jnp.float32) * s, 'wn2': jax.random.normal(ks[6], (F, F), jnp.float32) * s, 'b2': jnp.zeros((F,), jnp.float32), 'w_score': jax.random.normal(ks[7], (F, 1), jnp.float32) * s, 'b_score': jnp.zeros((1,), jnp.float32), 'wu1': jax.random.normal(ks[8], (F, F), jnp.float32) * s, 'wnu1': jax.random.normal(ks[9], (F, F), jnp.float32) * s, 'bu1': jnp.zeros((F,), jnp.float32), 'wu2': jax.random.normal(ks[10], (F, F), jnp.float32) * s, 'wnu2': jax.random.normal(ks[11], (F, F), jnp.float32) * s, 'bu2': jnp.zeros((F,), jnp.float32)}
        return inp
    _L3_gnn_all = _L3_gnn_setup()
    _L3_gnn_in = {k: v for k, v in _L3_gnn_all.items() if k in ('ws1', 'wn1', 'b1', 'ws2', 'wn2', 'b2', 'w_score', 'b_score', 'wu1', 'wnu1', 'bu1', 'wu2', 'wnu2', 'bu2')}
    del _L3_gnn_all
    return {'x': x, 'src': src, 'dst': dst, 'edge_attr_128': edge_attr_128, 'L0_gnn_lin_w': _L0_gnn_in['lin_w'], 'L0_gnn_att_src': _L0_gnn_in['att_src'], 'L0_gnn_att_dst': _L0_gnn_in['att_dst'], 'L0_gnn_gat_bias': _L0_gnn_in['gat_bias'], 'L0_gnn_proj_w': _L0_gnn_in['proj_w'], 'L0_gnn_proj_b': _L0_gnn_in['proj_b'], 'L0_gnn_ln_gamma': _L0_gnn_in['ln_gamma'], 'L0_gnn_ln_beta': _L0_gnn_in['ln_beta'], 'L1_gnn_W_msg': _L1_gnn_in['W_msg'], 'L1_gnn_b_msg': _L1_gnn_in['b_msg'], 'L1_gnn_W_upd': _L1_gnn_in['W_upd'], 'L1_gnn_b_upd': _L1_gnn_in['b_upd'], 'L2_gnn_Ws_k': _L2_gnn_in['Ws_k'], 'L2_gnn_Ws_b': _L2_gnn_in['Ws_b'], 'L2_gnn_Wr_k': _L2_gnn_in['Wr_k'], 'L2_gnn_Wr_b': _L2_gnn_in['Wr_b'], 'L2_gnn_We_k': _L2_gnn_in['We_k'], 'L2_gnn_We_b': _L2_gnn_in['We_b'], 'L2_gnn_attn_w': _L2_gnn_in['attn_w'], 'L2_gnn_attn_b': _L2_gnn_in['attn_b'], 'L3_gnn_ws1': _L3_gnn_in['ws1'], 'L3_gnn_wn1': _L3_gnn_in['wn1'], 'L3_gnn_b1': _L3_gnn_in['b1'], 'L3_gnn_ws2': _L3_gnn_in['ws2'], 'L3_gnn_wn2': _L3_gnn_in['wn2'], 'L3_gnn_b2': _L3_gnn_in['b2'], 'L3_gnn_w_score': _L3_gnn_in['w_score'], 'L3_gnn_b_score': _L3_gnn_in['b_score'], 'L3_gnn_wu1': _L3_gnn_in['wu1'], 'L3_gnn_wnu1': _L3_gnn_in['wnu1'], 'L3_gnn_bu1': _L3_gnn_in['bu1'], 'L3_gnn_wu2': _L3_gnn_in['wu2'], 'L3_gnn_wnu2': _L3_gnn_in['wnu2'], 'L3_gnn_bu2': _L3_gnn_in['bu2']}

def reference(x, src, dst, edge_attr_128, L0_gnn_lin_w, L0_gnn_att_src, L0_gnn_att_dst, L0_gnn_gat_bias, L0_gnn_proj_w, L0_gnn_proj_b, L0_gnn_ln_gamma, L0_gnn_ln_beta, L1_gnn_W_msg, L1_gnn_b_msg, L1_gnn_W_upd, L1_gnn_b_upd, L2_gnn_Ws_k, L2_gnn_Ws_b, L2_gnn_Wr_k, L2_gnn_Wr_b, L2_gnn_We_k, L2_gnn_We_b, L2_gnn_attn_w, L2_gnn_attn_b, L3_gnn_ws1, L3_gnn_wn1, L3_gnn_b1, L3_gnn_ws2, L3_gnn_wn2, L3_gnn_b2, L3_gnn_w_score, L3_gnn_b_score, L3_gnn_wu1, L3_gnn_wnu1, L3_gnn_bu1, L3_gnn_wu2, L3_gnn_wnu2, L3_gnn_bu2):
    import jax
    import jax.numpy as jnp

    def _L0_gnn_ref(x, edge_index, lin_w, att_src, att_dst, gat_bias, proj_w, proj_b, ln_gamma, ln_beta):
        import jax, jax.numpy as jnp
        import numpy as np
        N = 50000
        E = 18750
        IN_CH = 128
        HEADS = 8
        HEAD_DIM = 16
        OUT_CH = 128
        NEG_SLOPE = 0.2
        LN_EPS = 1e-05
        n = x.shape[0]
        h = (x @ lin_w.T).reshape(n, HEADS, HEAD_DIM)
        a_src = (h * att_src).sum(-1)
        a_dst = (h * att_dst).sum(-1)
        loops = jnp.arange(n, dtype=edge_index.dtype)
        src = jnp.concatenate([edge_index[0], loops])
        dst = jnp.concatenate([edge_index[1], loops])
        logits = jax.nn.leaky_relu(a_src[src] + a_dst[dst], NEG_SLOPE)
        seg_max = jax.ops.segment_max(logits, dst, num_segments=n)
        e = jnp.exp(logits - seg_max[dst])
        denom = jax.ops.segment_sum(e, dst, num_segments=n)
        alpha = e / denom[dst]
        agg = jax.ops.segment_sum(h[src] * alpha[:, :, None], dst, num_segments=n)
        gat_out = agg.reshape(n, HEADS * HEAD_DIM) + gat_bias
        out = gat_out @ proj_w.T + proj_b
        mu = out.mean(-1, keepdims=True)
        var = ((out - mu) ** 2).mean(-1, keepdims=True)
        out = (out - mu) * jax.lax.rsqrt(var + LN_EPS) * ln_gamma + ln_beta
        return out

    def _L1_gnn_ref(atom_features, edge_indices, W_msg, b_msg, W_upd, b_upd):
        import jax, jax.numpy as jnp
        import numpy as np
        N_ATOMS = 10000
        N_EDGES = 20000
        IN_F = 128
        OUT_F = 128
        src, dst = (edge_indices[0], edge_indices[1])
        edge_in = jnp.concatenate([atom_features[src], atom_features[dst]], axis=-1)
        messages = edge_in @ W_msg + b_msg
        agg = jax.ops.segment_sum(messages, dst, num_segments=atom_features.shape[0])
        upd_in = jnp.concatenate([atom_features, agg], axis=-1)
        return upd_in @ W_upd + b_upd

    def _L2_gnn_ref(nodes, edges, Ws_k, Ws_b, Wr_k, Wr_b, We_k, We_b, attn_w, attn_b, senders, receivers):
        import jax, jax.numpy as jnp
        import numpy as np
        N_NODES = 50000
        N_EDGES = 25000
        D_FEAT = 128
        N_HEADS = 4
        HEAD_DIM = 32

        def mish(x):
            return x * jnp.tanh(jax.nn.softplus(x))
        n = nodes.shape[0]
        sent = jnp.einsum('ef,fhd->ehd', nodes[senders], Ws_k) + Ws_b
        e_att = sent + jnp.einsum('ef,fhd->ehd', edges, We_k) + We_b
        recv = jnp.einsum('ef,fhd->ehd', nodes[receivers], Wr_k) + Wr_b
        logits = jnp.einsum('ehd,do->eho', mish(e_att + recv), attn_w) + attn_b
        seg_max = jax.ops.segment_max(logits, receivers, num_segments=n)
        w = jnp.exp(logits - seg_max[receivers])
        denom = jax.ops.segment_sum(w, receivers, num_segments=n)
        w = w / denom[receivers]
        msg = (w * e_att).reshape(e_att.shape[0], N_HEADS * HEAD_DIM)
        out_nodes = jax.ops.segment_sum(msg, receivers, num_segments=n)
        return out_nodes

    def _L3_gnn_ref(x, src, dst, ws1, wn1, b1, ws2, wn2, b2, w_score, b_score, wu1, wnu1, bu1, wu2, wnu2, bu2):
        import jax, jax.numpy as jnp
        import numpy as np
        N = 50000
        E = 25000
        F = 128
        COMP_RATIO = 4

        def _sage_mean(x, src, dst, w_self, w_neigh, b):
            n = x.shape[0]
            msg = x[src]
            summed = jax.ops.segment_sum(msg, dst, num_segments=n)
            deg = jax.ops.segment_sum(jnp.ones((src.shape[0],), x.dtype), dst, num_segments=n)
            mean = summed / jnp.maximum(deg, 1.0)[:, None]
            return x @ w_self + mean @ w_neigh + b
        n = x.shape[0]
        k = max(1, n // COMP_RATIO)
        h = jax.nn.relu(_sage_mean(x, src, dst, ws1, wn1, b1))
        h = _sage_mean(h, src, dst, ws2, wn2, b2)
        score = jax.nn.sigmoid(h @ w_score + b_score)[:, 0]
        _, idx = jax.lax.top_k(score, k)
        compressed = h[idx]
        new_val = jnp.zeros((n, h.shape[1]), h.dtype).at[idx].set(compressed)
        d = jax.nn.relu(_sage_mean(new_val, src, dst, wu1, wnu1, bu1))
        d = _sage_mean(d, src, dst, wu2, wnu2, bu2)
        return d
    edge_index = jnp.stack([src, dst])
    h = jnp.maximum(_layernorm(x, axis=-1), 0.0)
    x = x + _L0_gnn_ref(h, edge_index, L0_gnn_lin_w, L0_gnn_att_src, L0_gnn_att_dst, L0_gnn_gat_bias, L0_gnn_proj_w, L0_gnn_proj_b, L0_gnn_ln_gamma, L0_gnn_ln_beta)
    h = jnp.maximum(_layernorm(x, axis=-1), 0.0)
    x = x + _L1_gnn_ref(h, edge_index, L1_gnn_W_msg, L1_gnn_b_msg, L1_gnn_W_upd, L1_gnn_b_upd)
    h = jnp.maximum(_layernorm(x, axis=-1), 0.0)
    x = x + _L2_gnn_ref(h, edge_attr_128, L2_gnn_Ws_k, L2_gnn_Ws_b, L2_gnn_Wr_k, L2_gnn_Wr_b, L2_gnn_We_k, L2_gnn_We_b, L2_gnn_attn_w, L2_gnn_attn_b, src, dst)
    h = jnp.maximum(_layernorm(x, axis=-1), 0.0)
    x = x + _L3_gnn_ref(h, src, dst, L3_gnn_ws1, L3_gnn_wn1, L3_gnn_b1, L3_gnn_ws2, L3_gnn_wn2, L3_gnn_b2, L3_gnn_w_score, L3_gnn_b_score, L3_gnn_wu1, L3_gnn_wnu1, L3_gnn_bu1, L3_gnn_wu2, L3_gnn_wnu2, L3_gnn_bu2)
    return x

_drawn_inputs = setup_inputs


def setup_inputs(seed=0):
    import zlib

    import numpy as np

    out = dict(_drawn_inputs(seed))
    spreads = {'L0_gnn_gat_bias': (0.0, 0.1),
     'L0_gnn_proj_b': (0.0, 0.1),
     'L0_gnn_ln_gamma': (1.0, 0.2),
     'L0_gnn_ln_beta': (0.0, 0.1),
     'L2_gnn_Ws_b': (0.0, 0.1),
     'L2_gnn_Wr_b': (0.0, 0.8),
     'L2_gnn_We_b': (0.0, 0.1),
     'L3_gnn_b1': (0.0, 0.1),
     'L3_gnn_b2': (0.0, 0.287),
     'L3_gnn_bu1': (0.0, 0.1),
     'L3_gnn_bu2': (0.0, 0.1)}
    factors = {'L0_gnn_att_dst': 3.947, 'L1_gnn_b_msg': 3.166}
    for name, (base, spread) in spreads.items():
        noise = np.random.default_rng([zlib.crc32(name.encode()), seed]).standard_normal(out[name].shape)
        drawn = base * np.exp(spread * noise) if base else spread * noise
        out[name] = jnp.asarray(drawn.astype(out[name].dtype))
    for name, factor in factors.items():
        out[name] = (out[name] * factor).astype(out[name].dtype)
    return out
```

```python
from contextlib import ExitStack

import concourse.bass as bass
from concourse import mybir

ALU = mybir.AluOpType
ACT = mybir.ActivationFunctionType
AX_X = mybir.AxisListType.X
F32 = mybir.dt.float32
I32 = mybir.dt.int32
BF16 = mybir.dt.bfloat16

P = 128
F = 128
N = 50000
E = 25000
J = 3
GROUP = P * J
FULL = N // GROUP
REST = N - FULL * GROUP
NGROUPS = FULL + 1
ET = -(-E // P)
EPAD = ET * P
EREST = E - (ET - 1) * P
H0, D0 = 8, 16
H2, D2 = 4, 32
LN_EPS = 1e-5
BIG = 1e38
SKIP = 100000
RING = 8
BATCH = 4
CH = 14
CT = ET // CH
CL = CT * P
LOADS = 40
KEEP = N // 4
ATT = 2 * H0
T0W = F + ATT + F
T1W = 2 * F
SW = F + 4
assert CH * CT == ET and ET % BATCH == 0 and 0 < REST <= P and REST % 16 == 0


def pipeline(eng, total, stages):
    lags = max(lag for lag, _ in stages)
    head = RING * (1 + -(-lags // RING))
    loops = total // RING

    def step(s, u):
        for lag, stage in stages:
            if not isinstance(s, int) or 0 <= s - lag < total:
                stage(s - lag, (u - lag) % RING)

    for s in range(head):
        step(s, s % RING)
    with eng.Fori(head // RING, loops) as i:
        for u in range(RING):
            step(i * RING + u, u)
    for s in range(loops * RING, total + lags):
        step(s, s % RING)


def reached(eng, sem, value):
    if not isinstance(value, int) or value > 0:
        eng.wait_ge(sem, value)


def nth(s, u):
    return (s - u) * (16 // RING) + 16


def is_rest(g):
    return isinstance(g, int) and g == FULL


def span(g):
    return (REST, 1) if is_rest(g) else (P, J)


def node_rows(table, g):
    if is_rest(g):
        return table[FULL * GROUP:N, :].unsqueeze(1)
    return table[bass.ds(g * GROUP, GROUP), :].rearrange("(p j) f -> p j f", j=J)


def edge_rows(table, t, n=P):
    return table[bass.ds(t * P, n), :]


class Pass:

    def __init__(self, nc, name):
        self.nc, self.name, self.sems = nc, name, []
        self.ctx = ExitStack()

    def sb(self, name, shape, dt=F32):
        return self.ctx.enter_context(self.nc.sbuf_tensor(f"{self.name}_{name}", shape, dt))

    def ps(self, name, shape, dt=F32):
        return self.ctx.enter_context(self.nc.psum_tensor(f"{self.name}_{name}", shape, dt))

    def sem(self, name):
        self.sems.append(self.nc.alloc_semaphore(f"{self.name}_{name}"))
        return self.sems[-1]

    def ring(self, name):
        return [self.sem(f"{name}{i}") for i in range(RING)]

    def __enter__(self):
        return self

    def __exit__(self, *error):
        self.ctx.close()
        if error[0] is None:
            self.nc.clear_and_free_semaphores(self.sems)
            self.nc.all_engine_barrier()


class Resident:
    pass


def setup(nc, a, d, r):
    with Pass(nc, "setup") as k:
        pads = k.sb("pads", [1, 96], I32)
        zi = k.sb("zi", [1, 96], I32)
        zero = k.sb("zero", [P, 30 * SW])
        half = ET // 2
        li = k.sb("li", [half, 3, 2 * P], I32)
        lf = k.sb("lf", [half, 3, 2 * P])
        ends = k.sb("ends", [1, 2, ET], I32)
        wl = k.sb("wl", [P, 7, F])
        col = k.sb("col", [P, 8])
        rows = k.sb("rows", [1, 12, F])
        tr = k.sb("tr", [P, 5, F])
        blk = k.sb("blk", [P, H0])
        mask = k.sb("mask", [P, H0])
        bs = k.sb("bs", [P, ATT])
        mean = k.sb("mean", [P, 2])
        dr = k.sb("dr", [P, RING, BATCH * P], I32)
        nxt = k.sb("nxt", [P, ET])
        same = k.sb("same", [P, ET])
        ps = k.ps("ps", [P, 8, 512])
        s_pad, s_zero, s_put, s_w, s_list, s_ends, s_zs = (
            k.sem(n) for n in ("pad", "zero", "put", "w", "list", "ends", "zs"))
        s_row = k.ring("row")
        s_iota, s_eye, s_v, s_pe, s_act, s_seg, s_li = (k.sem(n) for n in ("iota", "eye", "v", "pe", "act", "seg", "li"))
        with nc.Block() as block:
            @block.sync
            def _(sp):
                n = 0

                def load(dst, src):
                    nonlocal n
                    sp.dma_start(dst, src).then_inc(s_w, 16)
                    n += 1

                row = lambda v: v.rearrange("(a n) -> a n", a=1)
                column = lambda v: v.rearrange("(n a) -> n a", a=1)
                load(wl[:, 0, :], a["L0_gnn_proj_w"][:, :])
                load(wl[:, 1, :], a["L1_gnn_W_msg"][0:F, :])
                load(wl[:, 2, :], a["L1_gnn_W_msg"][F:2 * F, :])
                load(wl[:, 5, :], a["L0_gnn_lin_w"][:, :])
                load(wl[:, 6, :], a["L1_gnn_W_upd"][F:2 * F, :])
                load(r.wu[:, 0:F], a["L1_gnn_W_upd"][0:F, :])
                load(r.ws[:, :], a["L2_gnn_Ws_k"].rearrange("f h d -> f (h d)"))
                load(r.wr[:, :], a["L2_gnn_Wr_k"].rearrange("f h d -> f (h d)"))
                load(r.we[:, :], a["L2_gnn_We_k"].rearrange("f h d -> f (h d)"))
                load(r.w3[:, 0, 0:F], a["L3_gnn_ws1"][:, :])
                load(r.w3[:, 1, 0:F], a["L3_gnn_wn1"][:, :])
                load(r.w3[:, 2, 0:F], a["L3_gnn_ws2"][:, :])
                load(r.w3[:, 3, 0:F], a["L3_gnn_wn2"][:, :])
                load(r.w3[:, 4, 0:F], a["L3_gnn_wu1"][:, :])
                load(r.w3[:, 5, 0:F], a["L3_gnn_wnu1"][:, :])
                load(r.w3[:, 6, 0:F], a["L3_gnn_wu2"][:, :])
                load(r.w3[:, 7, 0:F], a["L3_gnn_wnu2"][:, :])
                load(col[:, 0:1], column(a["L0_gnn_gat_bias"]))
                load(col[:, 1:2], column(a["L1_gnn_b_msg"]))
                load(col[:, 2:3], column(a["L3_gnn_b2"]))
                load(col[:, 3:4], a["L3_gnn_w_score"][:, :])
                load(col[:, 4:5], a["L0_gnn_att_src"].rearrange("a h (d b) -> (a h d) b", b=1))
                load(col[:, 5:6], a["L0_gnn_att_dst"].rearrange("a h (d b) -> (a h d) b", b=1))
                load(rows[:, 0, :], row(a["L0_gnn_proj_b"]))
                load(r.b1[:, 0:F], row(a["L1_gnn_b_upd"]))
                load(rows[:, 1, :], a["L2_gnn_Ws_b"].rearrange("(a h) d -> a (h d)", a=1))
                load(rows[:, 2, :], a["L2_gnn_We_b"].rearrange("(a h) d -> a (h d)", a=1))
                load(r.b2[:, F:2 * F], a["L2_gnn_Wr_b"].rearrange("(a h) d -> a (h d)", a=1))
                load(r.b3[:, 0, 0:F], row(a["L3_gnn_b1"]))
                load(r.b3[:, 1, 0:F], row(a["L3_gnn_b2"]))
                load(r.b3[:, 2, 0:F], row(a["L3_gnn_bu1"]))
                load(r.b3[:, 3, 0:F], row(a["L3_gnn_bu2"]))
                load(rows[:, 3, 0:1], row(a["L3_gnn_b_score"]))
                load(r.gamma[:, :], row(a["L0_gnn_ln_gamma"]).to_broadcast([P, F]))
                load(r.beta[:, :], row(a["L0_gnn_ln_beta"]).to_broadcast([P, F]))
                for h in range(H2):
                    load(r.attw[:, h, :], a["L2_gnn_attn_w"].rearrange("d a -> a d").to_broadcast([P, D2]))
                load(r.attb[:, :], row(a["L2_gnn_attn_b"]).to_broadcast([P, 1]))
                assert n == LOADS
                sp.wait_ge(s_pad, 4)
                sp.dma_start(d.dst[1:1 + E], a["dst"]).then_inc(s_put, 16)
                sp.dma_start(d.src[0:E], a["src"]).then_inc(s_put, 16)
                sp.dma_start(d.dst[1 + E:2 + EPAD].rearrange("(a n) -> a n", a=1), pads[:, 0:1 + EPAD - E]).then_inc(s_put, 16)
                sp.dma_start(d.dst[0:1].rearrange("(a n) -> a n", a=1), pads[:, 95:96]).then_inc(s_put, 16)
                sp.dma_start(d.src[E:EPAD].rearrange("(a n) -> a n", a=1), zi[:, 0:EPAD - E]).then_inc(s_put, 16)
                sp.wait_ge(s_put, 80)
                for n, v in enumerate((d.src[0:EPAD], d.dst[1:1 + EPAD], d.dst[2:2 + EPAD])):
                    sp.dma_start(li[:, n, :], v.rearrange("(q e) -> q e", e=2 * P)).then_inc(s_list, 16)
                with nc.allow_non_contiguous_dma(reason="one word of each edge tile"):
                    for n in range(2):
                        sp.dma_start(ends[:, n, :], d.dst[n:n + EPAD].rearrange("(a t p) -> a t p", a=1, p=P)[:, :, 0])\
                          .then_inc(s_ends, 16)
                def destinations(i, u):
                    reached(sp, s_seg, i - RING + 1)
                    sp.dma_start(dr[:, u, :], d.dst[bass.ds(1 + i * (BATCH * P), BATCH * P)].rearrange("(a n) -> a n", a=1)
                                 .to_broadcast([P, BATCH * P])).then_inc(s_row[u], 16)

                pipeline(sp, ET // BATCH, [(0, destinations)])

            @block.scalar
            def _(act):
                act.wait_ge(s_zero, 1)
                whole = d.sums[0:FULL * GROUP, :].rearrange("(p m) f -> p (m f)", p=P)
                for m in range(13):
                    act.dma_start(whole[:, m * 30 * SW:(m + 1) * 30 * SW], zero[:, :]).then_inc(s_zs, 16)
                act.dma_start(d.sums[FULL * GROUP:N, :], zero[0:REST, 0:SW]).then_inc(s_zs, 16)
                act.wait_ge(s_zs, 14 * 16)

            @block.gpsimd
            def _(pool):
                pool.memset(zero[:, :], 0.0).then_inc(s_zero, 1)
                pool.memset(pads[:, :], -1).then_inc(s_pad, 1)
                pool.wait_ge(s_pad, 1)
                pool.memset(pads[:, 95:96], -2).then_inc(s_pad, 1)
                pool.memset(zi[:, :], 0).then_inc(s_pad, 1)
                pool.memset(r.ones[:, :], 1.0).then_inc(s_pad, 1)
                pool.memset(r.ident[:, :], 0.0).then_inc(s_iota, 1)
                pool.memset(mask[:, :], 1.0).then_inc(s_iota, 1)
                pool.memset(r.eps[:, :], LN_EPS).then_inc(s_iota, 1)
                pool.wait_ge(s_iota, 2)
                pool.affine_select(out=r.ident[:, :], in_=r.ident[:, :], compare_op=ALU.not_equal, fill=1.0,
                                   base=0, pattern=[[-1, P]], channel_multiplier=1).then_inc(s_eye, 1)
                pool.affine_select(out=mask[:, :], in_=mask[:, :], compare_op=ALU.is_ge, fill=0.0,
                                   base=0, pattern=[[-D0, H0]], channel_multiplier=1).then_inc(s_eye, 1)
                pool.wait_ge(s_eye, 2)
                pool.affine_select(out=blk[:, :], in_=mask[:, :], compare_op=ALU.is_ge, fill=0.0,
                                   base=D0 - 1, pattern=[[D0, H0]], channel_multiplier=-1).then_inc(s_eye, 1)

            @block.tensor
            def _(pe):
                pe.wait_ge(s_w, 16 * LOADS)
                pe.wait_ge(s_eye, 1)
                pe.wait_ge(s_pad, 4)
                for n in range(3):
                    pe.transpose(ps[:, 0, n * F:(n + 1) * F], wl[:, n, :], r.ident[:, :])
                pe.transpose(ps[:, 1, 0:F], r.w3[:, 2, 0:F], r.ident[:, :])
                pe.transpose(ps[:, 1, F:2 * F], r.w3[:, 3, 0:F], r.ident[:, :]).then_inc(s_pe, 1)
                pe.wait_ge(s_v, 3)
                pe.matmul(ps[:, 2, 0:F], wl[:, 5, :], r.projc[:, :], start=True, stop=True)
                pe.matmul(ps[:, 2, F:F + ATT], wl[:, 5, :], bs[:, :], start=True, stop=True)
                pe.transpose(ps[:, 2, 256:256 + F], wl[:, 5, :], r.ident[:, :])
                pe.matmul(ps[0:1, 3, 0:F], col[:, 0:1], r.projc[:, :], start=True, stop=True)
                pe.matmul(ps[:, 3, F:2 * F], tr[:, 1, :], wl[:, 6, :], start=True, stop=True)
                pe.matmul(ps[:, 3, 2 * F:3 * F], tr[:, 2, :], wl[:, 6, :], start=True, stop=True)
                pe.matmul(ps[0:1, 3, 3 * F:4 * F], col[:, 1:2], wl[:, 6, :], start=True, stop=True)
                pe.matmul(ps[:, 4, 0:1], tr[:, 3, :], col[:, 3:4], start=True, stop=True)
                pe.matmul(ps[:, 4, 1:2], tr[:, 4, :], col[:, 3:4], start=True, stop=True)
                pe.matmul(ps[0:1, 4, 2:3], col[:, 2:3], col[:, 3:4], start=True, stop=True).then_inc(s_pe, 1)
                pe.wait_ge(s_li, 1)
                for n in range(3):
                    for h in range(2):
                        mm = pe.transpose(ps[:, 5 + n, h * P:h * P + half], lf[:, n, h * P:(h + 1) * P],
                                          r.ident[0:half, 0:half])
                mm.then_inc(s_pe, 1)

            @block.vector
            def _(dve):
                done = 0

                def link(ins):
                    nonlocal done
                    done += 1
                    ins.then_inc(s_act, 1)
                    dve.wait_ge(s_act, done)

                dve.wait_ge(s_w, 16 * LOADS)
                dve.wait_ge(s_pe, 1)
                for n in range(3):
                    dve.tensor_copy(tr[:, n, :], ps[:, 0, n * F:(n + 1) * F])
                link(dve.tensor_copy(tr[:, 3:5, :], ps[:, 1, 0:2 * F].rearrange("p (n f) -> p n f", n=2)))
                link(dve.reduce_sum(mean[:, 0:1], tr[:, 0, :], AX_X))
                link(dve.tensor_scalar(mean[:, 0:1], mean[:, 0:1], -1.0 / F, None, ALU.mult))
                dve.tensor_scalar(r.projc[:, :], tr[:, 0, :], mean[:, 0:1], None, ALU.add).then_inc(s_v, 1)
                dve.wait_ge(s_eye, 3)
                dve.tensor_scalar(bs[:, 0:H0], blk[:, :], col[:, 4:5], None, ALU.mult).then_inc(s_v, 1)
                dve.tensor_scalar(bs[:, H0:ATT], blk[:, :], col[:, 5:6], None, ALU.mult).then_inc(s_v, 1)
                link(dve.reduce_sum(mean[0:1, 1:2], rows[:, 0, :], AX_X))
                link(dve.tensor_scalar(mean[0:1, 1:2], mean[0:1, 1:2], -1.0 / F, None, ALU.mult))
                link(dve.tensor_scalar(rows[:, 4, :], rows[:, 0, :], mean[0:1, 1:2], None, ALU.add))
                dve.tensor_tensor(r.b2[:, 0:F], rows[:, 1, :], rows[:, 2, :], ALU.add)
                dve.wait_ge(s_pe, 2)
                dve.tensor_copy(r.w0[:, F + ATT:], ps[:, 2, 0:F])
                dve.tensor_copy(r.w0[:, F:F + ATT], ps[:, 2, F:F + ATT])
                dve.tensor_copy(r.w0[:, 0:F], ps[:, 2, 256:256 + F])
                dve.tensor_tensor(r.c0[:, :], ps[0:1, 3, 0:F], rows[:, 4, :], ALU.add)
                dve.tensor_copy(r.wa[:, :], ps[:, 3, F:2 * F])
                dve.tensor_copy(r.wu[:, F:2 * F], ps[:, 3, 2 * F:3 * F])
                dve.tensor_copy(r.b1[:, F:2 * F], ps[0:1, 3, 3 * F:4 * F])
                dve.tensor_copy(r.w3[:, 2, F:F + 1], ps[:, 4, 0:1])
                dve.tensor_copy(r.w3[:, 3, F:F + 1], ps[:, 4, 1:2])
                dve.tensor_tensor(r.b3[:, 1, F:F + 1], ps[0:1, 4, 2:3], rows[:, 3, 0:1], ALU.add)
                dve.wait_ge(s_list, 48)
                dve.tensor_copy(lf[:, :, :], li[:, :, :]).then_inc(s_li, 1)
                dve.wait_ge(s_pe, 3)
                view = lambda t, h: t[:, :].rearrange("p (q h) -> p q h", h=2)[:, :, h]
                for h in range(2):
                    part = lambda n: ps[:, 5 + n, h * P:h * P + half]
                    dve.tensor_copy(view(r.src, h), part(0))
                    dve.tensor_copy(view(r.srcf, h), part(0))
                    dve.tensor_scalar(view(r.dstg, h), part(1), 0.0, None, ALU.max)
                    dve.tensor_copy(view(r.dstf, h), part(1))
                    link(dve.tensor_copy(view(nxt, h), part(2)))
                link(dve.tensor_tensor(same[:, :], nxt[:, :], r.dstf[:, :], ALU.is_equal))
                dve.scalar_tensor_tensor(r.last[:, :], same[:, :], float(SKIP), r.dstf[:, :], ALU.mult, ALU.add)
                dve.wait_ge(s_ends, 32)
                link(dve.memset(r.cont[:, ET:ET + RING], 0.0))
                dve.tensor_tensor(r.cont[:, 0:ET], ends[:, 0, :], ends[:, 1, :], ALU.is_equal)

                def segments(i, u):
                    dve.wait_ge(s_row[u], nth(i, u))
                    for v in range(BATCH):
                        ins = dve.tensor_scalar(r.seg[:, bass.ds(i * BATCH + v, 1), :], dr[:, u, v * P:(v + 1) * P].unsqueeze(1),
                                                r.dstf[:, bass.ds(i * BATCH + v, 1)], None, ALU.is_equal)
                    ins.then_inc(s_seg, 1)

                pipeline(dve, ET // BATCH, [(0, segments)])



class Norm:

    def __init__(self, k, name, tiles=1):
        self.stat = k.sb(f"{name}_stat", [P, 4, tiles, 6])
        self.mv = k.sb(f"{name}_mv", [P, 4, tiles, 2])
        self.std = k.sb(f"{name}_std", [P, 4, tiles])
        self.rs = k.sb(f"{name}_rs", [P, 4, tiles])
        self.nm = k.sb(f"{name}_nm", [P, 4, tiles])
        self.s_bn, self.s_turn, self.s_mv, self.s_std, self.s_rs, self.s_nm = (
            k.sem(f"{name}_{x}") for x in ("bn", "turn", "mv", "std", "rs", "nm"))

    def stats(self, dve, src, i, u, p=P, j=1):
        for n in range(j):
            ins = dve.bn_stats(self.stat[0:p, u % 4, n, :], src(n))
        ins.then_inc(self.s_bn, 1)

    def aggregate(self, dve, i, u, p=P, j=1):
        dve.wait_ge(self.s_bn, i + 1)
        dve.sem_inc(self.s_turn, 1)
        for n in range(j):
            ins = dve.bn_aggr(self.mv[0:p, u % 4, n, :], self.stat[0:p, u % 4, n, :])
        ins.then_inc(self.s_mv, 1)

    def root(self, act, r, i, u, p=P, j=1):
        act.wait_ge(self.s_mv, i + 1)
        act.activation(self.std[0:p, u % 4, 0:j], self.mv[0:p, u % 4, 0:j, 1], ACT.Sqrt, bias=r.eps[0:p, :])\
           .then_inc(self.s_std, 1)

    def inverse(self, dve, i, u, p=P, j=1):
        dve.wait_ge(self.s_std, i + 1)
        dve.reciprocal(self.rs[0:p, u % 4, 0:j], self.std[0:p, u % 4, 0:j]).then_inc(self.s_rs, 1)

    def shift(self, dve, i, u, p=P, j=1):
        dve.wait_ge(self.s_rs, i + 1)
        dve.scalar_tensor_tensor(self.nm[0:p, u % 4, 0:j], self.mv[0:p, u % 4, 0:j, 0], -1.0, self.rs[0:p, u % 4, 0:j],
                                 ALU.mult, ALU.mult).then_inc(self.s_nm, 1)

    def relu(self, act, dst, src, i, u, p=P, j=1):
        act.wait_ge(self.s_nm, i + 1)
        for n in range(j):
            ins = act.activation(dst(n), src(n), ACT.Relu, scale=self.rs[0:p, u % 4, n:n + 1],
                                 bias=self.nm[0:p, u % 4, n:n + 1])
        return ins


def last_in(total, u):
    return (total - 1 - u) // RING * RING + u


def turned_width(p, j):
    return (j - 1) * F + p


def node_pass_0(nc, a, d, r):
    with Pass(nc, "n0") as k:
        t0 = k.sb("t0", [P, RING, J, T0W])
        t1 = k.sb("t1", [P, RING, J, T1W])
        h0 = k.sb("h0", [P, 2, J * F])
        ht = k.sb("ht", [P, 2, J * F])
        y = k.sb("y", [P, 2, J, F])
        na, nb, nn = Norm(k, "a", J), Norm(k, "b", J), Norm(k, "c", J)
        pst = k.ps("pst", [P, 2, 512])
        pso = k.ps("pso", [P, 2, J, 512])
        s_in, s_st0, s_st1 = k.ring("in"), k.ring("st0_"), k.ring("st1_")
        s_h0, s_tr, s_ht, s_mm, s_t0, s_y, s_yx, s_x1, s_h1 = (
            k.sem(x) for x in ("h0", "tr", "ht", "mm", "t0", "y", "yx", "x1", "h1"))
        x_of = lambda u, p: lambda n: t0[0:p, u, n, F + ATT:]
        with nc.Block() as block:
            @block.sync
            def _(sp):
                def load(g, u):
                    p, j = span(g)
                    reached(sp, s_st0[u], nth(g, u) - 16)
                    reached(sp, s_yx, g - RING + 1)
                    sp.dma_start(t0[0:p, u, 0:j, F + ATT:], node_rows(a["x"], g)).then_inc(s_in[u], 16)

                def store_0(g, u):
                    p, j = span(g)
                    sp.wait_ge(s_t0, g + 1)
                    sp.dma_start(node_rows(d.t0, g), t0[0:p, u, 0:j, :]).then_inc(s_st0[u], 16)

                def store_1(g, u):
                    p, j = span(g)
                    sp.wait_ge(s_h1, g + 1)
                    sp.dma_start(node_rows(d.t1, g), t1[0:p, u, 0:j, :]).then_inc(s_st1[u], 16)

                pipeline(sp, NGROUPS, [(7, store_0), (0, load), (9, store_1)])
                for u in range(RING):
                    sp.wait_ge(s_st0[u], nth(last_in(NGROUPS, u), u))
                    sp.wait_ge(s_st1[u], nth(last_in(NGROUPS, u), u))

            @block.vector
            def _(dve):
                def stats_a(g, u):
                    dve.wait_ge(s_in[u], nth(g, u))
                    na.stats(dve, x_of(u, span(g)[0]), g, u, *span(g))

                def stats_b(g, u):
                    p, j = span(g)
                    dve.wait_ge(s_t0, g + 1)
                    nb.stats(dve, lambda n: pso[0:p, u % 2, n, F + ATT:T0W], g, u, p, j)

                def stats_c(g, u):
                    p, j = span(g)
                    dve.wait_ge(s_x1, g + 1)
                    nn.stats(dve, lambda n: t1[0:p, u, n, 0:F], g, u, p, j)

                def affine(g, u):
                    p, j = span(g)
                    dve.wait_ge(nb.s_rs, g + 1)
                    for n in range(j):
                        ins = dve.scalar_tensor_tensor(y[0:p, u % 2, n, :], pso[0:p, u % 2, n, F + ATT:T0W],
                                                       nb.rs[0:p, u % 4, n:n + 1], r.gamma[0:p, :], ALU.mult, ALU.mult)
                    ins.then_inc(s_y, 1)

                def add_x(g, u):
                    p, j = span(g)
                    dve.wait_ge(s_y, g + 1)
                    dve.tensor_tensor(y[0:p, u % 2, 0:j, :], y[0:p, u % 2, 0:j, :], t0[0:p, u, 0:j, F + ATT:], ALU.add)\
                       .then_inc(s_yx, 1)

                def add_beta(g, u):
                    p, j = span(g)
                    dve.wait_ge(s_yx, g + 1)
                    reached(dve, s_st1[u], nth(g, u) - 16)
                    dve.tensor_tensor(t1[0:p, u, 0:j, 0:F], y[0:p, u % 2, 0:j, :],
                                      r.beta[0:p, :].unsqueeze(1).to_broadcast([p, j, F]), ALU.add).then_inc(s_x1, 1)

                on = lambda step: lambda g, u: step(dve, g, u, *span(g))
                pipeline(dve, NGROUPS, [
                    (0, stats_a), (5, stats_c), (0, on(na.aggregate)), (5, on(nn.aggregate)), (1, on(na.inverse)),
                    (6, on(nn.inverse)), (4, on(nb.inverse)), (1, on(na.shift)), (6, on(nn.shift)), (4, affine),
                    (3, stats_b), (4, add_x), (3, on(nb.aggregate)), (4, add_beta)])

            @block.scalar
            def _(act):
                def relu_a(g, u):
                    p, j = span(g)
                    reached(act, s_tr, g - 1)
                    na.relu(act, lambda n: h0[0:p, u % 2, n * F:(n + 1) * F], x_of(u, p), g, u, p, j).then_inc(s_h0, 1)

                def turned(g, u):
                    act.wait_ge(s_tr, g + 1)
                    reached(act, s_mm, g - 1)
                    w = turned_width(*span(g))
                    act.activation(ht[:, u % 2, 0:w], pst[:, u % 2, 0:w], ACT.Copy).then_inc(s_ht, 1)

                def keep(g, u):
                    p, j = span(g)
                    act.wait_ge(s_mm, g + 1)
                    act.activation(t0[0:p, u, 0:j, 0:F + ATT], pso[0:p, u % 2, 0:j, 0:F + ATT], ACT.Copy).then_inc(s_t0, 1)

                def relu_c(g, u):
                    p, j = span(g)
                    nn.relu(act, lambda n: t1[0:p, u, n, F:], lambda n: t1[0:p, u, n, 0:F], g, u, p, j).then_inc(s_h1, 1)

                root = lambda norm: lambda g, u: norm.root(act, r, g, u, *span(g))
                pipeline(act, NGROUPS, [(1, root(na)), (6, root(nn)), (4, root(nb)), (3, keep), (2, turned), (1, relu_a),
                                        (6, relu_c)])

            @block.tensor
            def _(pe):
                def turn(g, u):
                    p, j = span(g)
                    pe.wait_ge(s_h0, g + 1)
                    reached(pe, s_ht, g - 1)
                    for n in range(j):
                        ins = pe.transpose(pst[:, u % 2, n * F:n * F + p], h0[0:p, u % 2, n * F:(n + 1) * F], r.ident[0:p, 0:p])
                    ins.then_inc(s_tr, 1)

                def product(g, u):
                    p, j = span(g)
                    pe.wait_ge(s_ht, g + 1)
                    reached(pe, s_t0, g - 1)
                    reached(pe, s_y, g - 1)
                    for n in range(j):
                        pe.matmul(pso[0:p, u % 2, n, 0:T0W], ht[:, u % 2, n * F:n * F + p], r.w0[:, :], start=True, stop=False)
                        ins = pe.matmul(pso[0:p, u % 2, n, F + ATT:T0W], r.ones[0:1, 0:p], r.c0[:, :], start=False, stop=True)
                    ins.then_inc(s_mm, 1)

                pipeline(pe, NGROUPS, [(3, product), (2, turn)])


def node_pass_1(nc, d, r):
    with Pass(nc, "n1") as k:
        t1 = k.sb("t1", [P, RING, J, T1W])
        sm = k.sb("sm", [P, RING, J, SW])
        ht = k.sb("ht", [P, 2, J * F])
        st = k.sb("st", [P, 2, J * F])
        q = k.sb("q", [P, 2, J, F])
        x2 = k.sb("x2", [P, RING, J, F])
        h2 = k.sb("h2", [P, RING, J, F])
        nn = Norm(k, "c", J)
        pst = k.ps("pst", [P, 2, 512])
        pss = k.ps("pss", [P, 2, 512])
        pso = k.ps("pso", [P, 2, 4, 2 * F])
        s_t1, s_sm, s_stx, s_sth = (k.ring(x) for x in ("t1_", "sm", "stx", "sth"))
        s_tr, s_ht, s_st, s_mm, s_q, s_x2, s_h2 = (k.sem(x) for x in ("tr", "ht", "st", "mm", "q", "x2", "h2"))
        with nc.Block() as block:
            @block.sync
            def _(sp):
                def load(g, u):
                    p, j = span(g)
                    reached(sp, s_q, g - RING + 1)
                    reached(sp, s_tr, g - RING + 1)
                    sp.dma_start(t1[0:p, u, 0:j, :], node_rows(d.t1, g)).then_inc(s_t1[u], 16)
                    sp.dma_start(sm[0:p, u, 0:j, :], node_rows(d.sums, g)).then_inc(s_sm[u], 16)

                def store(g, u):
                    p, j = span(g)
                    sp.wait_ge(s_x2, g + 1)
                    sp.dma_start(node_rows(d.x2, g), x2[0:p, u, 0:j, :]).then_inc(s_stx[u], 16)
                    sp.wait_ge(s_h2, g + 1)
                    sp.dma_start(node_rows(d.h2, g), h2[0:p, u, 0:j, :]).then_inc(s_sth[u], 16)

                pipeline(sp, NGROUPS, [(0, load), (8, store)])
                for u in range(RING):
                    sp.wait_ge(s_stx[u], nth(last_in(NGROUPS, u), u))
                    sp.wait_ge(s_sth[u], nth(last_in(NGROUPS, u), u))

            @block.vector
            def _(dve):
                def turned(g, u):
                    dve.wait_ge(s_tr, g + 1)
                    reached(dve, s_mm, g - 1)
                    w = turned_width(*span(g))
                    dve.tensor_copy(st[:, u % 2, 0:w], pss[:, u % 2, 0:w]).then_inc(s_st, 1)

                def weigh(g, u):
                    p, j = span(g)
                    dve.wait_ge(s_mm, g + 1)
                    for n in range(j):
                        ins = dve.scalar_tensor_tensor(q[0:p, u % 2, n, :], pso[0:p, u % 2, n, F:2 * F], sm[0:p, u, n, F:F + 1],
                                                       t1[0:p, u, n, 0:F], ALU.mult, ALU.add)
                    ins.then_inc(s_q, 1)

                def add(g, u):
                    p, j = span(g)
                    dve.wait_ge(s_q, g + 1)
                    reached(dve, s_stx[u], nth(g, u) - 16)
                    dve.tensor_tensor(x2[0:p, u, 0:j, :], q[0:p, u % 2, 0:j, :], pso[0:p, u % 2, 0:j, 0:F], ALU.add)\
                       .then_inc(s_x2, 1)

                def stats(g, u):
                    p, j = span(g)
                    dve.wait_ge(s_x2, g + 1)
                    nn.stats(dve, lambda n: x2[0:p, u, n, :], g, u, p, j)

                on = lambda step: lambda g, u: step(dve, g, u, *span(g))
                pipeline(dve, NGROUPS, [(2, weigh), (4, on(nn.inverse)), (3, stats), (2, add), (4, on(nn.shift)),
                                        (3, on(nn.aggregate)), (1, turned)])

            @block.scalar
            def _(act):
                def turned(g, u):
                    act.wait_ge(s_tr, g + 1)
                    reached(act, s_mm, g - 1)
                    w = turned_width(*span(g))
                    act.activation(ht[:, u % 2, 0:w], pst[:, u % 2, 0:w], ACT.Copy).then_inc(s_ht, 1)

                def relu(g, u):
                    p, j = span(g)
                    reached(act, s_sth[u], nth(g, u) - 16)
                    nn.relu(act, lambda n: h2[0:p, u, n, :], lambda n: x2[0:p, u, n, :], g, u, p, j).then_inc(s_h2, 1)

                pipeline(act, NGROUPS, [(4, lambda g, u: nn.root(act, r, g, u, *span(g))), (1, turned), (4, relu)])

            @block.tensor
            def _(pe):
                def turn(g, u):
                    p, j = span(g)
                    pe.wait_ge(s_t1[u], nth(g, u))
                    reached(pe, s_ht, g - 1)
                    for n in range(j):
                        pe.transpose(pst[:, u % 2, n * F:n * F + p], t1[0:p, u, n, F:], r.ident[0:p, 0:p])
                    pe.wait_ge(s_sm[u], nth(g, u))
                    reached(pe, s_st, g - 1)
                    for n in range(j):
                        ins = pe.transpose(pss[:, u % 2, n * F:n * F + p], sm[0:p, u, n, 0:F], r.ident[0:p, 0:p])
                    ins.then_inc(s_tr, 1)

                def product(g, u):
                    p, j = span(g)
                    pe.wait_ge(s_ht, g + 1)
                    pe.wait_ge(s_st, g + 1)
                    reached(pe, s_x2, g - 1)
                    for n in range(j):
                        pe.matmul(pso[0:p, u % 2, n, :], ht[:, u % 2, n * F:n * F + p], r.wu[:, :], start=True, stop=False)
                        pe.matmul(pso[0:p, u % 2, n, :], r.ones[0:1, 0:p], r.b1[:, :], start=False, stop=False)
                        ins = pe.matmul(pso[0:p, u % 2, n, 0:F], st[:, u % 2, n * F:n * F + p], r.wa[:, :], start=False, stop=True)
                    ins.then_inc(s_mm, 1)

                pipeline(pe, NGROUPS, [(2, product), (1, turn)])


def node_pass_2(nc, d, r):
    with Pass(nc, "n2") as k:
        x2 = k.sb("x2", [P, RING, J, F])
        sm = k.sb("sm", [P, RING, J, SW])
        x3 = k.sb("x3", [P, RING, J, F])
        h3 = k.sb("h3", [P, RING, J, F])
        nn = Norm(k, "c", J)
        s_in, s_sm, s_stx, s_sth = (k.ring(x) for x in ("in", "sm", "stx", "sth"))
        s_x3, s_h3 = k.sem("x3"), k.sem("h3")
        with nc.Block() as block:
            @block.sync
            def _(sp):
                def load(g, u):
                    p, j = span(g)
                    reached(sp, s_x3, g - RING + 1)
                    sp.dma_start(x2[0:p, u, 0:j, :], node_rows(d.x2, g)).then_inc(s_in[u], 16)
                    sp.dma_start(sm[0:p, u, 0:j, :], node_rows(d.sums, g)).then_inc(s_sm[u], 16)

                def store(g, u):
                    p, j = span(g)
                    sp.wait_ge(s_x3, g + 1)
                    sp.dma_start(node_rows(d.x3, g), x3[0:p, u, 0:j, :]).then_inc(s_stx[u], 16)
                    sp.wait_ge(s_h3, g + 1)
                    sp.dma_start(node_rows(d.h3, g), h3[0:p, u, 0:j, :]).then_inc(s_sth[u], 16)

                pipeline(sp, NGROUPS, [(0, load), (6, store)])
                for u in range(RING):
                    sp.wait_ge(s_stx[u], nth(last_in(NGROUPS, u), u))
                    sp.wait_ge(s_sth[u], nth(last_in(NGROUPS, u), u))

            @block.vector
            def _(dve):
                def add(g, u):
                    p, j = span(g)
                    dve.wait_ge(s_in[u], nth(g, u))
                    dve.wait_ge(s_sm[u], nth(g, u))
                    reached(dve, s_stx[u], nth(g, u) - 16)
                    dve.tensor_tensor(x3[0:p, u, 0:j, :], x2[0:p, u, 0:j, :], sm[0:p, u, 0:j, 0:F], ALU.add).then_inc(s_x3, 1)

                def stats(g, u):
                    p, j = span(g)
                    dve.wait_ge(s_x3, g + 1)
                    nn.stats(dve, lambda n: x3[0:p, u, n, :], g, u, p, j)

                on = lambda step: lambda g, u: step(dve, g, u, *span(g))
                pipeline(dve, NGROUPS, [(1, stats), (3, on(nn.inverse)), (0, add), (1, on(nn.aggregate)), (3, on(nn.shift))])

            @block.scalar
            def _(act):
                def relu(g, u):
                    p, j = span(g)
                    reached(act, s_sth[u], nth(g, u) - 16)
                    nn.relu(act, lambda n: h3[0:p, u, n, :], lambda n: x3[0:p, u, n, :], g, u, p, j).then_inc(s_h3, 1)

                pipeline(act, NGROUPS, [(2, lambda g, u: nn.root(act, r, g, u, *span(g))), (3, relu)])


def node_pass_3(nc, d, r, name, rows, wn, bias, out, relu=True, score=False, masked=False, final=False):
    cols = F + 1 if score else F
    with Pass(nc, name) as k:
        a = k.sb("a", [P, RING, J, rows.shape[1]])
        sm = k.sb("sm", [P, RING, J, SW])
        ht = k.sb("ht", [P, 2, J * F])
        st = k.sb("st", [P, 2, J * F])
        o = k.sb("o", [P, RING, J, out.shape[1]])
        x3 = k.sb("x3", [P, RING, J, F]) if final else None
        ka = k.sb("ka", [P, 2, J, F]) if masked else None
        ex = k.sb("ex", [P, 2, J]) if score else None
        e1 = k.sb("e1", [P, 2, J]) if score else None
        pst = k.ps("pst", [P, 2, 512])
        pss = k.ps("pss", [P, 2, 512])
        pso = k.ps("pso", [P, 2, 512])
        s_in, s_sm, s_x3, s_out = (k.ring(x) for x in ("in", "sm", "x3_", "out"))
        s_ka, s_tr, s_ht, s_st, s_mm, s_o, s_ex, s_e1, s_sc, s_pre = (
            k.sem(x) for x in ("ka", "tr", "ht", "st", "mm", "o", "ex", "e1", "sc", "pre"))
        view = lambda u, p, j: pso[0:p, u % 2, 0:J * cols].rearrange("p (j f) -> p j f", j=J)[:, 0:j, :]
        with nc.Block() as block:
            @block.sync
            def _(sp):
                def load(g, u):
                    p, j = span(g)
                    reached(sp, s_tr, g - RING + 1)
                    if masked:
                        reached(sp, s_ka, g - RING + 1)
                    sp.dma_start(a[0:p, u, 0:j, :], node_rows(rows, g)).then_inc(s_in[u], 16)
                    sp.dma_start(sm[0:p, u, 0:j, :], node_rows(d.sums, g)).then_inc(s_sm[u], 16)
                    if final:
                        reached(sp, s_o, g - RING + 1)
                        sp.dma_start(x3[0:p, u, 0:j, :], node_rows(d.x3, g)).then_inc(s_x3[u], 16)

                def store(g, u):
                    p, j = span(g)
                    sp.wait_ge(s_o, g + 1)
                    if score:
                        sp.wait_ge(s_sc, g + 1)
                    sp.dma_start(node_rows(out, g), o[0:p, u, 0:j, :]).then_inc(s_out[u], 16)

                pipeline(sp, NGROUPS, [(0, load), (7, store)])
                for u in range(RING):
                    sp.wait_ge(s_out[u], nth(last_in(NGROUPS, u), u))

            @block.vector
            def _(dve):
                if score:
                    dve.memset(r.z[:, :, :], -1.0).then_inc(s_pre, 1)
                    dve.memset(o[:, :, :, F:], 0.0).then_inc(s_pre, 1)
                    dve.wait_ge(s_pre, 2)

                def keep(g, u):
                    p, j = span(g)
                    dve.wait_ge(s_in[u], nth(g, u))
                    reached(dve, s_tr, g - 1)
                    for n in range(j):
                        ins = dve.tensor_scalar(ka[0:p, u % 2, n, :], a[0:p, u, n, 0:F], r.keep[0:p, bass.ds(g * J + n, 1)],
                                                None, ALU.mult)
                    ins.then_inc(s_ka, 1)

                def turned(g, u):
                    dve.wait_ge(s_tr, g + 1)
                    reached(dve, s_mm, g - 1)
                    w = turned_width(*span(g))
                    dve.tensor_copy(st[:, u % 2, 0:w], pss[:, u % 2, 0:w]).then_inc(s_st, 1)

                def add(g, u):
                    p, j = span(g)
                    dve.wait_ge(s_mm, g + 1)
                    dve.wait_ge(s_x3[u], nth(g, u))
                    reached(dve, s_out[u], nth(g, u) - 16)
                    dve.tensor_tensor(o[0:p, u, 0:j, :], view(u, p, j), x3[0:p, u, 0:j, :], ALU.add).then_inc(s_o, 1)

                def plus_one(g, u):
                    p, j = span(g)
                    dve.wait_ge(s_ex, g + 1)
                    dve.tensor_scalar(e1[0:p, u % 2, 0:j], ex[0:p, u % 2, 0:j], 1.0, None, ALU.add).then_inc(s_e1, 1)

                def sigmoid(g, u):
                    p, j = span(g)
                    dve.wait_ge(s_e1, g + 1)
                    dve.reciprocal(o[0:p, u, 0:j, F:F + 1], e1[0:p, u % 2, 0:j].unsqueeze(2))
                    dve.reciprocal(r.z[0:p, bass.ds(g, 1), 0:j], e1[0:p, u % 2, 0:j].unsqueeze(1)).then_inc(s_sc, 1)

                stages = [(1, turned)]
                if final:
                    stages = [(2, add)] + stages
                if score:
                    stages = [(3, plus_one)] + stages + [(3, sigmoid)]
                if masked:
                    stages = stages + [(0, keep)]
                pipeline(dve, NGROUPS, stages)

            @block.scalar
            def _(act):
                def turned(g, u):
                    act.wait_ge(s_tr, g + 1)
                    reached(act, s_mm, g - 1)
                    w = turned_width(*span(g))
                    act.activation(ht[:, u % 2, 0:w], pst[:, u % 2, 0:w], ACT.Copy).then_inc(s_ht, 1)

                def finish(g, u):
                    p, j = span(g)
                    act.wait_ge(s_mm, g + 1)
                    reached(act, s_out[u], nth(g, u) - 16)
                    act.activation(o[0:p, u, 0:j, 0:F], view(u, p, j)[:, :, 0:F], ACT.Relu if relu else ACT.Copy).then_inc(s_o, 1)

                def exp(g, u):
                    p, j = span(g)
                    act.wait_ge(s_mm, g + 1)
                    reached(act, s_e1, g - 1)
                    act.activation(ex[0:p, u % 2, 0:j], view(u, p, j)[:, :, F], ACT.Exp, scale=-1.0).then_inc(s_ex, 1)

                if score:
                    act.wait_ge(s_pre, 2)
                pipeline(act, NGROUPS, ([(2, exp)] if score else []) + ([] if final else [(2, finish)]) + [(1, turned)])

            @block.tensor
            def _(pe):
                def turn(g, u):
                    p, j = span(g)
                    if masked:
                        pe.wait_ge(s_ka, g + 1)
                    else:
                        pe.wait_ge(s_in[u], nth(g, u))
                    reached(pe, s_ht, g - 1)
                    for n in range(j):
                        pe.transpose(pst[:, u % 2, n * F:n * F + p], ka[0:p, u % 2, n, :] if masked else a[0:p, u, n, 0:F],
                                     r.ident[0:p, 0:p])
                    pe.wait_ge(s_sm[u], nth(g, u))
                    reached(pe, s_st, g - 1)
                    for n in range(j):
                        ins = pe.transpose(pss[:, u % 2, n * F:n * F + p], sm[0:p, u, n, 0:F], r.ident[0:p, 0:p])
                    ins.then_inc(s_tr, 1)

                def product(g, u):
                    p, j = span(g)
                    pe.wait_ge(s_ht, g + 1)
                    pe.wait_ge(s_st, g + 1)
                    reached(pe, s_o, g - 1)
                    for n in range(j):
                        dst = pso[0:p, u % 2, n * cols:(n + 1) * cols]
                        pe.matmul(dst, ht[:, u % 2, n * F:n * F + p], r.w3[:, wn, 0:cols], start=True, stop=False)
                        pe.matmul(dst, st[:, u % 2, n * F:n * F + p], r.w3[:, wn + 1, 0:cols], start=False, stop=False)
                        ins = pe.matmul(dst, r.ones[0:1, 0:p], r.b3[:, bias, 0:cols], start=False, stop=True)
                    ins.then_inc(s_mm, 1)

                pipeline(pe, NGROUPS, [(2, product), (1, turn)])


class SegmentSum:

    def __init__(self, k, r, width):
        self.r, self.w = r, width
        self.sf = k.sb("segf", [P, 4, P])
        self.car = k.sb("carry", [1, 4, width])
        self.ps = k.ps("ps_sum", [P, 4, 512])
        self.pc = k.ps("ps_carry", [P, 2, 512])
        self.s_sf, self.s_turn, self.s_main, self.s_fix, self.s_car = (k.sem(x) for x in ("sf", "sf_turn", "main", "fix", "car"))

    def clear(self, dve):
        dve.memset(self.car[:, 0, :], 0.0).then_inc(self.s_car, 1)

    def widen(self, act, t, u):
        reached(act, self.s_fix, t - 3)
        act.sem_inc(self.s_turn, 1)
        act.activation(self.sf[:, u % 4, :], self.r.seg[:, bass.ds(t, 1), :].rearrange("p a f -> p (a f)"), ACT.Copy)\
           .then_inc(self.s_sf, 1)

    def main(self, pe, rows, t, u, out_free):
        pe.wait_ge(self.s_sf, t + 1)
        reached(pe, out_free, t - 3)
        reached(pe, self.s_car, t)
        pe.matmul(self.ps[:, u % 4, 0:self.w], self.sf[:, u % 4, :], rows, start=True, stop=False)
        pe.matmul(self.pc[0:1, u % 2, 0:self.w], self.sf[:, u % 4, P - 1:P], rows, start=True, stop=False)\
          .then_inc(self.s_main, 1)

    def fix(self, pe, t, u):
        pe.wait_ge(self.s_car, t + 1)
        pe.matmul(self.ps[:, u % 4, 0:self.w], self.sf[0:1, u % 4, :], self.car[:, u % 4, :], start=False, stop=True)
        pe.matmul(self.pc[0:1, u % 2, 0:self.w], self.sf[0:1, u % 4, P - 1:P], self.car[:, u % 4, :], start=False, stop=True)\
          .then_inc(self.s_fix, 1)

    def carry(self, dve, t, u):
        dve.wait_ge(self.s_fix, t + 1)
        dve.tensor_scalar(self.car[:, (u + 1) % 4, :], self.pc[0:1, u % 2, 0:self.w], self.r.cont[:, bass.ds(t + 1, 1)],
                          None, ALU.mult).then_inc(self.s_car, 1)


class Indices:

    def __init__(self, k, name, table):
        self.table = table
        self.at = k.sb(name, [P, RING], I32)
        self.s, self.s_turn, self.s_pool = k.sem(name), k.sem(f"{name}_turn"), k.sem(f"{name}_pool")

    def stage(self, dve, t, u, used):
        reached(dve, used[u], nth(t, u) - 16)
        dve.sem_inc(self.s_turn, 1)
        dve.tensor_copy(self.at[:, u:u + 1], self.table[:, bass.ds(t, 1)]).then_inc(self.s, 1)

    def gather(self, pool, dst, table, t, u, arrived):
        pool.wait_ge(self.s, t + 1)
        pool.sem_inc(self.s_pool, 1)
        pool.indirect_dma_start(dst, None, table, bass.IndirectOffsetOnAxis(ap=self.at[:, u:u + 1], axis=0))\
            .then_inc(arrived[u], 16)

    def scatter(self, pool, table, src, t, u, written):
        pool.wait_ge(self.s, t + 1)
        pool.sem_inc(self.s_pool, 1)
        pool.indirect_dma_start(table, bass.IndirectOffsetOnAxis(ap=self.at[:, u:u + 1], axis=0), src, None,
                                bounds_check=N - 1, oob_is_err=False).then_inc(written[u], 16)


def drained(eng, sems, total):
    for u in range(RING):
        eng.wait_ge(sems[u], nth(last_in(total, u), u))


def edge_pass(nc, d, r, name, table, first, degree=False, masked=False):
    width = table.shape[1]
    cols = F + 1 if degree else F
    with Pass(nc, name) as k:
        g = k.sb("g", [P, RING, width + 1])
        o = k.sb("o", [P, RING, SW])
        m = k.sb("m", [P, 4, F]) if masked else None
        km = k.sb("km", [P, 4, 2]) if masked else None
        seg = SegmentSum(k, r, cols)
        src, last = Indices(k, "src", r.src), Indices(k, "last", r.last)
        s_g, s_w = k.ring("g"), k.ring("w")
        s_pre, s_o, s_k0, s_k1, s_m = (k.sem(x) for x in ("pre", "o", "k0", "k1", "m"))
        with nc.Block() as block:
            @block.gpsimd
            def _(pool):
                pool.memset(g[:, :, width:], 1.0).then_inc(s_pre, 1)
                pool.memset(o[:, :, F:], 0.0).then_inc(s_pre, 1)

                pool.wait_ge(s_pre, 2)

                def gather(t, u):
                    reached(pool, seg.s_main, t - RING + 1)
                    if masked:
                        reached(pool, s_m, t - RING + 1)
                    src.gather(pool, g[:, u, 0:width], table, t, u, s_g)

                def scatter(t, u):
                    pool.wait_ge(s_o, t + 1)
                    last.scatter(pool, d.sums, o[:, u, :], t, u, s_w)

                pipeline(pool, ET, [(0, gather), (6, scatter)])
                drained(pool, s_w, ET)

            @block.vector
            def _(dve):
                seg.clear(dve)
                dve.wait_ge(s_pre, 2)

                def mask(t, u):
                    dve.wait_ge(s_g[u], nth(t, u))
                    dve.scalar_tensor_tensor(km[:, u % 4, 0:1], g[:, u, F:F + 1], r.thr[:, 0:1], r.below[:, bass.ds(t, 1)],
                                             ALU.is_equal, ALU.mult).then_inc(s_k0, 1)

                def mask_too(t, u):
                    dve.wait_ge(s_k0, t + 1)
                    dve.scalar_tensor_tensor(km[:, u % 4, 1:2], g[:, u, F:F + 1], r.thr[:, 0:1], km[:, u % 4, 0:1],
                                             ALU.is_gt, ALU.add).then_inc(s_k1, 1)

                def kept(t, u):
                    dve.wait_ge(s_k1, t + 1)
                    reached(dve, seg.s_main, t - 3)
                    dve.tensor_scalar(m[:, u % 4, :], g[:, u, 0:F], km[:, u % 4, 1:2], None, ALU.mult).then_inc(s_m, 1)

                def out(t, u):
                    dve.wait_ge(seg.s_fix, t + 1)
                    reached(dve, s_w[u], nth(t, u) - 16)
                    if degree:
                        dve.tensor_copy(o[:, u, 0:cols], seg.ps[:, u % 4, 0:cols])
                        dve.reciprocal(r.rdeg[:, bass.ds(t, 1)], seg.ps[:, u % 4, F:F + 1]).then_inc(s_o, 1)
                    else:
                        dve.tensor_scalar(o[:, u, 0:F], seg.ps[:, u % 4, 0:F], r.rdeg[:, bass.ds(t, 1)], None, ALU.mult)\
                           .then_inc(s_o, 1)

                stages = [(0, lambda t, u: src.stage(dve, t, u, s_g)), (4, lambda t, u: seg.carry(dve, t, u)),
                          (4, lambda t, u: last.stage(dve, t, u, s_w)), (4, out)]
                if masked:
                    late = [(lag + 1, stage) for lag, stage in stages[1:]]
                    stages = [stages[0], (3, mask), late[0], (3, mask_too), late[1], (3, kept), late[2]]
                pipeline(dve, ET, stages)

            @block.scalar
            def _(act):
                pipeline(act, ET, [(0, lambda t, u: seg.widen(act, t, u))])

            @block.tensor
            def _(pe):
                def main(t, u):
                    if masked:
                        pe.wait_ge(s_m, t + 1)
                        seg.main(pe, m[:, u % 4, :], t, u, s_o)
                    else:
                        pe.wait_ge(s_g[u], nth(t, u))
                        seg.main(pe, g[:, u, first:first + cols], t, u, s_o)

                pe.wait_ge(s_pre, 2)
                pipeline(pe, ET, [(0, main), (1, lambda t, u: seg.fix(pe, t, u))])


def edge_pass_0a(nc, d, r):
    with Pass(nc, "e0a") as k:
        gs = k.sb("gs", [P, RING, T0W])
        gd = k.sb("gd", [P, RING, T0W])
        src, dst = Indices(k, "src", r.src), Indices(k, "dst", r.dstg)
        s_gs, s_gd, s_eh, s_ed = (k.ring(x) for x in ("gs", "gd", "eh", "ed"))
        s_l = k.sem("l")
        with nc.Block() as block:
            @block.gpsimd
            def _(pool):
                def gather(t, u):
                    reached(pool, s_eh[u], nth(t, u) - 16)
                    reached(pool, s_ed[u], nth(t, u) - 16)
                    reached(pool, s_l, t - RING + 1)
                    src.gather(pool, gs[:, u, :], d.t0, t, u, s_gs)
                    dst.gather(pool, gd[:, u, :], d.t0, t, u, s_gd)

                pipeline(pool, ET, [(0, gather)])

            @block.sync
            def _(sp):
                def keep(t, u):
                    sp.wait_ge(s_gs[u], nth(t, u))
                    sp.dma_start(edge_rows(d.eh, t), gs[:, u, 0:F]).then_inc(s_eh[u], 16)
                    sp.wait_ge(s_gd[u], nth(t, u))
                    sp.dma_start(edge_rows(d.ed, t), gd[:, u, :]).then_inc(s_ed[u], 16)

                pipeline(sp, ET, [(0, keep)])
                drained(sp, s_eh, ET)
                drained(sp, s_ed, ET)

            @block.vector
            def _(dve):
                def logits(t, u):
                    dve.wait_ge(s_gs[u], nth(t, u))
                    dve.wait_ge(s_gd[u], nth(t, u))
                    dve.tensor_tensor(r.logit[:, bass.ds(t, 1), :], gs[:, u, F:F + H0].unsqueeze(1),
                                      gd[:, u, F + H0:F + ATT].unsqueeze(1), ALU.add)
                    dve.tensor_tensor(r.self_logit[:, bass.ds(t, 1), :], gd[:, u, F:F + H0].unsqueeze(1),
                                      gd[:, u, F + H0:F + ATT].unsqueeze(1), ALU.add).then_inc(s_l, 1)

                pipeline(dve, ET, [(0, lambda t, u: src.stage(dve, t, u, s_gs)), (0, lambda t, u: dst.stage(dve, t, u, s_gd)),
                                   (3, logits)])


def softmax_weights(nc, d, r, name, own_loop):
    rows = H0 * CH
    with Pass(nc, name) as k:
        xp = k.sb("xp", [P, CT, H0, CH])
        xt = k.sb("xt", [rows, CL])
        fw = k.sb("fw", [rows, CL])
        ids = k.sb("ids", [rows, 3, CL], I32)
        gate = k.sb("gate", [rows, 2, CL])
        eid = k.sb("eid", [H0, 4, CH], I32)
        egate = k.sb("egate", [H0, 2, CH])
        es = k.sb("es", [H0, 2, CH])
        ec = k.sb("ec", [H0, CH])
        cin = k.sb("cin", [rows, 1])
        mx = k.sb("mx", [P, ET, H0])
        ps = k.ps("ps", [P, 8, 512])
        s_ids, s_eid, s_xp, s_up, s_dn, s_x = (k.sem(x) for x in ("ids", "eid", "xp", "up", "dn", "x"))
        s_v, s_e, s_a = k.sem("v"), k.sem("e"), k.sem("a")
        s_hop = [k.sem(f"hop{n}") for n in range(4)]
        s_end, s_in = k.sem("end"), k.sem("in")
        with nc.Block() as block:
            @block.sync
            def _(sp):
                for n in range(3):
                    for h in range(H0):
                        sp.dma_start(ids[h * CH:(h + 1) * CH, n, :], d.dst[n:n + EPAD].rearrange("(c e) -> c e", c=CH))\
                          .then_inc(s_ids, 16)
                with nc.allow_non_contiguous_dma(reason="four words of each chunk"):
                    for n, at in enumerate((0, CL, CL + 1, 1)):
                        sp.dma_start(eid[:, n, :], d.dst[at:at + EPAD].rearrange("(a c e) -> a c e", a=1, e=CL)[:, :, 0]
                                     .to_broadcast([H0, CH])).then_inc(s_eid, 16)
                for n in range(2):
                    sp.wait_ge(s_end, n + 1)
                    with nc.allow_non_contiguous_dma(reason="one word a partition"):
                        sp.dma_start(d.hop[2 * n:2 * n + 1, :].rearrange("a (n b) -> (a n) b", b=1),
                                     fw[:, CL - 1:CL] if n == 0 else xt[:, 0:1]).then_inc(s_hop[2 * n], 16)
                        sp.wait_ge(s_hop[2 * n], 16)
                        sp.dma_start(es[:, n, :], d.hop[2 * n, :].rearrange("(h c) -> h c", c=CH)).then_inc(s_hop[2 * n], 16)
                        sp.wait_ge(s_in, n + 1)
                        sp.dma_start(d.hop[2 * n + 1, :].rearrange("(h c) -> h c", c=CH), ec[:, :]).then_inc(s_hop[2 * n + 1], 16)
                        sp.wait_ge(s_hop[2 * n + 1], 16)
                        sp.dma_start(cin[:, :], d.hop[2 * n + 1:2 * n + 2, :].rearrange("a (n b) -> (a n) b", b=1))\
                          .then_inc(s_hop[2 * n + 1], 16)

            @block.vector
            def _(dve):
                done = 0

                def link(ins):
                    nonlocal done
                    done += 1
                    ins.then_inc(s_v, 1)
                    dve.wait_ge(s_v, done)

                if own_loop:
                    for v in (r.logit, r.self_logit):
                        ins = dve.scalar_tensor_tensor(v[:, :, :], v[:, :, :], 0.2, v[:, :, :], ALU.mult, ALU.max)
                    link(ins)
                else:
                    link(dve.memset(r.logit[:, :, H2:], 0.0))
                    link(dve.tensor_scalar(r.logit[:, :, 0:H2], r.logit[:, :, 0:H2], r.attb[:, :], None, ALU.add))
                for h in range(H0):
                    ins = dve.tensor_copy(xp[:, :, h, :], r.logit[:, :, h].rearrange("p (c j) -> p j c", j=CT))
                ins.then_inc(s_xp, 1)
                dve.wait_ge(s_ids, 16 * 3 * H0)
                dve.tensor_tensor(gate[:, 0, :], ids[:, 0, :], ids[:, 1, :], ALU.is_equal)
                link(dve.tensor_tensor(gate[:, 1, :], ids[:, 2, :], ids[:, 1, :], ALU.is_equal))
                dve.wait_ge(s_eid, 16 * 4)
                dve.tensor_tensor(egate[:, 0, :], eid[:, 0, :], eid[:, 1, :], ALU.is_equal)
                dve.tensor_tensor(egate[:, 1, :], eid[:, 2, :], eid[:, 3, :], ALU.is_equal)
                link(dve.tensor_scalar(gate[:, :, :], gate[:, :, :], 2 * BIG, -BIG, ALU.mult, ALU.add))
                link(dve.tensor_scalar(egate[:, :, :], egate[:, :, :], 2 * BIG, -BIG, ALU.mult, ALU.add))
                for b in range(4):
                    w = min(4, CT - 4 * b) * P
                    dve.wait_ge(s_up, b + 1)
                    ins = dve.tensor_copy(xt[:, 4 * b * P:4 * b * P + w], ps[0:rows, b, 0:w])
                link(ins)
                link(dve.tensor_tensor_scan(fw[:, :], gate[:, 0, :], xt[:, :], initial=-BIG, op0=ALU.min, op1=ALU.max))
                link(dve.memset(ec[:, :], -BIG))
                dve.sem_inc(s_end, 1)
                dve.wait_ge(s_hop[0], 32)
                link(dve.tensor_tensor_scan(es[:, 0, :], egate[:, 0, :], es[:, 0, :], initial=-BIG, op0=ALU.min, op1=ALU.max))
                dve.tensor_copy(ec[:, 1:CH], es[:, 0, 0:CH - 1]).then_inc(s_in, 1)
                dve.wait_ge(s_hop[1], 32)
                link(dve.tensor_tensor_scan(fw[:, :], gate[:, 0, :], xt[:, :], initial=cin[:, :], op0=ALU.min, op1=ALU.max))
                link(dve.tensor_tensor_scan(xt[:, ::-1], gate[:, 1, ::-1], fw[:, ::-1], initial=-BIG, op0=ALU.min, op1=ALU.max))
                link(dve.memset(ec[:, :], -BIG))
                dve.sem_inc(s_end, 1)
                dve.wait_ge(s_hop[2], 32)
                link(dve.tensor_tensor_scan(es[:, 1, ::-1], egate[:, 1, ::-1], es[:, 1, ::-1], initial=-BIG, op0=ALU.min, op1=ALU.max))
                dve.tensor_copy(ec[:, 0:CH - 1], es[:, 1, 1:CH]).then_inc(s_in, 1)
                dve.wait_ge(s_hop[3], 32)
                dve.tensor_tensor_scan(xt[:, ::-1], gate[:, 1, ::-1], fw[:, ::-1], initial=cin[:, :], op0=ALU.min, op1=ALU.max)\
                   .then_inc(s_x, 1)
                for b in range(4):
                    m = min(4, CT - 4 * b)
                    dve.wait_ge(s_dn, b + 1)
                    for j in range(m):
                        ins = dve.tensor_copy(mx[:, :, :].rearrange("p (c j) h -> p j h c", j=CT)[:, 4 * b + j, :, :],
                                              ps[:, 4 + b, j * P:j * P + rows].rearrange("p (h c) -> p h c", c=CH))
                link(ins)
                if own_loop:
                    link(dve.tensor_tensor(mx[:, :, :], mx[:, :, :], r.self_logit[:, :, :], ALU.max))
                    dve.tensor_tensor(r.self_logit[:, :, :], r.self_logit[:, :, :], mx[:, :, :], ALU.subtract)
                dve.tensor_tensor(r.logit[:, :, :], r.logit[:, :, :], mx[:, :, :], ALU.subtract).then_inc(s_e, 1)

            @block.scalar
            def _(act):
                act.wait_ge(s_e, 1)
                act.activation(r.logit[:, :, :], r.logit[:, :, :], ACT.Exp).then_inc(s_a, 1)
                if own_loop:
                    act.activation(r.self_logit[:, :, :], r.self_logit[:, :, :], ACT.Exp).then_inc(s_a, 1)

            @block.tensor
            def _(pe):
                pe.wait_ge(s_xp, 1)
                for j in range(CT):
                    ins = pe.transpose(ps[0:rows, j // 4, j % 4 * P:(j % 4 + 1) * P], xp[:, j, :, :].rearrange("p h c -> p (h c)"),
                                       r.ident[:, :])
                    if j % 4 == 3 or j == CT - 1:
                        ins.then_inc(s_up, 1)
                pe.wait_ge(s_x, 1)
                for j in range(CT):
                    ins = pe.transpose(ps[:, 4 + j // 4, j % 4 * P:j % 4 * P + rows], xt[:, j * P:(j + 1) * P],
                                       r.ident[0:rows, 0:rows])
                    if j % 4 == 3 or j == CT - 1:
                        ins.then_inc(s_dn, 1)


def edge_pass_0b(nc, d, r):
    with Pass(nc, "e0b") as k:
        hs = k.sb("hs", [P, RING, F])
        hd = k.sb("hd", [P, RING, T0W])
        m = k.sb("m", [P, 4, F + H0])
        own = k.sb("own", [P, 4, F])
        num = k.sb("num", [P, 2, F])
        den = k.sb("den", [P, 2, 2, H0])
        agg = k.sb("agg", [P, 2, F])
        at = k.sb("at", [P, 2, F])
        y = k.sb("y", [P, 2, 2, F])
        o = k.sb("o", [P, RING, T1W])
        seg = SegmentSum(k, r, F + H0)
        nb, nn = Norm(k, "b"), Norm(k, "c")
        last = Indices(k, "last", r.last)
        px = k.ps("px", [P, 2, 512])
        s_hs, s_hd, s_w = k.ring("hs"), k.ring("hd"), k.ring("w")
        names = ("m", "m2", "own", "num", "den", "rden", "agg", "tr", "at", "mm", "y", "yx", "x1", "h1")
        s_m, s_m2, s_own, s_num, s_den, s_rden, s_agg, s_tr, s_at, s_mm, s_y, s_yx, s_x1, s_h1 = (k.sem(x) for x in names)
        heads = lambda v: v.rearrange("p (h d) -> p h d", d=D0)
        wide = lambda v: v.rearrange("p a h -> p (a h)").unsqueeze(2).to_broadcast([P, H0, D0])
        with nc.Block() as block:
            @block.sync
            def _(sp):
                def load(t, u):
                    reached(sp, s_m, t - RING + 1)
                    sp.dma_start(hs[:, u, :], edge_rows(d.eh, t)).then_inc(s_hs[u], 16)
                    reached(sp, s_yx, t - RING + 1)
                    sp.dma_start(hd[:, u, :], edge_rows(d.ed, t)).then_inc(s_hd[u], 16)

                pipeline(sp, ET, [(0, load)])

            @block.gpsimd
            def _(pool):
                def own_row(t, u):
                    pool.wait_ge(s_hd[u], nth(t, u))
                    reached(pool, s_num, t - 3)
                    pool.tensor_tensor(heads(own[:, u % 4, :]), heads(hd[:, u, 0:F]), wide(r.self_logit[:, bass.ds(t, 1), :]),
                                       ALU.mult).then_inc(s_own, 1)

                def scatter(t, u):
                    pool.wait_ge(s_h1, t + 1)
                    last.scatter(pool, d.t1, o[:, u, :], t, u, s_w)

                pipeline(pool, ET, [(0, own_row), (7, scatter)])
                drained(pool, s_w, ET)

            @block.vector
            def _(dve):
                seg.clear(dve)

                def weigh(t, u):
                    dve.wait_ge(s_hs[u], nth(t, u))
                    reached(dve, seg.s_main, t - 3)
                    dve.tensor_tensor(heads(m[:, u % 4, 0:F]), heads(hs[:, u, :]), wide(r.logit[:, bass.ds(t, 1), :]),
                                      ALU.mult).then_inc(s_m, 1)

                def weights(t, u):
                    dve.tensor_copy(m[:, u % 4, F:].unsqueeze(1), r.logit[:, bass.ds(t, 1), :]).then_inc(s_m2, 1)

                def add_own(t, u):
                    dve.wait_ge(s_own, t + 1)
                    dve.wait_ge(seg.s_fix, t + 1)
                    dve.tensor_tensor(num[:, u % 2, :], own[:, u % 4, :], seg.ps[:, u % 4, 0:F], ALU.add).then_inc(s_num, 1)

                def add_own_weight(t, u):
                    dve.tensor_tensor(den[:, u % 2, 0, :].unsqueeze(1), seg.ps[:, u % 4, F:F + H0].unsqueeze(1),
                                      r.self_logit[:, bass.ds(t, 1), :], ALU.add).then_inc(s_den, 1)

                def invert(t, u):
                    dve.wait_ge(s_den, t + 1)
                    dve.reciprocal(den[:, u % 2, 1, :], den[:, u % 2, 0, :]).then_inc(s_rden, 1)

                def divide(t, u):
                    dve.wait_ge(s_rden, t + 1)
                    dve.tensor_tensor(heads(agg[:, u % 2, :]), heads(num[:, u % 2, :]), wide(den[:, u % 2, 1:2, :]), ALU.mult)\
                       .then_inc(s_agg, 1)

                def stats_b(t, u):
                    dve.wait_ge(s_mm, t + 1)
                    nb.stats(dve, lambda n: px[:, u % 2, F:2 * F], t, u)

                def affine(t, u):
                    dve.wait_ge(nb.s_rs, t + 1)
                    dve.scalar_tensor_tensor(y[:, u % 2, 0, :], px[:, u % 2, F:2 * F], nb.rs[:, u % 4, 0:1], r.gamma[:, :],
                                             ALU.mult, ALU.mult).then_inc(s_y, 1)

                def add_x(t, u):
                    dve.wait_ge(s_hd[u], nth(t, u))
                    dve.wait_ge(s_y, t + 1)
                    dve.tensor_tensor(y[:, u % 2, 1, :], y[:, u % 2, 0, :], hd[:, u, F + ATT:], ALU.add).then_inc(s_yx, 1)

                def add_beta(t, u):
                    dve.wait_ge(s_yx, t + 1)
                    reached(dve, s_w[u], nth(t, u) - 16)
                    dve.tensor_tensor(o[:, u, 0:F], y[:, u % 2, 1, :], r.beta[:, :], ALU.add).then_inc(s_x1, 1)

                def stats_c(t, u):
                    dve.wait_ge(s_x1, t + 1)
                    nn.stats(dve, lambda n: o[:, u, 0:F], t, u)

                on = lambda step: lambda t, u: step(dve, t, u)
                pipeline(dve, ET, [
                    (0, weigh), (3, on(nb.inverse)), (5, on(nn.inverse)), (0, weights), (3, affine),
                    (5, on(nn.shift)), (1, lambda t, u: seg.carry(dve, t, u)), (3, add_x), (1, add_own_weight), (1, add_own), (3, add_beta),
                    (1, invert), (4, stats_c), (4, lambda t, u: last.stage(dve, t, u, s_w)), (2, stats_b), (1, divide),
                    (4, on(nn.aggregate)), (2, on(nb.aggregate))])

            @block.scalar
            def _(act):
                def turned(t, u):
                    act.wait_ge(s_tr, t + 1)
                    reached(act, s_mm, t - 1)
                    act.activation(at[:, u % 2, :], px[:, u % 2, 0:F], ACT.Copy).then_inc(s_at, 1)

                def relu(t, u):
                    nn.relu(act, lambda n: o[:, u, F:], lambda n: o[:, u, 0:F], t, u).then_inc(s_h1, 1)

                pipeline(act, ET, [(3, lambda t, u: nb.root(act, r, t, u)), (5, lambda t, u: nn.root(act, r, t, u)),
                                   (0, lambda t, u: seg.widen(act, t, u)), (2, turned), (5, relu)])

            @block.tensor
            def _(pe):
                def main(t, u):
                    pe.wait_ge(s_m2, t + 1)
                    seg.main(pe, m[:, u % 4, :], t, u, s_num)

                def turn(t, u):
                    pe.wait_ge(s_agg, t + 1)
                    reached(pe, s_y, t - 1)
                    pe.transpose(px[:, u % 2, 0:F], agg[:, u % 2, :], r.ident[:, :]).then_inc(s_tr, 1)

                def project(t, u):
                    pe.wait_ge(s_at, t + 1)
                    pe.matmul(px[:, u % 2, F:2 * F], at[:, u % 2, :], r.projc[:, :], start=True, stop=False)
                    pe.matmul(px[:, u % 2, F:2 * F], r.ones[0:1, :], r.c0[:, :], start=False, stop=True).then_inc(s_mm, 1)

                pipeline(pe, ET, [(2, turn), (0, main), (1, lambda t, u: seg.fix(pe, t, u)), (2, project)])


def edge_pass_2a(nc, a, d, r):
    with Pass(nc, "e2a") as k:
        gs = k.sb("gs", [P, RING, F])
        gd = k.sb("gd", [P, RING, F])
        ea = k.sb("ea", [P, RING, F])
        xt = k.sb("xt", [P, 2, 3 * F])
        e = k.sb("e", [P, RING, F])
        z, zc, uu, w, w2, wi, zw, zv = (k.sb(x, [P, 4, F]) for x in ("z", "zc", "uu", "w", "w2", "wi", "zw", "zv"))
        src, dst = Indices(k, "src", r.src), Indices(k, "dst", r.dstg)
        pst = k.ps("pst", [P, 2, 512])
        pso = k.ps("pso", [P, 2, 512])
        s_gs, s_gd, s_ea, s_e = (k.ring(x) for x in ("gs", "gd", "ea", "e"))
        names = ("pad", "tr", "xt", "mm", "ev", "z", "zc", "u", "w", "w2", "wi", "zw", "zv", "zz", "l")
        s_pad, s_tr, s_xt, s_mm, s_ev, s_z, s_zc, s_u, s_w, s_w2, s_wi, s_zw, s_zv, s_zz, s_l = (k.sem(x) for x in names)
        with nc.Block() as block:
            @block.gpsimd
            def _(pool):
                def gather(t, u):
                    reached(pool, s_tr, t - RING + 1)
                    src.gather(pool, gs[:, u, :], d.h2, t, u, s_gs)
                    dst.gather(pool, gd[:, u, :], d.h2, t, u, s_gd)

                pipeline(pool, ET, [(0, gather)])

            @block.sync
            def _(sp):
                def load(t, u):
                    n = EREST if isinstance(t, int) and t == ET - 1 else P
                    reached(sp, s_tr, t - RING + 1)
                    sp.dma_start(ea[0:n, u, :], edge_rows(a["edge_attr_128"], t, n)).then_inc(s_ea[u], 16)

                def store(t, u):
                    sp.wait_ge(s_ev, t + 1)
                    sp.dma_start(edge_rows(d.eh, t), e[:, u, :]).then_inc(s_e[u], 16)

                pipeline(sp, ET, [(0, load), (7, store)])
                drained(sp, s_e, ET)

            @block.vector
            def _(dve):
                def add(t, u):
                    dve.wait_ge(s_ev, t + 1)
                    dve.tensor_tensor(z[:, u % 4, :], e[:, u, :], pso[:, u % 2, F:2 * F], ALU.add).then_inc(s_z, 1)

                def cap(t, u):
                    dve.wait_ge(s_z, t + 1)
                    dve.tensor_scalar(zc[:, u % 4, :], z[:, u % 4, :], 20.0, None, ALU.min).then_inc(s_zc, 1)

                def square(t, u):
                    dve.wait_ge(s_u, t + 1)
                    dve.scalar_tensor_tensor(w[:, u % 4, :], uu[:, u % 4, :], 2.0, uu[:, u % 4, :], ALU.add, ALU.mult).then_inc(s_w, 1)

                def weigh(t, u):
                    dve.tensor_tensor(zw[:, u % 4, :], z[:, u % 4, :], r.attw[:, :, :].rearrange("p h d -> p (h d)"), ALU.mult)\
                       .then_inc(s_zw, 1)

                def invert(t, u):
                    dve.wait_ge(s_w2, t + 1)
                    dve.reciprocal(wi[:, u % 4, :], w2[:, u % 4, :]).then_inc(s_wi, 1)

                def times_w(t, u):
                    dve.wait_ge(s_zw, t + 1)
                    dve.tensor_tensor(zv[:, u % 4, :], zw[:, u % 4, :], w[:, u % 4, :], ALU.mult).then_inc(s_zv, 1)

                def divide(t, u):
                    dve.wait_ge(s_wi, t + 1)
                    dve.wait_ge(s_zv, t + 1)
                    dve.tensor_tensor(wi[:, u % 4, :], zv[:, u % 4, :], wi[:, u % 4, :], ALU.mult).then_inc(s_zz, 1)

                def reduce(t, u):
                    dve.wait_ge(s_zz, t + 1)
                    dve.tensor_reduce(r.logit[:, bass.ds(t, 1), 0:H2].rearrange("p a h -> p (a h)"),
                                      wi[:, u % 4, :].rearrange("p (h d) -> p h d", d=D2), AX_X, ALU.add).then_inc(s_l, 1)

                pipeline(dve, ET, [
                    (0, lambda t, u: src.stage(dve, t, u, s_gs)), (0, lambda t, u: dst.stage(dve, t, u, s_gd)),
                    (5, add), (6, square), (7, invert), (5, cap), (6, weigh), (7, times_w), (8, reduce), (7, divide)])

            @block.scalar
            def _(act):
                def turned(t, u):
                    act.wait_ge(s_tr, t + 1)
                    reached(act, s_mm, t - 1)
                    act.activation(xt[:, u % 2, :], pst[:, u % 2, 0:3 * F], ACT.Copy).then_inc(s_xt, 1)

                def keep(t, u):
                    act.wait_ge(s_mm, t + 1)
                    reached(act, s_e[u], nth(t, u) - 16)
                    reached(act, s_z, t - RING + 1)
                    act.activation(e[:, u, :], pso[:, u % 2, 0:F], ACT.Copy).then_inc(s_ev, 1)

                def exp(t, u):
                    act.wait_ge(s_zc, t + 1)
                    reached(act, s_w, t - 3)
                    act.activation(uu[:, u % 4, :], zc[:, u % 4, :], ACT.Exp).then_inc(s_u, 1)

                def plus_two(t, u):
                    act.wait_ge(s_w, t + 1)
                    reached(act, s_wi, t - 3)
                    act.activation(w2[:, u % 4, :], w[:, u % 4, :], ACT.Copy, bias=2.0).then_inc(s_w2, 1)

                pipeline(act, ET, [(1, keep), (2, exp), (0, turned), (3, plus_two)])

            @block.tensor
            def _(pe):
                def turn(t, u):
                    reached(pe, s_xt, t - 1)
                    for n, (rows, sem) in enumerate(((ea, s_ea), (gs, s_gs), (gd, s_gd))):
                        pe.wait_ge(sem[u], nth(t, u))
                        ins = pe.transpose(pst[:, u % 2, n * F:(n + 1) * F], rows[:, u, :], r.ident[:, :])
                    ins.then_inc(s_tr, 1)

                def product(t, u):
                    pe.wait_ge(s_xt, t + 1)
                    reached(pe, s_ev, t - 1)
                    reached(pe, s_z, t - 1)
                    x = lambda n: xt[:, u % 2, n * F:(n + 1) * F]
                    pe.matmul(pso[:, u % 2, 0:2 * F], r.ones[0:1, :], r.b2[:, :], start=True, stop=False)
                    pe.matmul(pso[:, u % 2, 0:F], x(0), r.we[:, :], start=False, stop=False)
                    pe.matmul(pso[:, u % 2, 0:F], x(1), r.ws[:, :], start=False, stop=False)
                    pe.matmul(pso[:, u % 2, F:2 * F], x(2), r.wr[:, :], start=False, stop=True).then_inc(s_mm, 1)

                pipeline(pe, ET, [(1, product), (0, turn)])


def edge_pass_2b(nc, d, r):
    with Pass(nc, "e2b") as k:
        e = k.sb("e", [P, RING, F])
        m = k.sb("m", [P, 4, F + H2])
        wi = k.sb("wi", [P, 2, H2])
        o = k.sb("o", [P, RING, SW])
        seg = SegmentSum(k, r, F + H2)
        last = Indices(k, "last", r.last)
        s_e, s_w = k.ring("e"), k.ring("w")
        s_pre, s_m, s_m2, s_wi, s_o = (k.sem(x) for x in ("pre", "m", "m2", "wi", "o"))
        heads = lambda v: v.rearrange("p (h d) -> p h d", d=D2)
        wide = lambda v: v.unsqueeze(2).to_broadcast([P, H2, D2])
        with nc.Block() as block:
            @block.sync
            def _(sp):
                def load(t, u):
                    reached(sp, s_m, t - RING + 1)
                    sp.dma_start(e[:, u, :], edge_rows(d.eh, t)).then_inc(s_e[u], 16)

                pipeline(sp, ET, [(0, load)])

            @block.gpsimd
            def _(pool):
                pool.memset(o[:, :, F:], 0.0).then_inc(s_pre, 1)
                pool.wait_ge(s_pre, 1)

                def scatter(t, u):
                    pool.wait_ge(s_o, t + 1)
                    last.scatter(pool, d.sums, o[:, u, :], t, u, s_w)

                pipeline(pool, ET, [(0, scatter)])
                drained(pool, s_w, ET)

            @block.vector
            def _(dve):
                seg.clear(dve)

                def weigh(t, u):
                    dve.wait_ge(s_e[u], nth(t, u))
                    reached(dve, seg.s_main, t - 3)
                    dve.tensor_tensor(heads(m[:, u % 4, 0:F]), heads(e[:, u, :]),
                                      wide(r.logit[:, bass.ds(t, 1), 0:H2].rearrange("p a h -> p (a h)")), ALU.mult).then_inc(s_m, 1)

                def weights(t, u):
                    dve.tensor_copy(m[:, u % 4, F:].unsqueeze(1), r.logit[:, bass.ds(t, 1), 0:H2]).then_inc(s_m2, 1)

                def invert(t, u):
                    dve.wait_ge(seg.s_fix, t + 1)
                    dve.reciprocal(wi[:, u % 2, :], seg.ps[:, u % 4, F:F + H2]).then_inc(s_wi, 1)

                def divide(t, u):
                    dve.wait_ge(s_wi, t + 1)
                    reached(dve, s_w[u], nth(t, u) - 16)
                    dve.tensor_tensor(heads(o[:, u, 0:F]), heads(seg.ps[:, u % 4, 0:F]), wide(wi[:, u % 2, :]), ALU.mult)\
                       .then_inc(s_o, 1)

                pipeline(dve, ET, [(3, invert), (2, lambda t, u: seg.carry(dve, t, u)), (0, weigh), (0, weights),
                                   (3, lambda t, u: last.stage(dve, t, u, s_w)), (3, divide)])

            @block.scalar
            def _(act):
                pipeline(act, ET, [(0, lambda t, u: seg.widen(act, t, u))])

            @block.tensor
            def _(pe):
                def main(t, u):
                    pe.wait_ge(s_m2, t + 1)
                    seg.main(pe, m[:, u % 4, :], t, u, s_o)

                pipeline(pe, ET, [(0, main), (1, lambda t, u: seg.fix(pe, t, u))])


def choose(nc, d, r):
    with Pass(nc, "top") as k:
        zf = r.z[:, :, :].rearrange("p g j -> p (g j)")
        n = NGROUPS * J
        ids = k.sb("ids", [P, n], I32)
        idt = k.sb("idt", [P, 1], I32)
        idf = k.sb("idf", [P, n])
        junk = k.sb("junk", [P, n])
        far = k.sb("far", [P, n])
        bit = k.sb("bit", [P, 1], I32)
        cand = k.sb("cand", [P, 1], I32)
        yes = k.sb("yes", [P, 1], I32)
        cnt = k.sb("cnt", [P, 1])
        need = k.sb("need", [P, 1])
        step = k.sb("step", [P, 1])
        bound = k.sb("bound", [P, 1])
        fit = k.sb("fit", [P, 1])
        tot = k.ps("tot", [P, 512])
        thr = r.thr[:, 0:1]
        thr_bits = thr.bitcast(I32)
        s_id, s_cnt, s_tot, s_v = (k.sem(x) for x in ("id", "cnt", "tot", "v"))
        VALUE_BITS, INDEX_BITS = 30, 17
        with nc.Block() as block:
            @block.gpsimd
            def _(pool):
                pool.iota(ids[:, :], pattern=[[GROUP, NGROUPS], [1, J]], base=0, channel_multiplier=J).then_inc(s_id, 1)
                pool.iota(idt[:, :], pattern=[[0, 1]], base=FULL * GROUP, channel_multiplier=1).then_inc(s_id, 1)

            @block.tensor
            def _(pe):
                with pe.Fori(0, VALUE_BITS + 1 + INDEX_BITS) as i:
                    pe.wait_ge(s_cnt, i + 1)
                    pe.matmul(tot[:, 0:1], r.ones[:, :], cnt[:, :], start=True, stop=True).then_inc(s_tot, 1)

            @block.vector
            def _(dve):
                FIRST, EACH, SECOND = 2, 5, 7

                def link(ins, value):
                    ins.then_inc(s_v, 1)
                    dve.wait_ge(s_v, value)

                dve.memset(thr, 0.0)
                link(dve.memset(bit[:, :], 1 << (VALUE_BITS - 1)), 1)
                dve.wait_ge(s_id, 2)
                dve.tensor_copy(idf[:, :], ids[:, :])
                link(dve.tensor_copy(junk[:, 0:1], idt[:, :]), 2)
                with dve.Fori(0, VALUE_BITS) as i:
                    at = FIRST + i * EACH
                    link(dve.tensor_tensor(cand[:, :], thr_bits, bit[:, :], ALU.bitwise_or), at + 1)
                    link(dve.tensor_scalar(junk[:, :], zf, cand[:, :].bitcast(F32), 0.0, ALU.is_ge, ALU.add,
                                           accum_out=cnt[:, :]), at + 2)
                    dve.sem_inc(s_cnt, 1)
                    dve.wait_ge(s_tot, i + 1)
                    link(dve.tensor_scalar(yes[:, :], tot[:, 0:1], float(KEEP), -1.0, ALU.is_ge, ALU.mult), at + 3)
                    link(dve.tensor_tensor(yes[:, :], yes[:, :], bit[:, :], ALU.bitwise_and), at + 4)
                    dve.tensor_tensor(thr_bits, thr_bits, yes[:, :], ALU.bitwise_or)
                    link(dve.tensor_scalar(bit[:, :], bit[:, :], 1, None, ALU.logical_shift_right), at + 5)
                at = FIRST + VALUE_BITS * EACH
                link(dve.tensor_scalar(junk[:, :], zf, thr, 0.0, ALU.is_gt, ALU.add, accum_out=cnt[:, :]), at + 1)
                dve.sem_inc(s_cnt, 1)
                dve.wait_ge(s_tot, VALUE_BITS + 1)
                dve.tensor_scalar(need[:, :], tot[:, 0:1], -1.0, float(KEEP), ALU.mult, ALU.add)
                dve.memset(bound[:, :], 0.0)
                dve.memset(step[:, :], float(1 << (INDEX_BITS - 1)))
                link(dve.tensor_scalar(far[:, :], zf, thr, float(1 << 20), ALU.not_equal, ALU.mult), at + 2)
                link(dve.tensor_copy(idf[0:REST, FULL * J:FULL * J + 1], idt[0:REST, :]), at + 3)
                link(dve.tensor_tensor(far[:, :], far[:, :], idf[:, :], ALU.add), at + 4)
                at += 4
                with dve.Fori(0, INDEX_BITS) as i:
                    v = at + i * SECOND
                    link(dve.tensor_tensor(cand[:, :].bitcast(F32), bound[:, :], step[:, :], ALU.add), v + 1)
                    link(dve.tensor_scalar(junk[:, :], far[:, :], cand[:, :].bitcast(F32), 0.0, ALU.is_lt, ALU.add,
                                           accum_out=cnt[:, :]), v + 2)
                    dve.sem_inc(s_cnt, 1)
                    dve.wait_ge(s_tot, i + (VALUE_BITS + 2))
                    link(dve.tensor_tensor(fit[:, :], tot[:, 0:1], need[:, :], ALU.is_le), v + 3)
                    link(dve.tensor_tensor(fit[:, :], fit[:, :], step[:, :], ALU.mult), v + 4)
                    link(dve.tensor_tensor(bound[:, :], bound[:, :], fit[:, :], ALU.add), v + 5)
                    link(dve.tensor_scalar(step[:, :], step[:, :], 0.5, None, ALU.mult), v + 6)
                    link(dve.tensor_copy(fit[:, :], bound[:, :]), v + 7)
                at += INDEX_BITS * SECOND
                link(dve.tensor_scalar(far[:, :], far[:, :], bound[:, :], None, ALU.is_lt), at + 1)
                dve.scalar_tensor_tensor(r.keep[:, :], zf, thr, far[:, :], ALU.is_gt, ALU.add)
                dve.tensor_scalar(r.below[:, :], r.srcf[:, :], bound[:, :], None, ALU.is_lt)




def main(nc, a, out):
    with ExitStack() as ctx:
        def sb(name, shape, dt=F32):
            return ctx.enter_context(nc.sbuf_tensor(name, shape, dt))
        d, r = Resident(), Resident()
        dram = lambda n, s, dt=F32: nc.dram_tensor(n, s, dt, kind="Internal").ap()
        d.dst = dram("dst_padded", (EPAD + CL + 2,), I32)
        d.hop = dram("chunk_values", (4, H0 * CH))
        d.src = dram("src_padded", (EPAD,), I32)
        d.t0 = dram("table0", (N, T0W))
        d.t1 = dram("table1", (N, T1W))
        d.x2 = dram("x2", (N, F))
        d.h2 = dram("h2", (N, F))
        d.x3 = dram("x3", (N, F))
        d.h3 = dram("h3", (N, F))
        d.g = dram("g_conv1", (N, F))
        d.hp = dram("h_scored", (N, SW))
        d.up = dram("up_conv1", (N, F))
        d.sums = dram("segment_sums", (N, SW))
        d.eh = dram("edge_source_rows", (EPAD, F))
        d.ed = dram("edge_target_rows", (EPAD, T0W))
        r.ident = sb("ident", [P, P])
        r.ones = sb("ones", [P, P])
        r.eps = sb("eps", [P, 1])
        r.src = sb("src_index", [P, ET], I32)
        r.dstg = sb("dst_index", [P, ET], I32)
        r.last = sb("last_index", [P, ET], I32)
        r.srcf = sb("src_float", [P, ET])
        r.dstf = sb("dst_float", [P, ET])
        r.rdeg = sb("degree_inverse", [P, ET])
        r.cont = sb("cont", [1, ET + RING])
        r.seg = sb("segments", [P, ET, P], BF16)
        r.projc = sb("projc", [P, F])
        r.w0 = sb("w0", [P, T0W])
        r.c0 = sb("c0", [1, F])
        r.gamma = sb("gamma", [P, F])
        r.beta = sb("beta", [P, F])
        r.wu = sb("wu", [P, 2 * F])
        r.wa = sb("wa", [P, F])
        r.b1 = sb("b1", [1, 2 * F])
        r.ws = sb("ws", [P, F])
        r.wr = sb("wr", [P, F])
        r.we = sb("we", [P, F])
        r.b2 = sb("b2", [1, 2 * F])
        r.attw = sb("attw", [P, H2, D2])
        r.attb = sb("attb", [P, 1])
        r.w3 = sb("w3", [P, 8, F + 1])
        r.b3 = sb("b3", [1, 4, F + 1])
        r.logit = sb("logit", [P, ET, H0])
        r.self_logit = sb("self_logit", [P, ET, H0])
        r.z = sb("score", [P, FULL + 1, J])
        r.thr = sb("threshold", [P, 2])
        r.keep = sb("keep", [P, NGROUPS * J])
        r.below = sb("below", [P, ET])
        passes(nc, a, d, r, out)


def passes(nc, a, d, r, out):
    setup(nc, a, d, r)
    node_pass_0(nc, a, d, r)
    edge_pass_0a(nc, d, r)
    softmax_weights(nc, d, r, "sm0", own_loop=True)
    edge_pass_0b(nc, d, r)
    edge_pass(nc, d, r, "e1", d.t1, F, degree=True)
    node_pass_1(nc, d, r)
    edge_pass_2a(nc, a, d, r)
    softmax_weights(nc, d, r, "sm2", own_loop=False)
    edge_pass_2b(nc, d, r)
    node_pass_2(nc, d, r)
    edge_pass(nc, d, r, "e3", d.h3, 0)
    node_pass_3(nc, d, r, "n3", d.h3, 0, 0, d.g)
    edge_pass(nc, d, r, "e4", d.g, 0)
    node_pass_3(nc, d, r, "n4", d.g, 2, 1, d.hp, relu=False, score=True)
    choose(nc, d, r)
    edge_pass(nc, d, r, "e5", d.hp, 0, masked=True)
    node_pass_3(nc, d, r, "n5", d.hp, 4, 2, d.up, masked=True)
    edge_pass(nc, d, r, "e6", d.up, 0)
    node_pass_3(nc, d, r, "n6", d.up, 6, 3, out, final=True)


_OUTS = [((N, F), 'float32')]


def kernel(**inputs):
    import numpy as _np
    import concourse.bacc as _bacc
    from concourse import mybir as _mybir
    from concourse.bass_utils import run_bass_kernel_spmd as _run

    nc = _bacc.Bacc("TRN2", target_bir_lowering=False, num_devices=1)
    arrays, args = {}, {}
    for name, value in inputs.items():
        v = _np.ascontiguousarray(value)
        arrays[f"in_{name}"] = v
        args[name] = nc.dram_tensor(f"in_{name}", v.shape, _mybir.dt.from_np(v.dtype), kind="ExternalInput").ap()
    out = nc.dram_tensor("out_x", (N, F), _mybir.dt.float32, kind="ExternalOutput").ap()
    main(nc, args, out)
    got = _run(nc, [arrays], core_ids=[0])
    return got.results[0]["out_x"]
```

```python
from contextlib import ExitStack

import concourse.bass as bass
from concourse import mybir

ALU = mybir.AluOpType
ACT = mybir.ActivationFunctionType
AX_X = mybir.AxisListType.X
F32 = mybir.dt.float32
I32 = mybir.dt.int32
BF16 = mybir.dt.bfloat16

P = 128
F = 128
N = 50000
E = 25000
J = 3
GROUP = P * J
FULL = N // GROUP
REST = N - FULL * GROUP
NGROUPS = FULL + 1
ET = -(-E // P)
EPAD = ET * P
EREST = E - (ET - 1) * P
H0, D0 = 8, 16
H2, D2 = 4, 32
LN_EPS = 1e-5
BIG = 1e38
SKIP = 100000
RING = 8
BATCH = 4
CH = 14
CT = ET // CH
CL = CT * P
LOADS = 40
KEEP = N // 4
ATT = 2 * H0
T0W = F + ATT + F
T1W = 2 * F
HPW = F + 4
C0, B1, B2, B3 = 0, F, 3 * F, 5 * F
BIASES = B3 + 4 * (F + 1)
assert CH * CT == ET and ET % BATCH == 0 and 0 < REST <= P and REST % 16 == 0


def pipeline(eng, total, stages):
    lags = max(lag for lag, _ in stages)
    head = RING * (1 + -(-lags // RING))
    loops = total // RING

    def step(s, u):
        for lag, stage in stages:
            if not isinstance(s, int) or 0 <= s - lag < total:
                stage(s - lag, (u - lag) % RING)

    for s in range(head):
        step(s, s % RING)
    with eng.Fori(head // RING, loops) as i:
        for u in range(RING):
            step(i * RING + u, u)
    for s in range(loops * RING, total + lags):
        step(s, s % RING)


def reached(eng, sem, value):
    if not isinstance(value, int) or value > 0:
        eng.wait_ge(sem, value)


def nth(s, u):
    return (s - u) * (16 // RING) + 16


def sent(eng, sems, s, u, depth):
    v = (u - depth) % RING
    reached(eng, sems[v], nth(s - depth, v))


def is_rest(g):
    return isinstance(g, int) and g == FULL


def span(g):
    return (REST, 1) if is_rest(g) else (P, J)


def node_rows(table, g):
    if is_rest(g):
        return table[FULL * GROUP:N, :].unsqueeze(1)
    return table[bass.ds(g * GROUP, GROUP), :].rearrange("(p j) f -> p j f", j=J)


def edge_rows(table, t, n=P):
    return table[bass.ds(t * P, n), :]


class Pass:

    def __init__(self, nc, name):
        self.nc, self.name, self.sems = nc, name, []
        self.ctx = ExitStack()

    def sb(self, name, shape, dt=F32):
        return self.ctx.enter_context(self.nc.sbuf_tensor(f"{self.name}_{name}", shape, dt))

    def ps(self, name, shape, dt=F32):
        return self.ctx.enter_context(self.nc.psum_tensor(f"{self.name}_{name}", shape, dt))

    def sem(self, name):
        self.sems.append(self.nc.alloc_semaphore(f"{self.name}_{name}"))
        return self.sems[-1]

    def ring(self, name):
        return [self.sem(f"{name}{i}") for i in range(RING)]

    def __enter__(self):
        return self

    def __exit__(self, *error):
        self.ctx.close()
        if error[0] is None:
            self.nc.clear_and_free_semaphores(self.sems)
            self.nc.all_engine_barrier()


class Resident:
    pass


def setup(nc, a, d, r):
    with Pass(nc, "setup") as k:
        pads = k.sb("pads", [1, 96], I32)
        zi = k.sb("zi", [1, 96], I32)
        half = ET // 2
        li = k.sb("li", [half, 4, 2 * P], I32)
        lf = k.sb("lf", [half, 4, 2 * P])
        res = k.sb("res", [1, 2, BIASES])
        part = k.sb("part", [1, 3, BIASES], BF16)
        wl = k.sb("wl", [P, 7, F])
        col = k.sb("col", [P, 8])
        rows = k.sb("rows", [1, 12, F])
        tr = k.sb("tr", [P, 5, F])
        blk = k.sb("blk", [P, H0])
        mask = k.sb("mask", [P, H0])
        bs = k.sb("bs", [P, ATT])
        mean = k.sb("mean", [P, 2])
        dr = k.sb("dr", [P, RING, 1 + BATCH * P], I32)
        nxt = k.sb("nxt", [P, ET])
        prev = k.sb("prev", [P, ET])
        same = k.sb("same", [P, ET])
        ps = k.ps("ps", [P, 8, 512])
        s_pad, s_put, s_w, s_list, s_ends, s_part = (k.sem(n) for n in ("pad", "put", "w", "list", "ends", "part"))
        s_row = k.ring("row")
        s_iota, s_eye, s_v, s_pe, s_act, s_seg, s_li = (k.sem(n) for n in ("iota", "eye", "v", "pe", "act", "seg", "li"))
        with nc.Block() as block:
            @block.sync
            def _(sp):
                n = 0

                def load(dst, src):
                    nonlocal n
                    sp.dma_start(dst, src).then_inc(s_w, 16)
                    n += 1

                row = lambda v: v.rearrange("(a n) -> a n", a=1)
                column = lambda v: v.rearrange("(n a) -> n a", a=1)
                load(wl[:, 0, :], a["L0_gnn_proj_w"][:, :])
                load(wl[:, 1, :], a["L1_gnn_W_msg"][0:F, :])
                load(wl[:, 2, :], a["L1_gnn_W_msg"][F:2 * F, :])
                load(wl[:, 5, :], a["L0_gnn_lin_w"][:, :])
                load(wl[:, 6, :], a["L1_gnn_W_upd"][F:2 * F, :])
                load(r.wu[:, 0:F], a["L1_gnn_W_upd"][0:F, :])
                load(r.ws[:, :], a["L2_gnn_Ws_k"].rearrange("f h d -> f (h d)"))
                load(r.wr[:, :], a["L2_gnn_Wr_k"].rearrange("f h d -> f (h d)"))
                load(r.we[:, :], a["L2_gnn_We_k"].rearrange("f h d -> f (h d)"))
                load(r.w3[:, 0, 0:F], a["L3_gnn_ws1"][:, :])
                load(r.w3[:, 1, 0:F], a["L3_gnn_wn1"][:, :])
                load(r.w3[:, 2, 0:F], a["L3_gnn_ws2"][:, :])
                load(r.w3[:, 3, 0:F], a["L3_gnn_wn2"][:, :])
                load(r.w3[:, 4, 0:F], a["L3_gnn_wu1"][:, :])
                load(r.w3[:, 5, 0:F], a["L3_gnn_wnu1"][:, :])
                load(r.w3[:, 6, 0:F], a["L3_gnn_wu2"][:, :])
                load(r.w3[:, 7, 0:F], a["L3_gnn_wnu2"][:, :])
                load(col[:, 0:1], column(a["L0_gnn_gat_bias"]))
                load(col[:, 1:2], column(a["L1_gnn_b_msg"]))
                load(col[:, 2:3], column(a["L3_gnn_b2"]))
                load(col[:, 3:4], a["L3_gnn_w_score"][:, :])
                load(col[:, 4:5], a["L0_gnn_att_src"].rearrange("a h (d b) -> (a h d) b", b=1))
                load(col[:, 5:6], a["L0_gnn_att_dst"].rearrange("a h (d b) -> (a h d) b", b=1))
                load(rows[:, 0, :], row(a["L0_gnn_proj_b"]))
                load(r.b1[:, 0:F], row(a["L1_gnn_b_upd"]))
                load(rows[:, 1, :], a["L2_gnn_Ws_b"].rearrange("(a h) d -> a (h d)", a=1))
                load(rows[:, 2, :], a["L2_gnn_We_b"].rearrange("(a h) d -> a (h d)", a=1))
                load(r.b2[:, F:2 * F], a["L2_gnn_Wr_b"].rearrange("(a h) d -> a (h d)", a=1))
                load(r.b3[:, 0, 0:F], row(a["L3_gnn_b1"]))
                load(r.b3[:, 1, 0:F], row(a["L3_gnn_b2"]))
                load(r.b3[:, 2, 0:F], row(a["L3_gnn_bu1"]))
                load(r.b3[:, 3, 0:F], row(a["L3_gnn_bu2"]))
                load(rows[:, 3, 0:1], row(a["L3_gnn_b_score"]))
                load(r.gamma[:, :], row(a["L0_gnn_ln_gamma"]).to_broadcast([P, F]))
                load(r.beta[:, :], row(a["L0_gnn_ln_beta"]).to_broadcast([P, F]))
                for h in range(H2):
                    load(r.attw[:, h, :], a["L2_gnn_attn_w"].rearrange("d a -> a d").to_broadcast([P, D2]))
                load(r.attb[:, :], row(a["L2_gnn_attn_b"]).to_broadcast([P, 1]))
                assert n == LOADS
                sp.wait_ge(s_pad, 4)
                sp.dma_start(d.dst[1:1 + E], a["dst"]).then_inc(s_put, 16)
                sp.dma_start(d.src[0:E], a["src"]).then_inc(s_put, 16)
                sp.dma_start(d.dst[1 + E:2 + EPAD].rearrange("(a n) -> a n", a=1), pads[:, 0:1 + EPAD - E]).then_inc(s_put, 16)
                sp.dma_start(d.dst[0:1].rearrange("(a n) -> a n", a=1), pads[:, 95:96]).then_inc(s_put, 16)
                sp.dma_start(d.src[E:EPAD].rearrange("(a n) -> a n", a=1), zi[:, 0:EPAD - E]).then_inc(s_put, 16)
                sp.wait_ge(s_put, 80)
                for n, v in enumerate((d.src[0:EPAD], d.dst[1:1 + EPAD], d.dst[2:2 + EPAD], d.dst[0:EPAD])):
                    sp.dma_start(li[:, n, :], v.rearrange("(q e) -> q e", e=2 * P)).then_inc(s_list, 16)
                sp.wait_ge(s_part, 1)
                sp.dma_start(d.parts.rearrange("(a n) f -> a n f", a=1), part[:, :, :]).then_inc(s_ends, 16)
                sp.wait_ge(s_ends, 16)
                sp.dma_start(r.bias3[:, :], d.parts[:, :]).then_inc(s_ends, 16)
                def destinations(i, u):
                    reached(sp, s_seg, i - RING + 1)
                    sp.dma_start(dr[:, u, :], d.dst[bass.ds(i * (BATCH * P), 1 + BATCH * P)].rearrange("(a n) -> a n", a=1)
                                 .to_broadcast([P, 1 + BATCH * P])).then_inc(s_row[u], 16)

                pipeline(sp, ET // BATCH, [(0, destinations)])
                sp.wait_ge(s_ends, 32)

            @block.gpsimd
            def _(pool):
                pool.memset(pads[:, :], -1).then_inc(s_pad, 1)
                pool.wait_ge(s_pad, 1)
                pool.memset(pads[:, 95:96], -2).then_inc(s_pad, 1)
                pool.memset(zi[:, :], 0).then_inc(s_pad, 1)
                pool.memset(r.ones[:, :], 1.0).then_inc(s_pad, 1)
                pool.memset(r.ones3[:, :], 1.0)
                pool.memset(r.ident[:, :], 0.0).then_inc(s_iota, 1)
                pool.memset(mask[:, :], 1.0).then_inc(s_iota, 1)
                pool.memset(r.eps[:, :], LN_EPS).then_inc(s_iota, 1)
                pool.wait_ge(s_iota, 2)
                pool.affine_select(out=r.ident[:, :], in_=r.ident[:, :], compare_op=ALU.not_equal, fill=1.0,
                                   base=0, pattern=[[-1, P]], channel_multiplier=1).then_inc(s_eye, 1)
                pool.affine_select(out=mask[:, :], in_=mask[:, :], compare_op=ALU.is_ge, fill=0.0,
                                   base=0, pattern=[[-D0, H0]], channel_multiplier=1).then_inc(s_eye, 1)
                pool.wait_ge(s_eye, 2)
                pool.affine_select(out=blk[:, :], in_=mask[:, :], compare_op=ALU.is_ge, fill=0.0,
                                   base=D0 - 1, pattern=[[D0, H0]], channel_multiplier=-1).then_inc(s_eye, 1)

            @block.tensor
            def _(pe):
                pe.wait_ge(s_w, 16 * LOADS)
                pe.wait_ge(s_eye, 1)
                pe.wait_ge(s_pad, 4)
                for n in range(3):
                    pe.transpose(ps[:, 0, n * F:(n + 1) * F], wl[:, n, :], r.ident[:, :])
                pe.transpose(ps[:, 1, 0:F], r.w3[:, 2, 0:F], r.ident[:, :])
                pe.transpose(ps[:, 1, F:2 * F], r.w3[:, 3, 0:F], r.ident[:, :]).then_inc(s_pe, 1)
                pe.wait_ge(s_v, 3)
                pe.matmul(ps[:, 2, 0:F], wl[:, 5, :], r.projc[:, :], start=True, stop=True)
                pe.matmul(ps[:, 2, F:F + ATT], wl[:, 5, :], bs[:, :], start=True, stop=True)
                pe.transpose(ps[:, 2, 256:256 + F], wl[:, 5, :], r.ident[:, :])
                pe.matmul(ps[0:1, 3, 0:F], col[:, 0:1], r.projc[:, :], start=True, stop=True)
                pe.matmul(ps[:, 3, F:2 * F], tr[:, 1, :], wl[:, 6, :], start=True, stop=True)
                pe.matmul(ps[:, 3, 2 * F:3 * F], tr[:, 2, :], wl[:, 6, :], start=True, stop=True)
                pe.matmul(ps[0:1, 3, 3 * F:4 * F], col[:, 1:2], wl[:, 6, :], start=True, stop=True)
                pe.matmul(ps[:, 4, 0:1], tr[:, 3, :], col[:, 3:4], start=True, stop=True)
                pe.matmul(ps[:, 4, 1:2], tr[:, 4, :], col[:, 3:4], start=True, stop=True)
                pe.matmul(ps[0:1, 4, 2:3], col[:, 2:3], col[:, 3:4], start=True, stop=True).then_inc(s_pe, 1)
                pe.wait_ge(s_li, 1)
                for n in range(4):
                    for h in range(2):
                        mm = pe.transpose(ps[:, 5 + n // 2, (n % 2 * 2 + h) * P:(n % 2 * 2 + h) * P + half], lf[:, n, h * P:(h + 1) * P],
                                          r.ident[0:half, 0:half])
                mm.then_inc(s_pe, 1)

            @block.vector
            def _(dve):
                done = 0

                def link(ins):
                    nonlocal done
                    done += 1
                    ins.then_inc(s_act, 1)
                    dve.wait_ge(s_act, done)

                dve.memset(r.b3[:, :, F:F + 1], 0.0)
                dve.wait_ge(s_w, 16 * LOADS)
                dve.wait_ge(s_pe, 1)
                for n in range(3):
                    dve.tensor_copy(tr[:, n, :], ps[:, 0, n * F:(n + 1) * F])
                link(dve.tensor_copy(tr[:, 3:5, :], ps[:, 1, 0:2 * F].rearrange("p (n f) -> p n f", n=2)))
                link(dve.reduce_sum(mean[:, 0:1], tr[:, 0, :], AX_X))
                link(dve.tensor_scalar(mean[:, 0:1], mean[:, 0:1], -1.0 / F, None, ALU.mult))
                dve.tensor_scalar(r.projc[:, :], tr[:, 0, :], mean[:, 0:1], None, ALU.add).then_inc(s_v, 1)
                dve.wait_ge(s_eye, 3)
                dve.tensor_scalar(bs[:, 0:H0], blk[:, :], col[:, 4:5], None, ALU.mult).then_inc(s_v, 1)
                dve.tensor_scalar(bs[:, H0:ATT], blk[:, :], col[:, 5:6], None, ALU.mult).then_inc(s_v, 1)
                link(dve.reduce_sum(mean[0:1, 1:2], rows[:, 0, :], AX_X))
                link(dve.tensor_scalar(mean[0:1, 1:2], mean[0:1, 1:2], -1.0 / F, None, ALU.mult))
                link(dve.tensor_scalar(rows[:, 4, :], rows[:, 0, :], mean[0:1, 1:2], None, ALU.add))
                dve.tensor_tensor(r.b2[:, 0:F], rows[:, 1, :], rows[:, 2, :], ALU.add)
                dve.wait_ge(s_pe, 2)
                dve.tensor_copy(r.w0[:, F + ATT:], ps[:, 2, 0:F])
                dve.tensor_copy(r.w0[:, F:F + ATT], ps[:, 2, F:F + ATT])
                dve.tensor_copy(r.w0[:, 0:F], ps[:, 2, 256:256 + F])
                dve.tensor_tensor(r.c0[:, :], ps[0:1, 3, 0:F], rows[:, 4, :], ALU.add)
                dve.tensor_copy(r.wa[:, :], ps[:, 3, F:2 * F])
                dve.tensor_copy(r.wu[:, F:2 * F], ps[:, 3, 2 * F:3 * F])
                dve.tensor_copy(r.b1[:, F:2 * F], ps[0:1, 3, 3 * F:4 * F])
                dve.tensor_copy(r.w3[:, 2, F:F + 1], ps[:, 4, 0:1])
                dve.tensor_copy(r.w3[:, 3, F:F + 1], ps[:, 4, 1:2])
                link(dve.tensor_tensor(r.b3[:, 1, F:F + 1], ps[0:1, 4, 2:3], rows[:, 3, 0:1], ALU.add))
                link(dve.tensor_copy(part[:, 0, :], r.bias[:, :]))
                link(dve.tensor_tensor(res[:, 0, :], r.bias[:, :], part[:, 0, :], ALU.subtract))
                link(dve.tensor_copy(part[:, 1, :], res[:, 0, :]))
                link(dve.tensor_tensor(res[:, 1, :], res[:, 0, :], part[:, 1, :], ALU.subtract))
                dve.tensor_copy(part[:, 2, :], res[:, 1, :]).then_inc(s_part, 1)
                dve.wait_ge(s_list, 64)
                dve.tensor_copy(lf[:, :, :], li[:, :, :]).then_inc(s_li, 1)
                dve.wait_ge(s_pe, 3)
                view = lambda t, h: t[:, :].rearrange("p (q h) -> p q h", h=2)[:, :, h]
                for h in range(2):
                    turned = lambda n: ps[:, 5 + n // 2, (n % 2 * 2 + h) * P:(n % 2 * 2 + h) * P + half]
                    dve.tensor_copy(view(r.src, h), turned(0))
                    dve.tensor_copy(view(r.srcf, h), turned(0))
                    dve.tensor_scalar(view(r.dstg, h), turned(1), 0.0, None, ALU.max)
                    dve.tensor_copy(view(r.dstf, h), turned(1))
                    dve.tensor_copy(view(prev, h), turned(3))
                    link(dve.tensor_copy(view(nxt, h), turned(2)))
                link(dve.tensor_tensor(same[:, :], nxt[:, :], r.dstf[:, :], ALU.is_equal))
                dve.scalar_tensor_tensor(r.last[:, :], same[:, :], float(SKIP), r.dstf[:, :], ALU.mult, ALU.add)
                link(dve.tensor_tensor(r.first[:, :], prev[:, :], r.dstf[:, :], ALU.not_equal))

                def segments(i, u):
                    dve.wait_ge(s_row[u], nth(i, u))
                    for v in range(BATCH):
                        ins = dve.tensor_scalar(r.seg[:, bass.ds(i * BATCH + v, 1), :], dr[:, u, 1 + v * P:1 + (v + 1) * P].unsqueeze(1),
                                                r.dstf[:, bass.ds(i * BATCH + v, 1)], None, ALU.is_equal)
                    for v in range(BATCH):
                        ins = dve.tensor_tensor(r.goes_on[:, bass.ds(i * BATCH + v, 1), :],
                                                dr[:, u, 1 + v * P:1 + (v + 1) * P].unsqueeze(1),
                                                dr[:, u, v * P:v * P + 1].unsqueeze(1).to_broadcast([P, 1, P]), ALU.is_equal)
                    ins.then_inc(s_seg, 1)

                pipeline(dve, ET // BATCH, [(0, segments)])



class Norm:

    def __init__(self, k, name, tiles=1):
        self.stat = k.sb(f"{name}_stat", [P, 4, tiles, 6])
        self.mv = k.sb(f"{name}_mv", [P, 4, tiles, 2])
        self.std = k.sb(f"{name}_std", [P, 4, tiles])
        self.rs = k.sb(f"{name}_rs", [P, 4, tiles])
        self.nm = k.sb(f"{name}_nm", [P, 4, tiles])
        self.s_bn, self.s_turn, self.s_mv, self.s_std, self.s_rs, self.s_nm = (
            k.sem(f"{name}_{x}") for x in ("bn", "turn", "mv", "std", "rs", "nm"))

    def stats(self, dve, src, i, u, p=P, j=1):
        for n in range(j):
            ins = dve.bn_stats(self.stat[0:p, u % 4, n, :], src(n))
        ins.then_inc(self.s_bn, 1)

    def aggregate(self, dve, i, u, p=P, j=1):
        dve.wait_ge(self.s_bn, i + 1)
        dve.sem_inc(self.s_turn, 1)
        for n in range(j):
            ins = dve.bn_aggr(self.mv[0:p, u % 4, n, :], self.stat[0:p, u % 4, n, :])
        ins.then_inc(self.s_mv, 1)

    def root(self, act, r, i, u, p=P, j=1):
        act.wait_ge(self.s_mv, i + 1)
        act.activation(self.std[0:p, u % 4, 0:j], self.mv[0:p, u % 4, 0:j, 1], ACT.Sqrt, bias=r.eps[0:p, :])\
           .then_inc(self.s_std, 1)

    def inverse(self, dve, i, u, p=P, j=1):
        dve.wait_ge(self.s_std, i + 1)
        dve.reciprocal(self.rs[0:p, u % 4, 0:j], self.std[0:p, u % 4, 0:j]).then_inc(self.s_rs, 1)

    def shift(self, dve, i, u, p=P, j=1):
        dve.wait_ge(self.s_rs, i + 1)
        dve.scalar_tensor_tensor(self.nm[0:p, u % 4, 0:j], self.mv[0:p, u % 4, 0:j, 0], -1.0, self.rs[0:p, u % 4, 0:j],
                                 ALU.mult, ALU.mult).then_inc(self.s_nm, 1)

    def relu(self, act, dst, src, i, u, p=P, j=1):
        act.wait_ge(self.s_nm, i + 1)
        for n in range(j):
            ins = act.activation(dst(n), src(n), ACT.Relu, scale=self.rs[0:p, u % 4, n:n + 1],
                                 bias=self.nm[0:p, u % 4, n:n + 1])
        return ins


def last_in(total, u):
    return (total - 1 - u) // RING * RING + u


def turned_width(p, j):
    return (j - 1) * F + p


def node_pass_0(nc, a, d, r):
    with Pass(nc, "n0") as k:
        t0 = k.sb("t0", [P, RING, J, T0W])
        t1 = k.sb("t1", [P, RING, J, T1W])
        h0 = k.sb("h0", [P, 2, J * F])
        ht = k.sb("ht", [P, 2, J * F])
        y = k.sb("y", [P, 2, J, F])
        na, nb, nn = Norm(k, "a", J), Norm(k, "b", J), Norm(k, "c", J)
        pst = k.ps("pst", [P, 2, 512])
        pso = k.ps("pso", [P, 2, J, 512])
        s_in, s_st0, s_st1 = k.ring("in"), k.ring("st0_"), k.ring("st1_")
        s_h0, s_tr, s_ht, s_mm, s_t0, s_y, s_yx, s_x1, s_h1 = (
            k.sem(x) for x in ("h0", "tr", "ht", "mm", "t0", "y", "yx", "x1", "h1"))
        x_of = lambda u, p: lambda n: t0[0:p, u, n, F + ATT:]
        with nc.Block() as block:
            @block.sync
            def _(sp):
                def load(g, u):
                    p, j = span(g)
                    reached(sp, s_st0[u], nth(g, u) - 16)
                    reached(sp, s_yx, g - RING + 1)
                    sp.dma_start(t0[0:p, u, 0:j, F + ATT:], node_rows(a["x"], g)).then_inc(s_in[u], 16)

                def store_0(g, u):
                    p, j = span(g)
                    sp.wait_ge(s_t0, g + 1)
                    sp.dma_start(node_rows(d.t0, g), t0[0:p, u, 0:j, :]).then_inc(s_st0[u], 16)

                def store_1(g, u):
                    p, j = span(g)
                    sp.wait_ge(s_h1, g + 1)
                    sp.dma_start(node_rows(d.t1, g), t1[0:p, u, 0:j, :]).then_inc(s_st1[u], 16)

                pipeline(sp, NGROUPS, [(7, store_0), (0, load), (9, store_1)])
                for u in range(RING):
                    sp.wait_ge(s_st0[u], nth(last_in(NGROUPS, u), u))
                    sp.wait_ge(s_st1[u], nth(last_in(NGROUPS, u), u))

            @block.vector
            def _(dve):
                def stats_a(g, u):
                    dve.wait_ge(s_in[u], nth(g, u))
                    na.stats(dve, x_of(u, span(g)[0]), g, u, *span(g))

                def stats_b(g, u):
                    p, j = span(g)
                    dve.wait_ge(s_t0, g + 1)
                    nb.stats(dve, lambda n: pso[0:p, u % 2, n, F + ATT:T0W], g, u, p, j)

                def stats_c(g, u):
                    p, j = span(g)
                    dve.wait_ge(s_x1, g + 1)
                    nn.stats(dve, lambda n: t1[0:p, u, n, 0:F], g, u, p, j)

                def affine(g, u):
                    p, j = span(g)
                    dve.wait_ge(nb.s_rs, g + 1)
                    for n in range(j):
                        ins = dve.scalar_tensor_tensor(y[0:p, u % 2, n, :], pso[0:p, u % 2, n, F + ATT:T0W],
                                                       nb.rs[0:p, u % 4, n:n + 1], r.gamma[0:p, :], ALU.mult, ALU.mult)
                    ins.then_inc(s_y, 1)

                def add_x(g, u):
                    p, j = span(g)
                    dve.wait_ge(s_y, g + 1)
                    dve.tensor_tensor(y[0:p, u % 2, 0:j, :], y[0:p, u % 2, 0:j, :], t0[0:p, u, 0:j, F + ATT:], ALU.add)\
                       .then_inc(s_yx, 1)

                def add_beta(g, u):
                    p, j = span(g)
                    dve.wait_ge(s_yx, g + 1)
                    reached(dve, s_st1[u], nth(g, u) - 16)
                    dve.tensor_tensor(t1[0:p, u, 0:j, 0:F], y[0:p, u % 2, 0:j, :],
                                      r.beta[0:p, :].unsqueeze(1).to_broadcast([p, j, F]), ALU.add).then_inc(s_x1, 1)

                on = lambda step: lambda g, u: step(dve, g, u, *span(g))
                pipeline(dve, NGROUPS, [
                    (0, stats_a), (5, stats_c), (0, on(na.aggregate)), (5, on(nn.aggregate)), (1, on(na.inverse)),
                    (6, on(nn.inverse)), (4, on(nb.inverse)), (1, on(na.shift)), (6, on(nn.shift)), (4, affine),
                    (3, stats_b), (4, add_x), (3, on(nb.aggregate)), (4, add_beta)])

            @block.scalar
            def _(act):
                def relu_a(g, u):
                    p, j = span(g)
                    reached(act, s_tr, g - 1)
                    na.relu(act, lambda n: h0[0:p, u % 2, n * F:(n + 1) * F], x_of(u, p), g, u, p, j).then_inc(s_h0, 1)

                def turned(g, u):
                    act.wait_ge(s_tr, g + 1)
                    reached(act, s_mm, g - 1)
                    w = turned_width(*span(g))
                    act.activation(ht[:, u % 2, 0:w], pst[:, u % 2, 0:w], ACT.Copy).then_inc(s_ht, 1)

                def keep(g, u):
                    p, j = span(g)
                    act.wait_ge(s_mm, g + 1)
                    act.activation(t0[0:p, u, 0:j, 0:F + ATT], pso[0:p, u % 2, 0:j, 0:F + ATT], ACT.Copy).then_inc(s_t0, 1)

                def relu_c(g, u):
                    p, j = span(g)
                    nn.relu(act, lambda n: t1[0:p, u, n, F:], lambda n: t1[0:p, u, n, 0:F], g, u, p, j).then_inc(s_h1, 1)

                root = lambda norm: lambda g, u: norm.root(act, r, g, u, *span(g))
                pipeline(act, NGROUPS, [(1, root(na)), (6, root(nn)), (4, root(nb)), (3, keep), (2, turned), (1, relu_a),
                                        (6, relu_c)])

            @block.tensor
            def _(pe):
                def turn(g, u):
                    p, j = span(g)
                    pe.wait_ge(s_h0, g + 1)
                    reached(pe, s_ht, g - 1)
                    for n in range(j):
                        ins = pe.transpose(pst[:, u % 2, n * F:n * F + p], h0[0:p, u % 2, n * F:(n + 1) * F], r.ident[0:p, 0:p])
                    ins.then_inc(s_tr, 1)

                def product(g, u):
                    p, j = span(g)
                    pe.wait_ge(s_ht, g + 1)
                    reached(pe, s_t0, g - 1)
                    reached(pe, s_y, g - 1)
                    for n in range(j):
                        pe.matmul(pso[0:p, u % 2, n, 0:T0W], ht[:, u % 2, n * F:n * F + p], r.w0[:, :], start=True, stop=False)
                        ins = pe.matmul(pso[0:p, u % 2, n, F + ATT:T0W], r.ones[0:1, 0:p], r.c0[:, :], start=False, stop=True)
                    ins.then_inc(s_mm, 1)

                pipeline(pe, NGROUPS, [(3, product), (2, turn)])


def node_pass_1(nc, d, r):
    cols = F + 1
    with Pass(nc, "n1") as k:
        t1 = k.sb("t1", [P, RING, J, T1W])
        ht = k.sb("ht", [P, 3, J * F])
        x2 = k.sb("x2", [P, 4, J, F])
        h2 = k.sb("h2", [P, 4, J, F])
        g1 = k.sb("g1", [P, 4, J, F])
        o = k.sb("o", [P, 4, J, HPW])
        ex = k.sb("ex", [P, 2, J])
        e1 = k.sb("e1", [P, 2, J])
        nn = Norm(k, "c", J)
        pst = k.ps("pst", [P, 3, 512])
        pso = k.ps("pso", [P, 3, 512])
        s_t1, s_stx, s_sth, s_stg, s_sto = (k.ring(x) for x in ("t1_", "stx", "sth", "stg", "sto"))
        s_x2, s_h2, s_g, s_ex, s_e1, s_o, s_sc, s_pre = (k.sem(x) for x in ("x2", "h2", "g", "ex", "e1", "o", "sc", "pre"))
        s_tr, s_ht, s_mm = ([k.sem(f"{x}{n}") for n in range(3)] for x in ("tr", "ht", "mm"))
        view = lambda u, p, j: pso[0:p, 2, 0:J * cols].rearrange("p (j f) -> p j f", j=J)[:, 0:j, :]
        grid = lambda n, p, j: pso[0:p, n, 0:J * F].rearrange("p (j f) -> p j f", j=J)[:, 0:j, :]
        with nc.Block() as block:
            @block.sync
            def _(sp):
                def load(g, u):
                    p, j = span(g)
                    reached(sp, s_x2, g - RING + 1)
                    reached(sp, s_tr[0], g - RING + 1)
                    sp.dma_start(t1[0:p, u, 0:j, :], node_rows(d.t1, g)).then_inc(s_t1[u], 16)

                def store(ready, table, rows, sems):
                    def stage(g, u):
                        p, j = span(g)
                        sp.wait_ge(ready, g + 1)
                        sp.dma_start(node_rows(table, g), rows[0:p, u % 4, 0:j, :]).then_inc(sems[u], 16)
                    return stage

                pipeline(sp, NGROUPS, [(0, load), (3, store(s_x2, d.x3, x2, s_stx)), (4, store(s_h2, d.h2, h2, s_sth)),
                                       (6, store(s_g, d.g, g1, s_stg)), (8, store(s_sc, d.hp, o, s_sto))])
                for sems in (s_stx, s_sth, s_stg, s_sto):
                    drained(sp, sems, NGROUPS)

            @block.vector
            def _(dve):
                dve.memset(o[:, :, :, F:], 0.0).then_inc(s_pre, 1)
                dve.wait_ge(s_pre, 1)

                def turned(n):
                    def stage(g, u):
                        w = turned_width(*span(g))
                        dve.wait_ge(s_tr[n], g + 1)
                        reached(dve, s_mm[n], g)
                        dve.tensor_copy(ht[:, n, 0:w], pst[:, n, 0:w]).then_inc(s_ht[n], 1)
                    return stage

                def add(g, u):
                    p, j = span(g)
                    dve.wait_ge(s_mm[0], g + 1)
                    sent(dve, s_stx, g, u, 4)
                    dve.tensor_tensor(x2[0:p, u % 4, 0:j, :], t1[0:p, u, 0:j, 0:F], grid(0, p, j), ALU.add).then_inc(s_x2, 1)

                def stats(g, u):
                    p, j = span(g)
                    dve.wait_ge(s_x2, g + 1)
                    nn.stats(dve, lambda n: x2[0:p, u % 4, n, :], g, u, p, j)

                def plus_one(g, u):
                    p, j = span(g)
                    dve.wait_ge(s_ex, g + 1)
                    dve.tensor_scalar(e1[0:p, u % 2, 0:j], ex[0:p, u % 2, 0:j], 1.0, None, ALU.add).then_inc(s_e1, 1)

                def sigmoid(g, u):
                    p, j = span(g)
                    dve.wait_ge(s_e1, g + 1)
                    dve.wait_ge(s_o, g + 1)
                    dve.reciprocal(o[0:p, u % 4, 0:j, F:F + 1], e1[0:p, u % 2, 0:j].unsqueeze(2)).then_inc(s_sc, 1)

                on = lambda step: lambda g, u: step(dve, g, u, *span(g))
                pipeline(dve, NGROUPS, [(2, add), (7, plus_one), (0, turned(0)), (3, on(nn.inverse)), (2, stats), (6, turned(2)),
                                        (3, on(nn.shift)), (2, on(nn.aggregate)), (7, sigmoid)])

            @block.scalar
            def _(act):
                def turned(g, u):
                    w = turned_width(*span(g))
                    act.wait_ge(s_tr[1], g + 1)
                    reached(act, s_mm[1], g)
                    act.activation(ht[:, 1, 0:w], pst[:, 1, 0:w], ACT.Copy).then_inc(s_ht[1], 1)

                def relu_h(g, u):
                    p, j = span(g)
                    sent(act, s_sth, g, u, 4)
                    nn.relu(act, lambda n: h2[0:p, u % 4, n, :], lambda n: x2[0:p, u % 4, n, :], g, u, p, j).then_inc(s_h2, 1)

                def relu_g(g, u):
                    p, j = span(g)
                    act.wait_ge(s_mm[1], g + 1)
                    sent(act, s_stg, g, u, 4)
                    act.activation(g1[0:p, u % 4, 0:j, :], grid(1, p, j), ACT.Relu).then_inc(s_g, 1)

                def exp(g, u):
                    p, j = span(g)
                    act.wait_ge(s_mm[2], g + 1)
                    reached(act, s_e1, g - 1)
                    act.activation(ex[0:p, u % 2, 0:j], view(u, p, j)[:, :, F], ACT.Exp, scale=-1.0).then_inc(s_ex, 1)

                def finish(g, u):
                    p, j = span(g)
                    sent(act, s_sto, g, u, 4)
                    act.activation(o[0:p, u % 4, 0:j, 0:F], view(u, p, j)[:, :, 0:F], ACT.Copy).then_inc(s_o, 1)

                act.wait_ge(s_pre, 1)
                pipeline(act, NGROUPS, [(3, lambda g, u: nn.root(act, r, g, u, *span(g))), (4, turned), (7, exp), (7, finish),
                                        (5, relu_g), (3, relu_h)])

            @block.tensor
            def _(pe):
                def turn(n):
                    def stage(g, u):
                        p, j = span(g)
                        if n == 0:
                            pe.wait_ge(s_t1[u], nth(g, u))
                        else:
                            pe.wait_ge((s_h2, s_g)[n - 1], g + 1)
                        reached(pe, s_ht[n], g)
                        rows = lambda v: (t1[0:p, u, v, F:], h2[0:p, u % 4, v, :], g1[0:p, u % 4, v, :])[n]
                        for v in range(j):
                            ins = pe.transpose(pst[:, n, v * F:v * F + p], rows(v), r.ident[0:p, 0:p])
                        ins.then_inc(s_tr[n], 1)
                    return stage

                def product(n):
                    def stage(g, u):
                        p, j = span(g)
                        w = (F, F, cols)[n]
                        pe.wait_ge(s_ht[n], g + 1)
                        reached(pe, (s_x2, s_g, s_o)[n], g)
                        weights = (r.wu[:, 0:F], r.w3[:, 0, 0:F], r.w3[:, 2, 0:cols])[n]
                        bias = (B1, B3, B3 + F + 1)[n]
                        for v in range(j):
                            ps = pso[0:p, n, v * w:(v + 1) * w]
                            pe.matmul(ps, ht[:, n, v * F:v * F + p], weights, start=True, stop=False)
                            ins = pe.matmul(ps, r.ones3[:, 0:p], r.bias3[:, bias:bias + w], start=False, stop=True)
                        ins.then_inc(s_mm[n], 1)
                    return stage

                pipeline(pe, NGROUPS, [(0, turn(0)), (1, product(0)), (4, turn(1)), (6, turn(2)), (5, product(1)), (7, product(2))])


def node_pass_2(nc, d, r, out):
    with Pass(nc, "n2") as k:
        a = k.sb("a", [P, RING, J, HPW])
        x3 = k.sb("x3", [P, RING, J, F])
        ka = k.sb("ka", [P, 2, J, F])
        ht = k.sb("ht", [P, 2, 2, J * F])
        up = k.sb("up", [P, RING, J, F])
        o = k.sb("o", [P, RING, J, F])
        pst = k.ps("pst", [P, 2, 2, 512])
        pso = k.ps("pso", [P, 2, 2, 512])
        s_in, s_x3, s_stu, s_sto = (k.ring(x) for x in ("in", "x3_", "stu", "sto"))
        s_ka, s_up, s_o = (k.sem(x) for x in ("ka", "up", "o"))
        s_tr, s_ht, s_mm = ([k.sem(f"{x}{n}") for n in range(2)] for x in ("tr", "ht", "mm"))
        grid = lambda n, u, p, j: pso[0:p, n, u % 2, 0:J * F].rearrange("p (j f) -> p j f", j=J)[:, 0:j, :]
        with nc.Block() as block:
            @block.sync
            def _(sp):
                def load(g, u):
                    p, j = span(g)
                    reached(sp, s_ka, g - RING + 1)
                    sp.dma_start(a[0:p, u, 0:j, :], node_rows(d.hp, g)).then_inc(s_in[u], 16)
                    reached(sp, s_o, g - RING + 1)
                    sp.dma_start(x3[0:p, u, 0:j, :], node_rows(d.x3, g)).then_inc(s_x3[u], 16)

                def store(g, u):
                    p, j = span(g)
                    sp.wait_ge(s_up, g + 1)
                    sp.dma_start(node_rows(d.up, g), up[0:p, u, 0:j, :]).then_inc(s_stu[u], 16)
                    sp.wait_ge(s_o, g + 1)
                    sp.dma_start(node_rows(out, g), o[0:p, u, 0:j, :]).then_inc(s_sto[u], 16)

                pipeline(sp, NGROUPS, [(0, load), (7, store)])
                drained(sp, s_stu, NGROUPS)
                drained(sp, s_sto, NGROUPS)

            @block.vector
            def _(dve):
                def keep(g, u):
                    p, j = span(g)
                    dve.wait_ge(s_in[u], nth(g, u))
                    reached(dve, s_tr[0], g - 1)
                    for n in range(j):
                        ins = dve.tensor_scalar(ka[0:p, u % 2, n, :], a[0:p, u, n, 0:F], r.keep[0:p, bass.ds(g * J + n, 1)],
                                                None, ALU.mult)
                    ins.then_inc(s_ka, 1)

                def turned(g, u):
                    w = turned_width(*span(g))
                    dve.wait_ge(s_tr[1], g + 1)
                    reached(dve, s_mm[1], g - 1)
                    dve.tensor_copy(ht[:, 1, u % 2, 0:w], pst[:, 1, u % 2, 0:w]).then_inc(s_ht[1], 1)

                def add(g, u):
                    p, j = span(g)
                    dve.wait_ge(s_mm[1], g + 1)
                    dve.wait_ge(s_x3[u], nth(g, u))
                    reached(dve, s_sto[u], nth(g, u) - 16)
                    dve.tensor_tensor(o[0:p, u, 0:j, :], x3[0:p, u, 0:j, :], grid(1, u, p, j), ALU.add).then_inc(s_o, 1)

                pipeline(dve, NGROUPS, [(0, keep), (4, add), (3, turned)])

            @block.scalar
            def _(act):
                def turned(g, u):
                    w = turned_width(*span(g))
                    act.wait_ge(s_tr[0], g + 1)
                    reached(act, s_mm[0], g - 1)
                    act.activation(ht[:, 0, u % 2, 0:w], pst[:, 0, u % 2, 0:w], ACT.Copy).then_inc(s_ht[0], 1)

                def relu(g, u):
                    p, j = span(g)
                    act.wait_ge(s_mm[0], g + 1)
                    reached(act, s_stu[u], nth(g, u) - 16)
                    act.activation(up[0:p, u, 0:j, :], grid(0, u, p, j), ACT.Relu).then_inc(s_up, 1)

                pipeline(act, NGROUPS, [(2, relu), (1, turned)])

            @block.tensor
            def _(pe):
                def turn(n):
                    def stage(g, u):
                        p, j = span(g)
                        pe.wait_ge((s_ka, s_up)[n], g + 1)
                        reached(pe, s_ht[n], g - 1)
                        for v in range(j):
                            ins = pe.transpose(pst[:, n, u % 2, v * F:v * F + p], (ka[0:p, u % 2, v, :], up[0:p, u, v, :])[n],
                                               r.ident[0:p, 0:p])
                        ins.then_inc(s_tr[n], 1)
                    return stage

                def product(n):
                    def stage(g, u):
                        p, j = span(g)
                        pe.wait_ge(s_ht[n], g + 1)
                        reached(pe, (s_up, s_o)[n], g - 1)
                        bias = B3 + (2 + n) * (F + 1)
                        for v in range(j):
                            ps = pso[0:p, n, u % 2, v * F:(v + 1) * F]
                            pe.matmul(ps, ht[:, n, u % 2, v * F:v * F + p], r.w3[:, 4 + 2 * n, 0:F], start=True, stop=False)
                            ins = pe.matmul(ps, r.ones3[:, 0:p], r.bias3[:, bias:bias + F], start=False, stop=True)
                        ins.then_inc(s_mm[n], 1)
                    return stage

                pipeline(pe, NGROUPS, [(0, turn(0)), (3, product(1)), (1, product(0)), (2, turn(1))])


def collect(nc, d, r):
    with Pass(nc, "col") as k:
        a = k.sb("a", [P, RING, J, HPW])
        s_in = k.ring("in")
        s_z, s_pre = k.sem("z"), k.sem("pre")
        with nc.Block() as block:
            @block.sync
            def _(sp):
                def load(g, u):
                    p, j = span(g)
                    reached(sp, s_z, g - RING + 1)
                    sp.dma_start(a[0:p, u, 0:j, :], node_rows(d.hp, g)).then_inc(s_in[u], 16)

                pipeline(sp, NGROUPS, [(0, load)])

            @block.vector
            def _(dve):
                dve.memset(r.z[:, :, :], -1.0).then_inc(s_pre, 1)
                dve.wait_ge(s_pre, 1)

                def score(g, u):
                    p, j = span(g)
                    dve.wait_ge(s_in[u], nth(g, u))
                    dve.sem_inc(s_pre, 1)
                    dve.tensor_copy(r.z[0:p, bass.ds(g, 1), 0:j], a[0:p, u, 0:j, F].unsqueeze(1)).then_inc(s_z, 1)

                pipeline(dve, NGROUPS, [(0, score)])


class SegmentSum:

    def __init__(self, k, r, parts=1):
        self.r, self.parts = r, parts
        self.sf = k.sb("segf", [P, 4, P])
        self.st = k.sb("sums", [P, 4, parts, P])
        self.ps = k.ps("ps_sum", [P, 2, 512])
        self.s_sf, self.s_turn, self.s_sum, self.s_st = (k.sem(x) for x in ("sf", "sf_turn", "sum", "st"))

    def clear(self, dve):
        dve.memset(self.st[:, :, :, :], 0.0).then_inc(self.s_st, 1)

    def widen(self, act, t, u):
        reached(act, self.s_sum, t - 3)
        act.sem_inc(self.s_turn, 1)
        act.activation(self.sf[:, u % 4, :], self.r.seg[:, bass.ds(t, 1), :].rearrange("p a f -> p (a f)"), ACT.Copy)\
           .then_inc(self.s_sf, 1)

    def sum(self, pe, rows, t, u):
        pe.wait_ge(self.s_sf, t + 1)
        reached(pe, self.s_st, t)
        for n, part in enumerate(rows):
            ins = pe.matmul(self.ps[:, u % 2, n * P:(n + 1) * P], part, self.sf[:, u % 4, :], start=True, stop=True)
        ins.then_inc(self.s_sum, 1)

    def follow(self, dve, used, t, u):
        dve.wait_ge(self.s_sum, t + 1)
        dve.wait_ge(self.s_st, t + 1)
        reached(dve, used, t - 3)
        for n in range(self.parts):
            ins = dve.scalar_tensor_tensor(self.st[:, u % 4, n, :].unsqueeze(1), self.r.goes_on[:, bass.ds(t, 1), :],
                                           self.st[:, (u - 1) % 4, n, P - 1:P], self.ps[:, u % 2, n * P:(n + 1) * P].unsqueeze(1),
                                           ALU.mult, ALU.add)
        ins.then_inc(self.s_st, 1)


class Indices:

    def __init__(self, k, name, table):
        self.table = table
        self.at = k.sb(name, [P, RING], I32)
        self.s, self.s_turn, self.s_pool = k.sem(name), k.sem(f"{name}_turn"), k.sem(f"{name}_pool")

    def stage(self, dve, t, u, used):
        reached(dve, used[u], nth(t, u) - 16)
        dve.sem_inc(self.s_turn, 1)
        dve.tensor_copy(self.at[:, u:u + 1], self.table[:, bass.ds(t, 1)]).then_inc(self.s, 1)

    def gather(self, pool, dst, table, t, u, arrived):
        pool.wait_ge(self.s, t + 1)
        pool.sem_inc(self.s_pool, 1)
        pool.indirect_dma_start(dst, None, table, bass.IndirectOffsetOnAxis(ap=self.at[:, u:u + 1], axis=0))\
            .then_inc(arrived[u], 16)

    def scatter(self, pool, table, src, t, u, written):
        pool.wait_ge(self.s, t + 1)
        pool.sem_inc(self.s_pool, 1)
        pool.indirect_dma_start(table, bass.IndirectOffsetOnAxis(ap=self.at[:, u:u + 1], axis=0), src, None,
                                bounds_check=N - 1, oob_is_err=False).then_inc(written[u], 16)


def drained(eng, sems, total):
    for u in range(RING):
        eng.wait_ge(sems[u], nth(last_in(total, u), u))


def edge_pass_0a(nc, d, r):
    with Pass(nc, "e0a") as k:
        gs = k.sb("gs", [P, RING, T0W])
        gd = k.sb("gd", [P, RING, T0W])
        src, dst = Indices(k, "src", r.src), Indices(k, "dst", r.dstg)
        s_gs, s_gd, s_eh, s_ed = (k.ring(x) for x in ("gs", "gd", "eh", "ed"))
        s_l = k.sem("l")
        with nc.Block() as block:
            @block.gpsimd
            def _(pool):
                def gather(t, u):
                    reached(pool, s_eh[u], nth(t, u) - 16)
                    reached(pool, s_ed[u], nth(t, u) - 16)
                    reached(pool, s_l, t - RING + 1)
                    src.gather(pool, gs[:, u, :], d.t0, t, u, s_gs)
                    dst.gather(pool, gd[:, u, :], d.t0, t, u, s_gd)

                pipeline(pool, ET, [(0, gather)])

            @block.sync
            def _(sp):
                def keep(t, u):
                    sp.wait_ge(s_gs[u], nth(t, u))
                    sp.dma_start(edge_rows(d.eh, t), gs[:, u, 0:F]).then_inc(s_eh[u], 16)
                    sp.wait_ge(s_gd[u], nth(t, u))
                    sp.dma_start(edge_rows(d.ed, t), gd[:, u, :]).then_inc(s_ed[u], 16)

                pipeline(sp, ET, [(0, keep)])
                drained(sp, s_eh, ET)
                drained(sp, s_ed, ET)

            @block.vector
            def _(dve):
                def logits(t, u):
                    dve.wait_ge(s_gs[u], nth(t, u))
                    dve.wait_ge(s_gd[u], nth(t, u))
                    dve.tensor_tensor(r.logit[:, bass.ds(t, 1), :], gs[:, u, F:F + H0].unsqueeze(1),
                                      gd[:, u, F + H0:F + ATT].unsqueeze(1), ALU.add)
                    dve.tensor_tensor(r.self_logit[:, bass.ds(t, 1), :], gd[:, u, F:F + H0].unsqueeze(1),
                                      gd[:, u, F + H0:F + ATT].unsqueeze(1), ALU.add).then_inc(s_l, 1)

                pipeline(dve, ET, [(0, lambda t, u: src.stage(dve, t, u, s_gs)), (0, lambda t, u: dst.stage(dve, t, u, s_gd)),
                                   (3, logits)])


def softmax_weights(nc, d, r, name, own_loop):
    rows = H0 * CH
    with Pass(nc, name) as k:
        xp = k.sb("xp", [P, CT, H0, CH])
        xt = k.sb("xt", [rows, CL])
        fw = k.sb("fw", [rows, CL])
        ids = k.sb("ids", [rows, 3, CL], I32)
        gate = k.sb("gate", [rows, 2, CL])
        eid = k.sb("eid", [H0, 4, CH], I32)
        egate = k.sb("egate", [H0, 2, CH])
        es = k.sb("es", [H0, 2, CH])
        ec = k.sb("ec", [H0, CH])
        cin = k.sb("cin", [rows, 1])
        mx = k.sb("mx", [P, ET, H0])
        ps = k.ps("ps", [P, 8, 512])
        s_ids, s_eid, s_xp, s_up, s_dn, s_x = (k.sem(x) for x in ("ids", "eid", "xp", "up", "dn", "x"))
        s_v, s_e, s_a = k.sem("v"), k.sem("e"), k.sem("a")
        s_hop = [k.sem(f"hop{n}") for n in range(4)]
        s_end, s_in = k.sem("end"), k.sem("in")
        with nc.Block() as block:
            @block.sync
            def _(sp):
                for n in range(3):
                    for h in range(H0):
                        sp.dma_start(ids[h * CH:(h + 1) * CH, n, :], d.dst[n:n + EPAD].rearrange("(c e) -> c e", c=CH))\
                          .then_inc(s_ids, 16)
                with nc.allow_non_contiguous_dma(reason="four words of each chunk"):
                    for n, at in enumerate((0, CL, CL + 1, 1)):
                        sp.dma_start(eid[:, n, :], d.dst[at:at + EPAD].rearrange("(a c e) -> a c e", a=1, e=CL)[:, :, 0]
                                     .to_broadcast([H0, CH])).then_inc(s_eid, 16)
                for n in range(2):
                    sp.wait_ge(s_end, n + 1)
                    with nc.allow_non_contiguous_dma(reason="one word a partition"):
                        sp.dma_start(d.hop[2 * n:2 * n + 1, :].rearrange("a (n b) -> (a n) b", b=1),
                                     fw[:, CL - 1:CL] if n == 0 else xt[:, 0:1]).then_inc(s_hop[2 * n], 16)
                        sp.wait_ge(s_hop[2 * n], 16)
                        sp.dma_start(es[:, n, :], d.hop[2 * n, :].rearrange("(h c) -> h c", c=CH)).then_inc(s_hop[2 * n], 16)
                        sp.wait_ge(s_in, n + 1)
                        sp.dma_start(d.hop[2 * n + 1, :].rearrange("(h c) -> h c", c=CH), ec[:, :]).then_inc(s_hop[2 * n + 1], 16)
                        sp.wait_ge(s_hop[2 * n + 1], 16)
                        sp.dma_start(cin[:, :], d.hop[2 * n + 1:2 * n + 2, :].rearrange("a (n b) -> (a n) b", b=1))\
                          .then_inc(s_hop[2 * n + 1], 16)

            @block.vector
            def _(dve):
                done = 0

                def link(ins):
                    nonlocal done
                    done += 1
                    ins.then_inc(s_v, 1)
                    dve.wait_ge(s_v, done)

                if own_loop:
                    for v in (r.logit, r.self_logit):
                        ins = dve.scalar_tensor_tensor(v[:, :, :], v[:, :, :], 0.2, v[:, :, :], ALU.mult, ALU.max)
                    link(ins)
                else:
                    link(dve.memset(r.logit[:, :, H2:], 0.0))
                    link(dve.tensor_scalar(r.logit[:, :, 0:H2], r.logit[:, :, 0:H2], r.attb[:, :], None, ALU.add))
                for h in range(H0):
                    ins = dve.tensor_copy(xp[:, :, h, :], r.logit[:, :, h].rearrange("p (c j) -> p j c", j=CT))
                ins.then_inc(s_xp, 1)
                dve.wait_ge(s_ids, 16 * 3 * H0)
                dve.tensor_tensor(gate[:, 0, :], ids[:, 0, :], ids[:, 1, :], ALU.is_equal)
                link(dve.tensor_tensor(gate[:, 1, :], ids[:, 2, :], ids[:, 1, :], ALU.is_equal))
                dve.wait_ge(s_eid, 16 * 4)
                dve.tensor_tensor(egate[:, 0, :], eid[:, 0, :], eid[:, 1, :], ALU.is_equal)
                dve.tensor_tensor(egate[:, 1, :], eid[:, 2, :], eid[:, 3, :], ALU.is_equal)
                link(dve.tensor_scalar(gate[:, :, :], gate[:, :, :], 2 * BIG, -BIG, ALU.mult, ALU.add))
                link(dve.tensor_scalar(egate[:, :, :], egate[:, :, :], 2 * BIG, -BIG, ALU.mult, ALU.add))
                for b in range(4):
                    w = min(4, CT - 4 * b) * P
                    dve.wait_ge(s_up, b + 1)
                    ins = dve.tensor_copy(xt[:, 4 * b * P:4 * b * P + w], ps[0:rows, b, 0:w])
                link(ins)
                link(dve.tensor_tensor_scan(fw[:, :], gate[:, 0, :], xt[:, :], initial=-BIG, op0=ALU.min, op1=ALU.max))
                link(dve.memset(ec[:, :], -BIG))
                dve.sem_inc(s_end, 1)
                dve.wait_ge(s_hop[0], 32)
                link(dve.tensor_tensor_scan(es[:, 0, :], egate[:, 0, :], es[:, 0, :], initial=-BIG, op0=ALU.min, op1=ALU.max))
                dve.tensor_copy(ec[:, 1:CH], es[:, 0, 0:CH - 1]).then_inc(s_in, 1)
                dve.wait_ge(s_hop[1], 32)
                link(dve.tensor_tensor_scan(fw[:, :], gate[:, 0, :], xt[:, :], initial=cin[:, :], op0=ALU.min, op1=ALU.max))
                link(dve.tensor_tensor_scan(xt[:, ::-1], gate[:, 1, ::-1], fw[:, ::-1], initial=-BIG, op0=ALU.min, op1=ALU.max))
                link(dve.memset(ec[:, :], -BIG))
                dve.sem_inc(s_end, 1)
                dve.wait_ge(s_hop[2], 32)
                link(dve.tensor_tensor_scan(es[:, 1, ::-1], egate[:, 1, ::-1], es[:, 1, ::-1], initial=-BIG, op0=ALU.min, op1=ALU.max))
                dve.tensor_copy(ec[:, 0:CH - 1], es[:, 1, 1:CH]).then_inc(s_in, 1)
                dve.wait_ge(s_hop[3], 32)
                dve.tensor_tensor_scan(xt[:, ::-1], gate[:, 1, ::-1], fw[:, ::-1], initial=cin[:, :], op0=ALU.min, op1=ALU.max)\
                   .then_inc(s_x, 1)
                for b in range(4):
                    m = min(4, CT - 4 * b)
                    dve.wait_ge(s_dn, b + 1)
                    for j in range(m):
                        ins = dve.tensor_copy(mx[:, :, :].rearrange("p (c j) h -> p j h c", j=CT)[:, 4 * b + j, :, :],
                                              ps[:, 4 + b, j * P:j * P + rows].rearrange("p (h c) -> p h c", c=CH))
                link(ins)
                if own_loop:
                    link(dve.tensor_tensor(mx[:, :, :], mx[:, :, :], r.self_logit[:, :, :], ALU.max))
                    dve.tensor_tensor(r.self_logit[:, :, :], r.self_logit[:, :, :], mx[:, :, :], ALU.subtract)
                dve.tensor_tensor(r.logit[:, :, :], r.logit[:, :, :], mx[:, :, :], ALU.subtract).then_inc(s_e, 1)
                if own_loop:
                    dve.wait_ge(s_a, 2)
                    link(dve.tensor_tensor(r.self_logit[:, :, :], r.self_logit[:, :, :],
                                           r.first[:, :].unsqueeze(2).to_broadcast([P, ET, H0]), ALU.mult))
                    dve.tensor_tensor(r.both[:, :, :], r.logit[:, :, :], r.self_logit[:, :, :], ALU.add)

            @block.scalar
            def _(act):
                act.wait_ge(s_e, 1)
                act.activation(r.logit[:, :, :], r.logit[:, :, :], ACT.Exp).then_inc(s_a, 1)
                if own_loop:
                    act.activation(r.self_logit[:, :, :], r.self_logit[:, :, :], ACT.Exp).then_inc(s_a, 1)

            @block.tensor
            def _(pe):
                pe.wait_ge(s_xp, 1)
                for j in range(CT):
                    ins = pe.transpose(ps[0:rows, j // 4, j % 4 * P:(j % 4 + 1) * P], xp[:, j, :, :].rearrange("p h c -> p (h c)"),
                                       r.ident[:, :])
                    if j % 4 == 3 or j == CT - 1:
                        ins.then_inc(s_up, 1)
                pe.wait_ge(s_x, 1)
                for j in range(CT):
                    ins = pe.transpose(ps[:, 4 + j // 4, j % 4 * P:j % 4 * P + rows], xt[:, j * P:(j + 1) * P],
                                       r.ident[0:rows, 0:rows])
                    if j % 4 == 3 or j == CT - 1:
                        ins.then_inc(s_dn, 1)


def edge_pass_2a(nc, a, d, r):
    with Pass(nc, "e2a") as k:
        gs = k.sb("gs", [P, RING, F])
        gd = k.sb("gd", [P, RING, F])
        ea = k.sb("ea", [P, RING, F])
        xt = k.sb("xt", [P, 2, 3 * F])
        e = k.sb("e", [P, RING, F])
        z, zc, uu, w, w2, wi, zw, zv = (k.sb(x, [P, 4, F]) for x in ("z", "zc", "uu", "w", "w2", "wi", "zw", "zv"))
        src, dst = Indices(k, "src", r.src), Indices(k, "dst", r.dstg)
        pst = k.ps("pst", [P, 2, 512])
        pso = k.ps("pso", [P, 2, 512])
        s_gs, s_gd, s_ea, s_e = (k.ring(x) for x in ("gs", "gd", "ea", "e"))
        names = ("pad", "tr", "xt", "mm", "ev", "z", "zc", "u", "w", "w2", "wi", "zw", "zv", "zz", "l")
        s_pad, s_tr, s_xt, s_mm, s_ev, s_z, s_zc, s_u, s_w, s_w2, s_wi, s_zw, s_zv, s_zz, s_l = (k.sem(x) for x in names)
        with nc.Block() as block:
            @block.gpsimd
            def _(pool):
                def gather(t, u):
                    reached(pool, s_tr, t - RING + 1)
                    src.gather(pool, gs[:, u, :], d.h2, t, u, s_gs)
                    dst.gather(pool, gd[:, u, :], d.h2, t, u, s_gd)

                pipeline(pool, ET, [(0, gather)])

            @block.sync
            def _(sp):
                def load(t, u):
                    n = EREST if isinstance(t, int) and t == ET - 1 else P
                    reached(sp, s_tr, t - RING + 1)
                    sp.dma_start(ea[0:n, u, :], edge_rows(a["edge_attr_128"], t, n)).then_inc(s_ea[u], 16)

                def store(t, u):
                    sp.wait_ge(s_ev, t + 1)
                    sp.dma_start(edge_rows(d.eh, t), e[:, u, :]).then_inc(s_e[u], 16)

                pipeline(sp, ET, [(0, load), (7, store)])
                drained(sp, s_e, ET)

            @block.vector
            def _(dve):
                def add(t, u):
                    dve.wait_ge(s_ev, t + 1)
                    dve.tensor_tensor(z[:, u % 4, :], e[:, u, :], pso[:, u % 2, F:2 * F], ALU.add).then_inc(s_z, 1)

                def cap(t, u):
                    dve.wait_ge(s_z, t + 1)
                    dve.tensor_scalar(zc[:, u % 4, :], z[:, u % 4, :], 20.0, None, ALU.min).then_inc(s_zc, 1)

                def square(t, u):
                    dve.wait_ge(s_u, t + 1)
                    dve.scalar_tensor_tensor(w[:, u % 4, :], uu[:, u % 4, :], 2.0, uu[:, u % 4, :], ALU.add, ALU.mult).then_inc(s_w, 1)

                def weigh(t, u):
                    dve.tensor_tensor(zw[:, u % 4, :], z[:, u % 4, :], r.attw[:, :, :].rearrange("p h d -> p (h d)"), ALU.mult)\
                       .then_inc(s_zw, 1)

                def invert(t, u):
                    dve.wait_ge(s_w2, t + 1)
                    dve.reciprocal(wi[:, u % 4, :], w2[:, u % 4, :]).then_inc(s_wi, 1)

                def times_w(t, u):
                    dve.wait_ge(s_zw, t + 1)
                    dve.tensor_tensor(zv[:, u % 4, :], zw[:, u % 4, :], w[:, u % 4, :], ALU.mult).then_inc(s_zv, 1)

                def divide(t, u):
                    dve.wait_ge(s_wi, t + 1)
                    dve.wait_ge(s_zv, t + 1)
                    dve.tensor_tensor(wi[:, u % 4, :], zv[:, u % 4, :], wi[:, u % 4, :], ALU.mult).then_inc(s_zz, 1)

                def reduce(t, u):
                    dve.wait_ge(s_zz, t + 1)
                    dve.tensor_reduce(r.logit[:, bass.ds(t, 1), 0:H2].rearrange("p a h -> p (a h)"),
                                      wi[:, u % 4, :].rearrange("p (h d) -> p h d", d=D2), AX_X, ALU.add).then_inc(s_l, 1)

                pipeline(dve, ET, [
                    (0, lambda t, u: src.stage(dve, t, u, s_gs)), (0, lambda t, u: dst.stage(dve, t, u, s_gd)),
                    (5, add), (6, square), (7, invert), (5, cap), (6, weigh), (7, times_w), (8, reduce), (7, divide)])

            @block.scalar
            def _(act):
                def turned(t, u):
                    act.wait_ge(s_tr, t + 1)
                    reached(act, s_mm, t - 1)
                    act.activation(xt[:, u % 2, :], pst[:, u % 2, 0:3 * F], ACT.Copy).then_inc(s_xt, 1)

                def keep(t, u):
                    act.wait_ge(s_mm, t + 1)
                    reached(act, s_e[u], nth(t, u) - 16)
                    reached(act, s_z, t - RING + 1)
                    act.activation(e[:, u, :], pso[:, u % 2, 0:F], ACT.Copy).then_inc(s_ev, 1)

                def exp(t, u):
                    act.wait_ge(s_zc, t + 1)
                    reached(act, s_w, t - 3)
                    act.activation(uu[:, u % 4, :], zc[:, u % 4, :], ACT.Exp).then_inc(s_u, 1)

                def plus_two(t, u):
                    act.wait_ge(s_w, t + 1)
                    reached(act, s_wi, t - 3)
                    act.activation(w2[:, u % 4, :], w[:, u % 4, :], ACT.Copy, bias=2.0).then_inc(s_w2, 1)

                pipeline(act, ET, [(1, keep), (2, exp), (0, turned), (3, plus_two)])

            @block.tensor
            def _(pe):
                def turn(t, u):
                    reached(pe, s_xt, t - 1)
                    for n, (rows, sem) in enumerate(((ea, s_ea), (gs, s_gs), (gd, s_gd))):
                        pe.wait_ge(sem[u], nth(t, u))
                        ins = pe.transpose(pst[:, u % 2, n * F:(n + 1) * F], rows[:, u, :], r.ident[:, :])
                    ins.then_inc(s_tr, 1)

                def product(t, u):
                    pe.wait_ge(s_xt, t + 1)
                    reached(pe, s_ev, t - 1)
                    reached(pe, s_z, t - 1)
                    x = lambda n: xt[:, u % 2, n * F:(n + 1) * F]
                    pe.matmul(pso[:, u % 2, 0:2 * F], r.ones[0:1, :], r.b2[:, :], start=True, stop=False)
                    pe.matmul(pso[:, u % 2, 0:F], x(0), r.we[:, :], start=False, stop=False)
                    pe.matmul(pso[:, u % 2, 0:F], x(1), r.ws[:, :], start=False, stop=False)
                    pe.matmul(pso[:, u % 2, F:2 * F], x(2), r.wr[:, :], start=False, stop=True).then_inc(s_mm, 1)

                pipeline(pe, ET, [(1, product), (0, turn)])


def edge_pass_0b(nc, d, r):
    with Pass(nc, "e0b") as k:
        hs = k.sb("hs", [P, RING, F])
        hd = k.sb("hd", [P, RING, T0W])
        own = k.sb("own", [P, 4, F])
        m = k.sb("m", [P, 4, 2, F])
        mw = k.sb("mw", [P, 4, F])
        rden = k.sb("rden", [P, 2, F])
        agg = k.sb("agg", [P, 2, F])
        y = k.sb("y", [P, 4, 2, F])
        o = k.sb("o", [P, RING, T1W])
        seg = SegmentSum(k, r, 2)
        nb, nn = Norm(k, "b"), Norm(k, "c")
        last = Indices(k, "last", r.last)
        px = k.ps("px", [P, 2, 512])
        s_hs, s_hd, s_w, s_st = k.ring("hs"), k.ring("hd"), k.ring("w"), k.ring("st")
        names = ("own", "m", "m2", "mw", "rden", "agg", "mm", "y", "yx", "x1", "h1")
        s_own, s_m, s_m2, s_mw, s_rden, s_agg, s_mm, s_y, s_yx, s_x1, s_h1 = (k.sem(x) for x in names)
        heads = lambda v: v.rearrange("p (h d) -> p h d", d=D0)
        wide = lambda v: v.rearrange("p a h -> p (a h)").unsqueeze(2).to_broadcast([P, H0, D0])
        with nc.Block() as block:
            @block.sync
            def _(sp):
                def load(t, u):
                    reached(sp, s_m, t - RING + 1)
                    sp.dma_start(hs[:, u, :], edge_rows(d.eh, t)).then_inc(s_hs[u], 16)
                    reached(sp, s_yx, t - RING + 1)
                    sp.dma_start(hd[:, u, :], edge_rows(d.ed, t)).then_inc(s_hd[u], 16)

                def store(t, u):
                    sp.wait_ge(s_h1, t + 1)
                    sp.dma_start(edge_rows(d.e1, t), o[:, u, :]).then_inc(s_st[u], 16)

                pipeline(sp, ET, [(0, load), (7, store)])
                drained(sp, s_st, ET)

            @block.gpsimd
            def _(pool):
                def own_row(t, u):
                    pool.wait_ge(s_hd[u], nth(t, u))
                    reached(pool, s_m2, t - 3)
                    pool.tensor_tensor(heads(own[:, u % 4, :]), heads(hd[:, u, 0:F]), wide(r.self_logit[:, bass.ds(t, 1), :]),
                                       ALU.mult).then_inc(s_own, 1)

                def add_x(t, u):
                    pool.wait_ge(s_y, t + 1)
                    pool.tensor_tensor(y[:, u % 4, 1, :], y[:, u % 4, 0, :], hd[:, u, F + ATT:], ALU.add).then_inc(s_yx, 1)

                def scatter(t, u):
                    pool.wait_ge(s_h1, t + 1)
                    last.scatter(pool, d.t1, o[:, u, :], t, u, s_w)

                pipeline(pool, ET, [(0, own_row), (4, add_x), (7, scatter)])
                drained(pool, s_w, ET)

            @block.vector
            def _(dve):
                seg.clear(dve)

                def weigh(t, u):
                    dve.wait_ge(s_hs[u], nth(t, u))
                    reached(dve, s_m2, t - 3)
                    dve.tensor_tensor(heads(m[:, u % 4, 0, :]), heads(hs[:, u, :]), wide(r.logit[:, bass.ds(t, 1), :]),
                                      ALU.mult).then_inc(s_m, 1)

                def add_own(t, u):
                    dve.wait_ge(s_m, t + 1)
                    dve.wait_ge(s_own, t + 1)
                    reached(dve, seg.s_sum, t - 3)
                    dve.tensor_tensor(m[:, u % 4, 1, :], m[:, u % 4, 0, :], own[:, u % 4, :], ALU.add).then_inc(s_m2, 1)

                def invert(t, u):
                    dve.wait_ge(seg.s_st, t + 2)
                    reached(dve, s_agg, t - 1)
                    dve.reciprocal(rden[:, u % 2, :], seg.st[:, u % 4, 1, :]).then_inc(s_rden, 1)

                def divide(t, u):
                    dve.wait_ge(s_rden, t + 1)
                    reached(dve, s_mm, t - 1)
                    dve.tensor_tensor(agg[:, u % 2, :], seg.st[:, u % 4, 0, :], rden[:, u % 2, :], ALU.mult).then_inc(s_agg, 1)

                def stats_b(t, u):
                    dve.wait_ge(s_mm, t + 1)
                    nb.stats(dve, lambda n: px[:, u % 2, 0:F], t, u)

                def affine(t, u):
                    dve.wait_ge(nb.s_rs, t + 1)
                    reached(dve, s_yx, t - 3)
                    dve.scalar_tensor_tensor(y[:, u % 4, 0, :], px[:, u % 2, 0:F], nb.rs[:, u % 4, 0:1], r.gamma[:, :],
                                             ALU.mult, ALU.mult).then_inc(s_y, 1)

                def add_beta(t, u):
                    dve.wait_ge(s_yx, t + 1)
                    reached(dve, s_w[u], nth(t, u) - 16)
                    reached(dve, s_st[u], nth(t, u) - 16)
                    dve.tensor_tensor(o[:, u, 0:F], y[:, u % 4, 1, :], r.beta[:, :], ALU.add).then_inc(s_x1, 1)

                def stats_c(t, u):
                    dve.wait_ge(s_x1, t + 1)
                    nn.stats(dve, lambda n: o[:, u, 0:F], t, u)

                on = lambda step: lambda t, u: step(dve, t, u)
                pipeline(dve, ET, [
                    (0, weigh), (3, on(nb.inverse)), (2, lambda t, u: seg.follow(dve, s_agg, t, u)), (6, on(nn.inverse)),
                    (0, add_own), (3, affine), (2, invert), (6, on(nn.shift)), (5, add_beta), (2, divide),
                    (4, lambda t, u: last.stage(dve, t, u, s_w)), (5, stats_c), (2, stats_b), (5, on(nn.aggregate)),
                    (2, on(nb.aggregate))])

            @block.scalar
            def _(act):
                def wide_weights(t, u):
                    reached(act, seg.s_sum, t - 3)
                    act.sem_inc(seg.s_turn, 1)
                    act.activation(heads(mw[:, u % 4, :]), wide(r.both[:, bass.ds(t, 1), :]), ACT.Copy).then_inc(s_mw, 1)

                def relu(t, u):
                    nn.relu(act, lambda n: o[:, u, F:], lambda n: o[:, u, 0:F], t, u).then_inc(s_h1, 1)

                pipeline(act, ET, [(3, lambda t, u: nb.root(act, r, t, u)), (6, lambda t, u: nn.root(act, r, t, u)),
                                   (0, lambda t, u: seg.widen(act, t, u)), (0, wide_weights), (6, relu)])

            @block.tensor
            def _(pe):
                def sums(t, u):
                    pe.wait_ge(s_m2, t + 1)
                    pe.wait_ge(s_mw, t + 1)
                    seg.sum(pe, (m[:, u % 4, 1, :], mw[:, u % 4, :]), t, u)

                def project(t, u):
                    pe.wait_ge(s_agg, t + 1)
                    reached(pe, s_y, t - 1)
                    pe.matmul(px[:, u % 2, 0:F], agg[:, u % 2, :], r.projc[:, :], start=True, stop=False)
                    pe.matmul(px[:, u % 2, 0:F], r.ones3[:, :], r.bias3[:, C0:C0 + F], start=False, stop=True).then_inc(s_mm, 1)

                pipeline(pe, ET, [(0, sums), (2, project)])


def edge_pass_1(nc, d, r):
    with Pass(nc, "e1") as k:
        g = k.sb("g", [P, RING, T1W])
        t1 = k.sb("t1", [P, RING, T1W])
        ht = k.sb("ht", [P, 4, F])
        dg = k.sb("dg", [P, 4])
        q = k.sb("q", [P, 4, F])
        o = k.sb("o", [P, RING, T1W])
        seg = SegmentSum(k, r, 2)
        nn = Norm(k, "c")
        src, last = Indices(k, "src", r.src), Indices(k, "last", r.last)
        pt = k.ps("pt", [P, 2, 512])
        po = k.ps("po", [P, 2, 512])
        s_g, s_t1, s_w, s_st = k.ring("g"), k.ring("t1_"), k.ring("w"), k.ring("st")
        s_tr, s_ht, s_mm, s_dg, s_q, s_x2, s_h2 = (k.sem(x) for x in ("tr", "ht", "mm", "dg", "q", "x2", "h2"))
        with nc.Block() as block:
            @block.sync
            def _(sp):
                def load(t, u):
                    reached(sp, s_tr, t - RING + 1)
                    reached(sp, s_q, t - RING + 1)
                    sp.dma_start(t1[:, u, :], edge_rows(d.e1, t)).then_inc(s_t1[u], 16)

                def store(t, u):
                    sp.wait_ge(s_h2, t + 1)
                    sp.dma_start(edge_rows(d.e2, t), o[:, u, :]).then_inc(s_st[u], 16)

                pipeline(sp, ET, [(0, load), (7, store)])
                drained(sp, s_st, ET)

            @block.gpsimd
            def _(pool):
                def gather(t, u):
                    reached(pool, seg.s_sum, t - RING + 1)
                    src.gather(pool, g[:, u, :], d.t1, t, u, s_g)

                def scatter(t, u):
                    pool.wait_ge(s_h2, t + 1)
                    last.scatter(pool, d.h2, o[:, u, F:], t, u, s_w)

                pipeline(pool, ET, [(0, gather), (7, scatter)])
                drained(pool, s_w, ET)

            @block.vector
            def _(dve):
                seg.clear(dve)

                def degree(t, u):
                    dve.wait_ge(s_mm, t + 1)
                    reached(dve, s_q, t - 3)
                    dve.tensor_copy(dg[:, u % 4:u % 4 + 1], po[:, u % 2, 3 * F:3 * F + 1]).then_inc(s_dg, 1)

                def weigh(t, u):
                    dve.wait_ge(s_dg, t + 1)
                    dve.scalar_tensor_tensor(q[:, u % 4, :], po[:, u % 2, F:2 * F], dg[:, u % 4:u % 4 + 1], t1[:, u, 0:F],
                                             ALU.mult, ALU.add)
                    dve.reciprocal(r.rdeg[:, bass.ds(t, 1)], dg[:, u % 4:u % 4 + 1]).then_inc(s_q, 1)

                def add(t, u):
                    dve.wait_ge(s_q, t + 1)
                    reached(dve, s_w[u], nth(t, u) - 16)
                    reached(dve, s_st[u], nth(t, u) - 16)
                    dve.tensor_tensor(o[:, u, 0:F], q[:, u % 4, :], po[:, u % 2, 0:F], ALU.add).then_inc(s_x2, 1)

                def stats(t, u):
                    dve.wait_ge(s_x2, t + 1)
                    nn.stats(dve, lambda n: o[:, u, 0:F], t, u)

                on = lambda step: lambda t, u: step(dve, t, u)
                pipeline(dve, ET, [
                    (0, lambda t, u: src.stage(dve, t, u, s_g)), (4, degree), (3, lambda t, u: seg.follow(dve, s_mm, t, u)),
                    (5, on(nn.inverse)), (4, weigh), (4, lambda t, u: last.stage(dve, t, u, s_w)), (5, on(nn.shift)),
                    (4, add), (4, stats), (4, on(nn.aggregate))])

            @block.scalar
            def _(act):
                def turned(t, u):
                    act.wait_ge(s_tr, t + 1)
                    reached(act, s_mm, t - 3)
                    act.activation(ht[:, u % 4, :], pt[:, u % 2, 0:F], ACT.Copy).then_inc(s_ht, 1)

                def relu(t, u):
                    nn.relu(act, lambda n: o[:, u, F:], lambda n: o[:, u, 0:F], t, u).then_inc(s_h2, 1)

                pipeline(act, ET, [(4, lambda t, u: nn.root(act, r, t, u)), (0, lambda t, u: seg.widen(act, t, u)), (0, turned),
                                   (4, relu)])

            @block.tensor
            def _(pe):
                def turn(t, u):
                    pe.wait_ge(s_t1[u], nth(t, u))
                    reached(pe, s_ht, t - 1)
                    pe.transpose(pt[:, u % 2, 0:F], t1[:, u, F:], r.ident[:, :]).then_inc(s_tr, 1)

                def sums(t, u):
                    pe.wait_ge(s_g[u], nth(t, u))
                    seg.sum(pe, (g[:, u, F:], r.ones[:, :]), t, u)

                def product(t, u):
                    pe.wait_ge(s_ht, t + 1)
                    pe.wait_ge(seg.s_st, t + 2)
                    reached(pe, s_x2, t - 1)
                    pe.matmul(po[:, u % 2, 0:2 * F], ht[:, u % 4, :], r.wu[:, :], start=True, stop=False)
                    pe.matmul(po[:, u % 2, 0:2 * F], r.ones3[:, :], r.bias3[:, B1:B2], start=False, stop=False)
                    pe.matmul(po[:, u % 2, 0:F], seg.st[:, u % 4, 0, :], r.wa[:, :], start=False, stop=True)
                    pe.matmul(po[:, u % 2, 3 * F:3 * F + 1], seg.st[0:1, u % 4, 1, :], r.ones[0:1, 0:1], start=True, stop=True)\
                      .then_inc(s_mm, 1)

                pipeline(pe, ET, [(0, turn), (0, sums), (1, product)])


def edge_pass_2b(nc, d, r):
    with Pass(nc, "e2b") as k:
        e = k.sb("e", [P, RING, F])
        x2 = k.sb("x2", [P, RING, T1W])
        m = k.sb("m", [P, 4, F])
        mw = k.sb("mw", [P, 4, F])
        rden = k.sb("rden", [P, 2, F])
        agg = k.sb("agg", [P, 2, F])
        o = k.sb("o", [P, RING, T1W])
        seg = SegmentSum(k, r, 2)
        nn = Norm(k, "c")
        last = Indices(k, "last", r.last)
        px = k.ps("px", [P, 2, 512])
        s_e, s_x2, s_w, s_st = k.ring("e"), k.ring("x2_"), k.ring("w"), k.ring("st")
        s_m, s_mw, s_rden, s_agg, s_tr, s_x3, s_h3 = (k.sem(x) for x in ("m", "mw", "rden", "agg", "tr", "x3", "h3"))
        heads = lambda v: v.rearrange("p (h d) -> p h d", d=D2)
        wide = lambda t: r.logit[:, bass.ds(t, 1), 0:H2].rearrange("p a h -> p (a h)").unsqueeze(2).to_broadcast([P, H2, D2])
        with nc.Block() as block:
            @block.sync
            def _(sp):
                def load(t, u):
                    reached(sp, s_m, t - RING + 1)
                    sp.dma_start(e[:, u, :], edge_rows(d.eh, t)).then_inc(s_e[u], 16)
                    reached(sp, s_x3, t - RING + 1)
                    sp.dma_start(x2[:, u, :], edge_rows(d.e2, t)).then_inc(s_x2[u], 16)

                def store(t, u):
                    sp.wait_ge(s_h3, t + 1)
                    sp.dma_start(edge_rows(d.e3, t), o[:, u, :]).then_inc(s_st[u], 16)

                pipeline(sp, ET, [(0, load), (7, store)])
                drained(sp, s_st, ET)

            @block.gpsimd
            def _(pool):
                def scatter(t, u):
                    pool.wait_ge(s_h3, t + 1)
                    last.scatter(pool, d.h2, o[:, u, F:], t, u, s_w)

                pipeline(pool, ET, [(0, scatter)])
                drained(pool, s_w, ET)

            @block.vector
            def _(dve):
                seg.clear(dve)

                def weigh(t, u):
                    dve.wait_ge(s_e[u], nth(t, u))
                    reached(dve, seg.s_sum, t - 3)
                    dve.tensor_tensor(heads(m[:, u % 4, :]), heads(e[:, u, :]), wide(t), ALU.mult).then_inc(s_m, 1)

                def invert(t, u):
                    dve.wait_ge(seg.s_st, t + 2)
                    reached(dve, s_agg, t - 1)
                    dve.reciprocal(rden[:, u % 2, :], seg.st[:, u % 4, 1, :]).then_inc(s_rden, 1)

                def divide(t, u):
                    dve.wait_ge(s_rden, t + 1)
                    reached(dve, s_tr, t - 1)
                    dve.tensor_tensor(agg[:, u % 2, :], seg.st[:, u % 4, 0, :], rden[:, u % 2, :], ALU.mult).then_inc(s_agg, 1)

                def add(t, u):
                    dve.wait_ge(s_tr, t + 1)
                    dve.wait_ge(s_x2[u], nth(t, u))
                    reached(dve, s_w[u], nth(t, u) - 16)
                    reached(dve, s_st[u], nth(t, u) - 16)
                    dve.tensor_tensor(o[:, u, 0:F], x2[:, u, 0:F], px[:, u % 2, 0:F], ALU.add).then_inc(s_x3, 1)

                def stats(t, u):
                    dve.wait_ge(s_x3, t + 1)
                    nn.stats(dve, lambda n: o[:, u, 0:F], t, u)

                on = lambda step: lambda t, u: step(dve, t, u)
                pipeline(dve, ET, [
                    (0, weigh), (4, on(nn.inverse)), (2, lambda t, u: seg.follow(dve, s_agg, t, u)), (3, add),
                    (3, lambda t, u: last.stage(dve, t, u, s_w)), (2, invert), (4, on(nn.shift)), (3, stats), (2, divide),
                    (3, on(nn.aggregate))])

            @block.scalar
            def _(act):
                def wide_weights(t, u):
                    reached(act, seg.s_sum, t - 3)
                    act.sem_inc(seg.s_turn, 1)
                    act.activation(heads(mw[:, u % 4, :]), wide(t), ACT.Copy).then_inc(s_mw, 1)

                def relu(t, u):
                    nn.relu(act, lambda n: o[:, u, F:], lambda n: o[:, u, 0:F], t, u).then_inc(s_h3, 1)

                pipeline(act, ET, [(4, lambda t, u: nn.root(act, r, t, u)), (0, lambda t, u: seg.widen(act, t, u)),
                                   (0, wide_weights), (4, relu)])

            @block.tensor
            def _(pe):
                def sums(t, u):
                    pe.wait_ge(s_m, t + 1)
                    pe.wait_ge(s_mw, t + 1)
                    seg.sum(pe, (m[:, u % 4, :], mw[:, u % 4, :]), t, u)

                def turn(t, u):
                    pe.wait_ge(s_agg, t + 1)
                    reached(pe, s_x3, t - 1)
                    pe.transpose(px[:, u % 2, 0:F], agg[:, u % 2, :], r.ident[:, :]).then_inc(s_tr, 1)

                pipeline(pe, ET, [(0, sums), (2, turn)])


def edge_conv(nc, d, r, name, gather, own, wn, bias, out, own_at=0, out_own=None, score=False, masked=False, add=None):
    cols = F + 1 if score else F
    relu = not score and add is None
    with Pass(nc, name) as k:
        gw, ow = gather.shape[1], own.shape[1]
        ga = k.sb("ga", [P, RING, 2, max(gw, ow)])
        x3 = k.sb("x3", [P, RING, F]) if add is not None else None
        km = k.sb("km", [P, 4, 2, 2]) if masked else None
        m = k.sb("m", [P, 4, 2, F]) if masked else None
        ht = k.sb("ht", [P, 4, F])
        q = k.sb("q", [P, 4, 2, cols])
        y = k.sb("y", [P, 4, F]) if not score else None
        ex = k.sb("ex", [P, 4, 2]) if score else None
        o = k.sb("o", [P, RING, out.shape[1]])
        seg = SegmentSum(k, r)
        src, last = Indices(k, "src", r.src), Indices(k, "last", r.last)
        pt = k.ps("pt", [P, 2, 512])
        po = k.ps("po", [P, 2, 512])
        s_g, s_a, s_x3, s_w, s_st = k.ring("g"), k.ring("a"), k.ring("x3_"), k.ring("w"), k.ring("st")
        names = ("pre", "k0", "k1", "m", "tr", "ht", "mm", "q", "y", "o", "ex", "e1", "out")
        s_pre, s_k0, s_k1, s_m, s_tr, s_ht, s_mm, s_q, s_y, s_o, s_ex, s_e1, s_out = (k.sem(x) for x in names)
        with nc.Block() as block:
            @block.sync
            def _(sp):
                def load(t, u):
                    reached(sp, s_m if masked else s_tr, t - RING + 1)
                    sp.dma_start(ga[:, u, 1, 0:ow], edge_rows(own, t)).then_inc(s_a[u], 16)
                    if add is not None:
                        reached(sp, s_out, t - RING + 1)
                        sp.dma_start(x3[:, u, :], edge_rows(add, t)[:, 0:F]).then_inc(s_x3[u], 16)

                def store(t, u):
                    sp.wait_ge(s_out, t + 1)
                    sp.dma_start(edge_rows(out_own, t), o[:, u, :]).then_inc(s_st[u], 16)

                pipeline(sp, ET, [(0, load)] + ([(7, store)] if out_own is not None else []))
                if out_own is not None:
                    drained(sp, s_st, ET)

            @block.gpsimd
            def _(pool):
                def fetch(t, u):
                    reached(pool, s_m if masked else seg.s_sum, t - RING + 1)
                    src.gather(pool, ga[:, u, 0, 0:gw], gather, t, u, s_g)

                def scatter(t, u):
                    pool.wait_ge(s_out, t + 1)
                    last.scatter(pool, out, o[:, u, :], t, u, s_w)

                pipeline(pool, ET, [(0, fetch), (7, scatter)])
                drained(pool, s_w, ET)

            @block.vector
            def _(dve):
                seg.clear(dve)
                if score:
                    dve.memset(o[:, :, F:], 0.0).then_inc(s_pre, 1)
                    dve.wait_ge(s_pre, 1)

                def mask(t, u):
                    dve.wait_ge(s_g[u], nth(t, u))
                    dve.wait_ge(s_a[u], nth(t, u))
                    dve.scalar_tensor_tensor(km[:, u % 4, 0, :].unsqueeze(1), ga[:, u, :, F].unsqueeze(1), r.thr[:, 0:1],
                                             r.below[:, bass.ds(t, 1), :], ALU.is_equal, ALU.mult).then_inc(s_k0, 1)

                def mask_too(t, u):
                    dve.wait_ge(s_k0, t + 1)
                    dve.scalar_tensor_tensor(km[:, u % 4, 1, :], ga[:, u, :, F], r.thr[:, 0:1], km[:, u % 4, 0, :],
                                             ALU.is_gt, ALU.add).then_inc(s_k1, 1)

                def kept(t, u):
                    dve.wait_ge(s_k1, t + 1)
                    reached(dve, seg.s_sum, t - 3)
                    reached(dve, s_tr, t - 3)
                    for n in range(2):
                        ins = dve.tensor_scalar(m[:, u % 4, n, :], ga[:, u, n, 0:F], km[:, u % 4, 1, n:n + 1], None, ALU.mult)
                    ins.then_inc(s_m, 1)

                def weigh(t, u):
                    dve.wait_ge(s_mm, t + 1)
                    dve.tensor_scalar(q[:, u % 4, 0, :], po[:, u % 2, 256:256 + cols], r.rdeg[:, bass.ds(t, 1)], None, ALU.mult)\
                       .then_inc(s_q, 1)

                def combine(t, u):
                    dve.wait_ge(s_q, t + 1)
                    if score:
                        reached(dve, s_w[u], nth(t, u) - 16)
                        reached(dve, s_st[u], nth(t, u) - 16)
                    else:
                        reached(dve, s_out, t - 3)
                    dve.tensor_tensor(o[:, u, 0:cols] if score else y[:, u % 4, :], q[:, u % 4, 0, :], po[:, u % 2, 0:cols],
                                      ALU.add).then_inc(s_y, 1)

                def plus_x3(t, u):
                    dve.wait_ge(s_y, t + 1)
                    dve.wait_ge(s_x3[u], nth(t, u))
                    reached(dve, s_w[u], nth(t, u) - 16)
                    dve.tensor_tensor(o[:, u, :], y[:, u % 4, :], x3[:, u, :], ALU.add).then_inc(s_out, 1)

                def plus_one(t, u):
                    dve.wait_ge(s_ex, t + 1)
                    dve.tensor_scalar(ex[:, u % 4, 1:2], ex[:, u % 4, 0:1], 1.0, None, ALU.add).then_inc(s_e1, 1)

                def sigmoid(t, u):
                    dve.wait_ge(s_e1, t + 1)
                    dve.reciprocal(o[:, u, F:F + 1], ex[:, u % 4, 1:2]).then_inc(s_out, 1)

                pipeline(dve, ET,
                         [(0, lambda t, u: src.stage(dve, t, u, s_g))] + ([(3, mask)] if masked else []) +
                         ([(6, plus_one)] if score else []) + [(5, weigh)] + ([(3, mask_too)] if masked else []) +
                         [(4, lambda t, u: seg.follow(dve, s_mm, t, u))] + ([(3, kept)] if masked else []) +
                         [(5, combine), (5, lambda t, u: last.stage(dve, t, u, s_w))] + ([(6, sigmoid)] if score else []) +
                         ([(6, plus_x3)] if add is not None else []))

            @block.scalar
            def _(act):
                def turned(t, u):
                    act.wait_ge(s_tr, t + 1)
                    reached(act, s_mm, t - 3)
                    act.activation(ht[:, u % 4, :], pt[:, u % 2, 0:F], ACT.Copy).then_inc(s_ht, 1)

                def finish(t, u):
                    act.wait_ge(s_y, t + 1)
                    reached(act, s_w[u], nth(t, u) - 16)
                    reached(act, s_st[u], nth(t, u) - 16)
                    act.activation(o[:, u, :], y[:, u % 4, :], ACT.Relu).then_inc(s_out, 1)

                def exp(t, u):
                    act.wait_ge(s_y, t + 1)
                    reached(act, s_e1, t - 3)
                    act.activation(ex[:, u % 4, 0:1], o[:, u, F:F + 1], ACT.Exp, scale=-1.0).then_inc(s_ex, 1)

                pipeline(act, ET, ([(4, finish)] if relu else []) + ([(4, exp)] if score else []) +
                         [(0, lambda t, u: seg.widen(act, t, u)), (0, turned)])

            @block.tensor
            def _(pe):
                def turn(t, u):
                    if masked:
                        pe.wait_ge(s_m, t + 1)
                    else:
                        pe.wait_ge(s_a[u], nth(t, u))
                    reached(pe, s_ht, t - 1)
                    pe.transpose(pt[:, u % 2, 0:F], m[:, u % 4, 1, :] if masked else ga[:, u, 1, own_at:own_at + F], r.ident[:, :])\
                      .then_inc(s_tr, 1)

                def sums(t, u):
                    if not masked:
                        pe.wait_ge(s_g[u], nth(t, u))
                    seg.sum(pe, (m[:, u % 4, 0, :] if masked else ga[:, u, 0, 0:F],), t, u)

                def product(t, u):
                    pe.wait_ge(s_ht, t + 1)
                    pe.wait_ge(seg.s_st, t + 2)
                    reached(pe, s_y, t - 1)
                    at = B3 + bias * (F + 1)
                    pe.matmul(po[:, u % 2, 0:cols], ht[:, u % 4, :], r.w3[:, wn, 0:cols], start=True, stop=False)
                    pe.matmul(po[:, u % 2, 0:cols], r.ones3[:, :], r.bias3[:, at:at + cols], start=False, stop=True)
                    pe.matmul(po[:, u % 2, 256:256 + cols], seg.st[:, u % 4, 0, :], r.w3[:, wn + 1, 0:cols], start=True, stop=True)\
                      .then_inc(s_mm, 1)

                pipeline(pe, ET, [(0, turn), (0, sums), (1, product)])


def choose(nc, d, r):
    with Pass(nc, "top") as k:
        zf = r.z[:, :, :].rearrange("p g j -> p (g j)")
        n = NGROUPS * J
        ids = k.sb("ids", [P, n], I32)
        idt = k.sb("idt", [P, 1], I32)
        idf = k.sb("idf", [P, n])
        junk = k.sb("junk", [P, n])
        far = k.sb("far", [P, n])
        bit = k.sb("bit", [P, 1], I32)
        cand = k.sb("cand", [P, 1], I32)
        yes = k.sb("yes", [P, 1], I32)
        cnt = k.sb("cnt", [P, 1])
        need = k.sb("need", [P, 1])
        step = k.sb("step", [P, 1])
        bound = k.sb("bound", [P, 1])
        fit = k.sb("fit", [P, 1])
        tot = k.ps("tot", [P, 512])
        thr = r.thr[:, 0:1]
        thr_bits = thr.bitcast(I32)
        s_id, s_cnt, s_tot, s_v = (k.sem(x) for x in ("id", "cnt", "tot", "v"))
        VALUE_BITS, INDEX_BITS = 30, 17
        with nc.Block() as block:
            @block.gpsimd
            def _(pool):
                pool.iota(ids[:, :], pattern=[[GROUP, NGROUPS], [1, J]], base=0, channel_multiplier=J).then_inc(s_id, 1)
                pool.iota(idt[:, :], pattern=[[0, 1]], base=FULL * GROUP, channel_multiplier=1).then_inc(s_id, 1)

            @block.tensor
            def _(pe):
                with pe.Fori(0, VALUE_BITS + 1 + INDEX_BITS) as i:
                    pe.wait_ge(s_cnt, i + 1)
                    pe.matmul(tot[:, 0:1], r.ones[:, :], cnt[:, :], start=True, stop=True).then_inc(s_tot, 1)

            @block.vector
            def _(dve):
                FIRST, EACH, SECOND = 2, 5, 7

                def link(ins, value):
                    ins.then_inc(s_v, 1)
                    dve.wait_ge(s_v, value)

                dve.memset(thr, 0.0)
                link(dve.memset(bit[:, :], 1 << (VALUE_BITS - 1)), 1)
                dve.wait_ge(s_id, 2)
                dve.tensor_copy(idf[:, :], ids[:, :])
                link(dve.tensor_copy(junk[:, 0:1], idt[:, :]), 2)
                with dve.Fori(0, VALUE_BITS) as i:
                    at = FIRST + i * EACH
                    link(dve.tensor_tensor(cand[:, :], thr_bits, bit[:, :], ALU.bitwise_or), at + 1)
                    link(dve.tensor_scalar(junk[:, :], zf, cand[:, :].bitcast(F32), 0.0, ALU.is_ge, ALU.add,
                                           accum_out=cnt[:, :]), at + 2)
                    dve.sem_inc(s_cnt, 1)
                    dve.wait_ge(s_tot, i + 1)
                    link(dve.tensor_scalar(yes[:, :], tot[:, 0:1], float(KEEP), -1.0, ALU.is_ge, ALU.mult), at + 3)
                    link(dve.tensor_tensor(yes[:, :], yes[:, :], bit[:, :], ALU.bitwise_and), at + 4)
                    dve.tensor_tensor(thr_bits, thr_bits, yes[:, :], ALU.bitwise_or)
                    link(dve.tensor_scalar(bit[:, :], bit[:, :], 1, None, ALU.logical_shift_right), at + 5)
                at = FIRST + VALUE_BITS * EACH
                link(dve.tensor_scalar(junk[:, :], zf, thr, 0.0, ALU.is_gt, ALU.add, accum_out=cnt[:, :]), at + 1)
                dve.sem_inc(s_cnt, 1)
                dve.wait_ge(s_tot, VALUE_BITS + 1)
                dve.tensor_scalar(need[:, :], tot[:, 0:1], -1.0, float(KEEP), ALU.mult, ALU.add)
                dve.memset(bound[:, :], 0.0)
                dve.memset(step[:, :], float(1 << (INDEX_BITS - 1)))
                link(dve.tensor_scalar(far[:, :], zf, thr, float(1 << 20), ALU.not_equal, ALU.mult), at + 2)
                link(dve.tensor_copy(idf[0:REST, FULL * J:FULL * J + 1], idt[0:REST, :]), at + 3)
                link(dve.tensor_tensor(far[:, :], far[:, :], idf[:, :], ALU.add), at + 4)
                at += 4
                with dve.Fori(0, INDEX_BITS) as i:
                    v = at + i * SECOND
                    link(dve.tensor_tensor(cand[:, :].bitcast(F32), bound[:, :], step[:, :], ALU.add), v + 1)
                    link(dve.tensor_scalar(junk[:, :], far[:, :], cand[:, :].bitcast(F32), 0.0, ALU.is_lt, ALU.add,
                                           accum_out=cnt[:, :]), v + 2)
                    dve.sem_inc(s_cnt, 1)
                    dve.wait_ge(s_tot, i + (VALUE_BITS + 2))
                    link(dve.tensor_tensor(fit[:, :], tot[:, 0:1], need[:, :], ALU.is_le), v + 3)
                    link(dve.tensor_tensor(fit[:, :], fit[:, :], step[:, :], ALU.mult), v + 4)
                    link(dve.tensor_tensor(bound[:, :], bound[:, :], fit[:, :], ALU.add), v + 5)
                    link(dve.tensor_scalar(step[:, :], step[:, :], 0.5, None, ALU.mult), v + 6)
                    link(dve.tensor_copy(fit[:, :], bound[:, :]), v + 7)
                at += INDEX_BITS * SECOND
                link(dve.tensor_scalar(far[:, :], far[:, :], bound[:, :], None, ALU.is_lt), at + 1)
                dve.scalar_tensor_tensor(r.keep[:, :], zf, thr, far[:, :], ALU.is_gt, ALU.add)
                dve.tensor_scalar(r.below[:, :, 0], r.srcf[:, :], bound[:, :], None, ALU.is_lt)
                dve.tensor_scalar(r.below[:, :, 1], r.dstf[:, :], bound[:, :], None, ALU.is_lt)




def main(nc, a, out):
    with ExitStack() as ctx:
        def sb(name, shape, dt=F32):
            return ctx.enter_context(nc.sbuf_tensor(name, shape, dt))
        d, r = Resident(), Resident()
        dram = lambda n, s, dt=F32: nc.dram_tensor(n, s, dt, kind="Internal").ap()
        d.dst = dram("dst_padded", (EPAD + CL + 2,), I32)
        d.hop = dram("chunk_values", (4, H0 * CH))
        d.src = dram("src_padded", (EPAD,), I32)
        d.t0 = dram("table0", (N, T0W))
        d.t1 = dram("table1", (N, T1W))
        d.x3 = dram("x3", (N, F))
        d.h2 = dram("h2", (N, F))
        d.g = dram("g_conv1", (N, F))
        d.hp = dram("h_scored", (N, HPW))
        d.up = dram("up_conv1", (N, F))
        d.parts = dram("bias_parts_list", (3, BIASES), BF16)
        d.e1 = dram("edge_x1_h1", (EPAD, T1W))
        d.e2 = dram("edge_x2_h2", (EPAD, T1W))
        d.e3 = dram("edge_x3_h3", (EPAD, T1W))
        d.eg = dram("edge_g", (EPAD, F))
        d.ehp = dram("edge_scored", (EPAD, HPW))
        d.eup = dram("edge_up", (EPAD, F))
        d.eh = dram("edge_source_rows", (EPAD, F))
        d.ed = dram("edge_target_rows", (EPAD, T0W))
        r.ident = sb("ident", [P, P])
        r.ones = sb("ones", [P, P])
        r.eps = sb("eps", [P, 1])
        r.src = sb("src_index", [P, ET], I32)
        r.dstg = sb("dst_index", [P, ET], I32)
        r.last = sb("last_index", [P, ET], I32)
        r.srcf = sb("src_float", [P, ET])
        r.dstf = sb("dst_float", [P, ET])
        r.first = sb("first", [P, ET])
        r.rdeg = sb("degree_inverse", [P, ET])
        r.seg = sb("segments", [P, ET, P], BF16)
        r.goes_on = sb("goes_on", [P, ET, P], BF16)
        r.projc = sb("projc", [P, F])
        r.w0 = sb("w0", [P, T0W])
        r.bias = sb("bias", [1, BIASES])
        r.bias3 = sb("bias_parts", [3, BIASES], BF16)
        r.ones3 = sb("ones_parts", [3, P], BF16)
        r.c0, r.b1, r.b2 = r.bias[:, C0:B1], r.bias[:, B1:B2], r.bias[:, B2:B3]
        r.b3 = r.bias[:, B3:BIASES].rearrange("a (n f) -> a n f", n=4)
        r.gamma = sb("gamma", [P, F])
        r.beta = sb("beta", [P, F])
        r.wu = sb("wu", [P, 2 * F])
        r.wa = sb("wa", [P, F])
        r.ws = sb("ws", [P, F])
        r.wr = sb("wr", [P, F])
        r.we = sb("we", [P, F])
        r.attw = sb("attw", [P, H2, D2])
        r.attb = sb("attb", [P, 1])
        r.w3 = sb("w3", [P, 8, F + 1])
        r.logit = sb("logit", [P, ET, H0])
        r.self_logit = sb("self_logit", [P, ET, H0])
        r.both = sb("weights_with_own", [P, ET, H0])
        r.z = sb("score", [P, FULL + 1, J])
        r.thr = sb("threshold", [P, 2])
        r.keep = sb("keep", [P, NGROUPS * J])
        r.below = sb("below", [P, ET, 2])
        passes(nc, a, d, r, out)


def passes(nc, a, d, r, out):
    setup(nc, a, d, r)
    node_pass_0(nc, a, d, r)
    node_pass_1(nc, d, r)
    edge_pass_0a(nc, d, r)
    softmax_weights(nc, d, r, "sm0", own_loop=True)
    edge_pass_0b(nc, d, r)
    edge_pass_1(nc, d, r)
    edge_pass_2a(nc, a, d, r)
    softmax_weights(nc, d, r, "sm2", own_loop=False)
    edge_pass_2b(nc, d, r)
    edge_conv(nc, d, r, "e3", gather=d.h2, own=d.e3, own_at=F, wn=0, bias=0, out=d.g, out_own=d.eg)
    edge_conv(nc, d, r, "e4", gather=d.g, own=d.eg, wn=2, bias=1, out=d.hp, out_own=d.ehp, score=True)
    collect(nc, d, r)
    choose(nc, d, r)
    node_pass_2(nc, d, r, out)
    edge_conv(nc, d, r, "e5", gather=d.hp, own=d.ehp, wn=4, bias=2, out=d.up, out_own=d.eup, masked=True)
    edge_conv(nc, d, r, "e6", gather=d.up, own=d.eup, wn=6, bias=3, out=out, add=d.e3)


_OUTS = [((N, F), 'float32')]


def kernel(**inputs):
    import numpy as _np
    import concourse.bacc as _bacc
    from concourse import mybir as _mybir
    from concourse.bass_utils import run_bass_kernel_spmd as _run

    nc = _bacc.Bacc("TRN2", target_bir_lowering=False, num_devices=1)
    arrays, args = {}, {}
    for name, value in inputs.items():
        v = _np.ascontiguousarray(value)
        arrays[f"in_{name}"] = v
        args[name] = nc.dram_tensor(f"in_{name}", v.shape, _mybir.dt.from_np(v.dtype), kind="ExternalInput").ap()
    out = nc.dram_tensor("out_x", (N, F), _mybir.dt.float32, kind="ExternalOutput").ap()
    main(nc, args, out)
    got = _run(nc, [arrays], core_ids=[0])
    return got.results[0]["out_x"]
```

```python
from contextlib import ExitStack

import concourse.bass as bass
from concourse import mybir

ALU = mybir.AluOpType
ACT = mybir.ActivationFunctionType
AX_X = mybir.AxisListType.X
F32 = mybir.dt.float32
I32 = mybir.dt.int32
BF16 = mybir.dt.bfloat16

P = 128
F = 128
N = 50000
E = 25000
J = 3
GROUP = P * J
FULL = N // GROUP
REST = N - FULL * GROUP
NGROUPS = FULL + 1
ET = -(-E // P)
EPAD = ET * P
EREST = E - (ET - 1) * P
H0, D0 = 8, 16
H2, D2 = 4, 32
LN_EPS = 1e-5
BIG = 1e38
SKIP = 100000
RING = 8
UNROLL = 8
CH = 14
CT = ET // CH
CL = CT * P
LOADS = 40
KEEP = N // 4
ATT = 2 * H0
T0W = F + ATT + F
T1W = 2 * F
HPW = F + 4
C0, B1, B2, B3 = 0, F, 3 * F, 5 * F
BIASES = B3 + 4 * (F + 1)
PAIR = 2
assert N // (P * PAIR) + 1 == ET and N % (P * PAIR) == REST
assert CH * CT == ET and 0 < REST <= P and REST % 16 == 0


def pipeline(eng, total, stages):
    lags = max(lag for lag, _ in stages)
    head = UNROLL * (1 + -(-lags // UNROLL))
    loops = total // UNROLL

    def step(s, u):
        for lag, stage in stages:
            if not isinstance(s, int) or 0 <= s - lag < total:
                stage(s - lag, (u - lag) % RING)

    for s in range(head):
        step(s, s % RING)
    with eng.Fori(head // UNROLL, loops) as i:
        for u in range(UNROLL):
            step(i * UNROLL + u, u)
    for s in range(loops * UNROLL, total + lags):
        step(s, s % RING)


def reached(eng, sem, value):
    if not isinstance(value, int) or value > 0:
        eng.wait_ge(sem, value)


def nth(s, u):
    return (s - u) * (16 // RING) + 16


def sent(eng, sems, s, u, depth):
    v = (u - depth) % RING
    reached(eng, sems[v], nth(s - depth, v))


def span(g, tiles=J):
    return (REST, 1) if isinstance(g, int) and g == N // (P * tiles) else (P, tiles)


def node_rows(table, g, tiles=J):
    p, j = span(g, tiles)
    if p == REST:
        return table[FULL * GROUP:N, :].unsqueeze(1)
    return table[bass.ds(g * (P * tiles), P * tiles), :].rearrange("(p j) f -> p j f", j=j)


def edge_rows(table, t, n=P):
    return table[bass.ds(t * P, n), :]


class Pass:

    def __init__(self, nc, name):
        self.nc, self.name, self.sems = nc, name, []
        self.ctx = ExitStack()

    def sb(self, name, shape, dt=F32):
        return self.ctx.enter_context(self.nc.sbuf_tensor(f"{self.name}_{name}", shape, dt))

    def ps(self, name, shape, dt=F32):
        return self.ctx.enter_context(self.nc.psum_tensor(f"{self.name}_{name}", shape, dt))

    def sem(self, name):
        self.sems.append(self.nc.alloc_semaphore(f"{self.name}_{name}"))
        return self.sems[-1]

    def ring(self, name):
        return [self.sem(f"{name}{i}") for i in range(RING)]

    def __enter__(self):
        return self

    def __exit__(self, *error):
        self.ctx.close()
        if error[0] is None:
            self.nc.clear_and_free_semaphores(self.sems)
            self.nc.all_engine_barrier()


class Resident:
    pass


def setup(nc, a, d, r):
    with Pass(nc, "setup") as k:
        pads = k.sb("pads", [1, 96], I32)
        zi = k.sb("zi", [1, 96], I32)
        half = ET // 2
        li = k.sb("li", [half, 3, 2 * P], I32)
        lf = k.sb("lf", [half, 3, 2 * P])
        res = k.sb("res", [1, 2, BIASES])
        part = k.sb("part", [1, 3, BIASES], BF16)
        wl = k.sb("wl", [P, 7, F])
        col = k.sb("col", [P, 8])
        rows = k.sb("rows", [1, 12, F])
        tr = k.sb("tr", [P, 5, F])
        blk = k.sb("blk", [P, H0])
        mask = k.sb("mask", [P, H0])
        bs = k.sb("bs", [P, ATT])
        mean = k.sb("mean", [P, 2])
        nxt = k.sb("nxt", [P, ET])
        same = k.sb("same", [P, ET])
        ps = k.ps("ps", [P, 8, 512])
        s_pad, s_put, s_w, s_list, s_ends, s_part = (k.sem(n) for n in ("pad", "put", "w", "list", "ends", "part"))
        s_iota, s_eye, s_v, s_pe, s_act, s_li = (k.sem(n) for n in ("iota", "eye", "v", "pe", "act", "li"))
        with nc.Block() as block:
            @block.sync
            def _(sp):
                n = 0

                def load(dst, src):
                    nonlocal n
                    sp.dma_start(dst, src).then_inc(s_w, 16)
                    n += 1

                row = lambda v: v.rearrange("(a n) -> a n", a=1)
                column = lambda v: v.rearrange("(n a) -> n a", a=1)
                load(wl[:, 0, :], a["L0_gnn_proj_w"][:, :])
                load(wl[:, 1, :], a["L1_gnn_W_msg"][0:F, :])
                load(wl[:, 2, :], a["L1_gnn_W_msg"][F:2 * F, :])
                load(wl[:, 5, :], a["L0_gnn_lin_w"][:, :])
                load(wl[:, 6, :], a["L1_gnn_W_upd"][F:2 * F, :])
                load(r.wu[:, 0:F], a["L1_gnn_W_upd"][0:F, :])
                load(r.ws[:, :], a["L2_gnn_Ws_k"].rearrange("f h d -> f (h d)"))
                load(r.wr[:, :], a["L2_gnn_Wr_k"].rearrange("f h d -> f (h d)"))
                load(r.we[:, :], a["L2_gnn_We_k"].rearrange("f h d -> f (h d)"))
                load(r.w3[:, 0, 0:F], a["L3_gnn_ws1"][:, :])
                load(r.w3[:, 1, 0:F], a["L3_gnn_wn1"][:, :])
                load(r.w3[:, 2, 0:F], a["L3_gnn_ws2"][:, :])
                load(r.w3[:, 3, 0:F], a["L3_gnn_wn2"][:, :])
                load(r.w3[:, 4, 0:F], a["L3_gnn_wu1"][:, :])
                load(r.w3[:, 5, 0:F], a["L3_gnn_wnu1"][:, :])
                load(r.w3[:, 6, 0:F], a["L3_gnn_wu2"][:, :])
                load(r.w3[:, 7, 0:F], a["L3_gnn_wnu2"][:, :])
                load(col[:, 0:1], column(a["L0_gnn_gat_bias"]))
                load(col[:, 1:2], column(a["L1_gnn_b_msg"]))
                load(col[:, 2:3], column(a["L3_gnn_b2"]))
                load(col[:, 3:4], a["L3_gnn_w_score"][:, :])
                load(col[:, 4:5], a["L0_gnn_att_src"].rearrange("a h (d b) -> (a h d) b", b=1))
                load(col[:, 5:6], a["L0_gnn_att_dst"].rearrange("a h (d b) -> (a h d) b", b=1))
                load(rows[:, 0, :], row(a["L0_gnn_proj_b"]))
                load(r.b1[:, 0:F], row(a["L1_gnn_b_upd"]))
                load(rows[:, 1, :], a["L2_gnn_Ws_b"].rearrange("(a h) d -> a (h d)", a=1))
                load(rows[:, 2, :], a["L2_gnn_We_b"].rearrange("(a h) d -> a (h d)", a=1))
                load(r.b2[:, F:2 * F], a["L2_gnn_Wr_b"].rearrange("(a h) d -> a (h d)", a=1))
                load(r.b3[:, 0, 0:F], row(a["L3_gnn_b1"]))
                load(r.b3[:, 1, 0:F], row(a["L3_gnn_b2"]))
                load(r.b3[:, 2, 0:F], row(a["L3_gnn_bu1"]))
                load(r.b3[:, 3, 0:F], row(a["L3_gnn_bu2"]))
                load(rows[:, 3, 0:1], row(a["L3_gnn_b_score"]))
                load(r.gamma[:, :], row(a["L0_gnn_ln_gamma"]).to_broadcast([P, F]))
                load(r.beta[:, :], row(a["L0_gnn_ln_beta"]).to_broadcast([P, F]))
                for h in range(H2):
                    load(r.attw[:, h, :], a["L2_gnn_attn_w"].rearrange("d a -> a d").to_broadcast([P, D2]))
                load(r.attb[:, :], row(a["L2_gnn_attn_b"]).to_broadcast([P, 1]))
                assert n == LOADS
                sp.wait_ge(s_pad, 4)
                sp.dma_start(d.dst[1:1 + E], a["dst"]).then_inc(s_put, 16)
                sp.dma_start(d.src[0:E], a["src"]).then_inc(s_put, 16)
                sp.dma_start(d.dst[1 + E:2 + EPAD].rearrange("(a n) -> a n", a=1), pads[:, 0:1 + EPAD - E]).then_inc(s_put, 16)
                sp.dma_start(d.dst[0:1].rearrange("(a n) -> a n", a=1), pads[:, 95:96]).then_inc(s_put, 16)
                sp.dma_start(d.src[E:EPAD].rearrange("(a n) -> a n", a=1), zi[:, 0:EPAD - E]).then_inc(s_put, 16)
                sp.wait_ge(s_put, 80)
                for n, v in enumerate((d.src[0:EPAD], d.dst[1:1 + EPAD], d.dst[2:2 + EPAD])):
                    sp.dma_start(li[:, n, :], v.rearrange("(q e) -> q e", e=2 * P)).then_inc(s_list, 16)
                sp.wait_ge(s_part, 1)
                sp.dma_start(d.parts.rearrange("(a n) f -> a n f", a=1), part[:, :, :]).then_inc(s_ends, 16)
                sp.wait_ge(s_ends, 16)
                sp.dma_start(r.bias3[:, :], d.parts[:, :]).then_inc(s_ends, 16)
                sp.wait_ge(s_ends, 32)

            @block.gpsimd
            def _(pool):
                pool.memset(pads[:, :], N).then_inc(s_pad, 1)
                pool.wait_ge(s_pad, 1)
                pool.memset(pads[:, EPAD - E:95], N + 1)
                pool.memset(pads[:, 95:96], -1).then_inc(s_pad, 1)
                pool.memset(zi[:, :], 0).then_inc(s_pad, 1)
                pool.memset(r.ones[:, :], 1.0).then_inc(s_pad, 1)
                pool.memset(r.ones3[:, :], 1.0)
                pool.memset(r.ident[:, :], 0.0).then_inc(s_iota, 1)
                pool.memset(mask[:, :], 1.0).then_inc(s_iota, 1)
                pool.memset(r.eps[:, :], LN_EPS).then_inc(s_iota, 1)
                pool.wait_ge(s_iota, 2)
                pool.affine_select(out=r.ident[:, :], in_=r.ident[:, :], compare_op=ALU.not_equal, fill=1.0,
                                   base=0, pattern=[[-1, P]], channel_multiplier=1).then_inc(s_eye, 1)
                pool.affine_select(out=mask[:, :], in_=mask[:, :], compare_op=ALU.is_ge, fill=0.0,
                                   base=0, pattern=[[-D0, H0]], channel_multiplier=1).then_inc(s_eye, 1)
                pool.wait_ge(s_eye, 2)
                pool.affine_select(out=blk[:, :], in_=mask[:, :], compare_op=ALU.is_ge, fill=0.0,
                                   base=D0 - 1, pattern=[[D0, H0]], channel_multiplier=-1).then_inc(s_eye, 1)

            @block.tensor
            def _(pe):
                pe.wait_ge(s_w, 16 * LOADS)
                pe.wait_ge(s_eye, 1)
                pe.wait_ge(s_pad, 4)
                for n in range(3):
                    pe.transpose(ps[:, 0, n * F:(n + 1) * F], wl[:, n, :], r.ident[:, :])
                pe.transpose(ps[:, 1, 0:F], r.w3[:, 2, 0:F], r.ident[:, :])
                pe.transpose(ps[:, 1, F:2 * F], r.w3[:, 3, 0:F], r.ident[:, :]).then_inc(s_pe, 1)
                pe.wait_ge(s_v, 3)
                pe.matmul(ps[:, 2, 0:F], wl[:, 5, :], r.projc[:, :], start=True, stop=True)
                pe.matmul(ps[:, 2, F:F + ATT], wl[:, 5, :], bs[:, :], start=True, stop=True)
                pe.transpose(ps[:, 2, 256:256 + F], wl[:, 5, :], r.ident[:, :])
                pe.matmul(ps[0:1, 3, 0:F], col[:, 0:1], r.projc[:, :], start=True, stop=True)
                pe.matmul(ps[:, 3, F:2 * F], tr[:, 1, :], wl[:, 6, :], start=True, stop=True)
                pe.matmul(ps[:, 3, 2 * F:3 * F], tr[:, 2, :], wl[:, 6, :], start=True, stop=True)
                pe.matmul(ps[0:1, 3, 3 * F:4 * F], col[:, 1:2], wl[:, 6, :], start=True, stop=True)
                pe.matmul(ps[:, 4, 0:1], tr[:, 3, :], col[:, 3:4], start=True, stop=True)
                pe.matmul(ps[:, 4, 1:2], tr[:, 4, :], col[:, 3:4], start=True, stop=True)
                pe.matmul(ps[0:1, 4, 2:3], col[:, 2:3], col[:, 3:4], start=True, stop=True).then_inc(s_pe, 1)
                pe.wait_ge(s_li, 1)
                for n in range(3):
                    for h in range(2):
                        mm = pe.transpose(ps[:, 5 + n // 2, (n % 2 * 2 + h) * P:(n % 2 * 2 + h) * P + half], lf[:, n, h * P:(h + 1) * P],
                                          r.ident[0:half, 0:half])
                mm.then_inc(s_pe, 1)

            @block.vector
            def _(dve):
                done = 0

                def link(ins):
                    nonlocal done
                    done += 1
                    ins.then_inc(s_act, 1)
                    dve.wait_ge(s_act, done)

                dve.memset(r.b3[:, :, F:F + 1], 0.0)
                dve.wait_ge(s_w, 16 * LOADS)
                dve.wait_ge(s_pe, 1)
                for n in range(3):
                    dve.tensor_copy(tr[:, n, :], ps[:, 0, n * F:(n + 1) * F])
                link(dve.tensor_copy(tr[:, 3:5, :], ps[:, 1, 0:2 * F].rearrange("p (n f) -> p n f", n=2)))
                link(dve.reduce_sum(mean[:, 0:1], tr[:, 0, :], AX_X))
                link(dve.tensor_scalar(mean[:, 0:1], mean[:, 0:1], -1.0 / F, None, ALU.mult))
                dve.tensor_scalar(r.projc[:, :], tr[:, 0, :], mean[:, 0:1], None, ALU.add).then_inc(s_v, 1)
                dve.wait_ge(s_eye, 3)
                dve.tensor_scalar(bs[:, 0:H0], blk[:, :], col[:, 4:5], None, ALU.mult).then_inc(s_v, 1)
                dve.tensor_scalar(bs[:, H0:ATT], blk[:, :], col[:, 5:6], None, ALU.mult).then_inc(s_v, 1)
                link(dve.reduce_sum(mean[0:1, 1:2], rows[:, 0, :], AX_X))
                link(dve.tensor_scalar(mean[0:1, 1:2], mean[0:1, 1:2], -1.0 / F, None, ALU.mult))
                link(dve.tensor_scalar(rows[:, 4, :], rows[:, 0, :], mean[0:1, 1:2], None, ALU.add))
                dve.tensor_tensor(r.b2[:, 0:F], rows[:, 1, :], rows[:, 2, :], ALU.add)
                dve.wait_ge(s_pe, 2)
                dve.tensor_copy(r.w0[:, F + ATT:], ps[:, 2, 0:F])
                dve.tensor_copy(r.w0[:, F:F + ATT], ps[:, 2, F:F + ATT])
                dve.tensor_copy(r.w0[:, 0:F], ps[:, 2, 256:256 + F])
                dve.tensor_tensor(r.c0[:, :], ps[0:1, 3, 0:F], rows[:, 4, :], ALU.add)
                dve.tensor_copy(r.wa[:, :], ps[:, 3, F:2 * F])
                dve.tensor_copy(r.wu[:, F:2 * F], ps[:, 3, 2 * F:3 * F])
                dve.tensor_copy(r.b1[:, F:2 * F], ps[0:1, 3, 3 * F:4 * F])
                dve.tensor_copy(r.w3[:, 2, F:F + 1], ps[:, 4, 0:1])
                dve.tensor_copy(r.w3[:, 3, F:F + 1], ps[:, 4, 1:2])
                link(dve.tensor_tensor(r.b3[:, 1, F:F + 1], ps[0:1, 4, 2:3], rows[:, 3, 0:1], ALU.add))
                link(dve.tensor_copy(part[:, 0, :], r.bias[:, :]))
                link(dve.tensor_tensor(res[:, 0, :], r.bias[:, :], part[:, 0, :], ALU.subtract))
                link(dve.tensor_copy(part[:, 1, :], res[:, 0, :]))
                link(dve.tensor_tensor(res[:, 1, :], res[:, 0, :], part[:, 1, :], ALU.subtract))
                dve.tensor_copy(part[:, 2, :], res[:, 1, :]).then_inc(s_part, 1)
                dve.wait_ge(s_list, 48)
                dve.tensor_copy(lf[:, :, :], li[:, :, :]).then_inc(s_li, 1)
                dve.wait_ge(s_pe, 3)
                view = lambda t, h: t[:, :].rearrange("p (q h) -> p q h", h=2)[:, :, h]
                for h in range(2):
                    turned = lambda n: ps[:, 5 + n // 2, (n % 2 * 2 + h) * P:(n % 2 * 2 + h) * P + half]
                    dve.tensor_copy(view(r.src, h), turned(0))
                    dve.tensor_copy(view(r.srcf, h), turned(0))
                    dve.tensor_scalar(view(r.dstg, h), turned(1), float(N - 1), None, ALU.min)
                    dve.tensor_copy(view(r.dstf, h), turned(1))
                    link(dve.tensor_copy(view(nxt, h), turned(2)))
                link(dve.tensor_tensor(same[:, :], nxt[:, :], r.dstf[:, :], ALU.is_equal))
                dve.scalar_tensor_tensor(r.last[:, :], same[:, :], float(SKIP), r.dstf[:, :], ALU.mult, ALU.add)


class Norm:

    def __init__(self, k, name, tiles=1):
        self.stat = k.sb(f"{name}_stat", [P, 4, tiles, 6])
        self.mv = k.sb(f"{name}_mv", [P, 4, tiles, 2])
        self.std = k.sb(f"{name}_std", [P, 4, tiles])
        self.rs = k.sb(f"{name}_rs", [P, 4, tiles])
        self.nm = k.sb(f"{name}_nm", [P, 4, tiles])
        self.s_bn, self.s_turn, self.s_mv, self.s_std, self.s_rs, self.s_nm = (
            k.sem(f"{name}_{x}") for x in ("bn", "turn", "mv", "std", "rs", "nm"))

    def stats(self, dve, src, i, u, p=P, j=1):
        for n in range(j):
            ins = dve.bn_stats(self.stat[0:p, u % 4, n, :], src(n))
        ins.then_inc(self.s_bn, 1)

    def aggregate(self, dve, i, u, p=P, j=1):
        dve.wait_ge(self.s_bn, i + 1)
        dve.sem_inc(self.s_turn, 1)
        for n in range(j):
            ins = dve.bn_aggr(self.mv[0:p, u % 4, n, :], self.stat[0:p, u % 4, n, :])
        ins.then_inc(self.s_mv, 1)

    def root(self, act, r, i, u, p=P, j=1):
        act.wait_ge(self.s_mv, i + 1)
        act.activation(self.std[0:p, u % 4, 0:j], self.mv[0:p, u % 4, 0:j, 1], ACT.Sqrt, bias=r.eps[0:p, :])\
           .then_inc(self.s_std, 1)

    def inverse(self, dve, i, u, p=P, j=1):
        dve.wait_ge(self.s_std, i + 1)
        dve.reciprocal(self.rs[0:p, u % 4, 0:j], self.std[0:p, u % 4, 0:j]).then_inc(self.s_rs, 1)

    def shift(self, dve, i, u, p=P, j=1):
        dve.wait_ge(self.s_rs, i + 1)
        dve.scalar_tensor_tensor(self.nm[0:p, u % 4, 0:j], self.mv[0:p, u % 4, 0:j, 0], -1.0, self.rs[0:p, u % 4, 0:j],
                                 ALU.mult, ALU.mult).then_inc(self.s_nm, 1)

    def relu(self, act, dst, src, i, u, p=P, j=1):
        act.wait_ge(self.s_nm, i + 1)
        for n in range(j):
            ins = act.activation(dst(n), src(n), ACT.Relu, scale=self.rs[0:p, u % 4, n:n + 1],
                                 bias=self.nm[0:p, u % 4, n:n + 1])
        return ins


def last_in(total, u):
    return (total - 1 - u) // RING * RING + u


def turned_width(p, j):
    return (j - 1) * F + p


def node_pass_0(nc, a, d, r):
    with Pass(nc, "n0") as k:
        t0 = k.sb("t0", [P, RING, J, T0W])
        t1 = k.sb("t1", [P, 4, J, T1W])
        h0 = k.sb("h0", [P, 2, J * F])
        ht = k.sb("ht", [P, 2, J * F])
        y = k.sb("y", [P, 4, J, F])
        na, nb, nn = Norm(k, "a", J), Norm(k, "b", J), Norm(k, "c", J)
        pst = k.ps("pst", [P, 2, 512])
        pso = k.ps("pso", [P, 2, J, 512])
        s_in, s_st0, s_st1 = k.ring("in"), k.ring("st0_"), k.ring("st1_")
        s_h0, s_tr, s_ht, s_mm, s_t0, s_y, s_yx, s_x1, s_h1 = (
            k.sem(x) for x in ("h0", "tr", "ht", "mm", "t0", "y", "yx", "x1", "h1"))
        x_of = lambda u, p: lambda n: t0[0:p, u, n, F + ATT:]
        with nc.Block() as block:
            @block.sync
            def _(sp):
                def load(g, u):
                    p, j = span(g)
                    reached(sp, s_st0[u], nth(g, u) - 16)
                    reached(sp, s_yx, g - RING + 1)
                    sp.dma_start(t0[0:p, u, 0:j, F + ATT:], node_rows(a["x"], g)).then_inc(s_in[u], 16)

                def store_0(g, u):
                    p, j = span(g)
                    sp.wait_ge(s_t0, g + 1)
                    sp.dma_start(node_rows(d.t0, g), t0[0:p, u, 0:j, :]).then_inc(s_st0[u], 16)

                def store_1(g, u):
                    p, j = span(g)
                    sp.wait_ge(s_h1, g + 1)
                    sp.dma_start(node_rows(d.t1, g), t1[0:p, u % 4, 0:j, :]).then_inc(s_st1[u], 16)

                pipeline(sp, NGROUPS, [(7, store_0), (0, load), (9, store_1)])
                for u in range(RING):
                    sp.wait_ge(s_st0[u], nth(last_in(NGROUPS, u), u))
                    sp.wait_ge(s_st1[u], nth(last_in(NGROUPS, u), u))

            @block.gpsimd
            def _(pool):
                def add_x(g, u):
                    p, j = span(g)
                    pool.wait_ge(s_y, g + 1)
                    pool.tensor_tensor(y[0:p, u % 4, 0:j, :], y[0:p, u % 4, 0:j, :], t0[0:p, u, 0:j, F + ATT:], ALU.add)\
                        .then_inc(s_yx, 1)

                def add_beta(g, u):
                    p, j = span(g)
                    pool.wait_ge(s_yx, g + 1)
                    sent(pool, s_st1, g, u, 4)
                    reached(pool, s_h1, g - 3)
                    pool.tensor_tensor(t1[0:p, u % 4, 0:j, 0:F], y[0:p, u % 4, 0:j, :],
                                       r.beta[0:p, :].unsqueeze(1).to_broadcast([p, j, F]), ALU.add).then_inc(s_x1, 1)

                pipeline(pool, NGROUPS, [(0, add_x), (0, add_beta)])

            @block.vector
            def _(dve):
                def stats_a(g, u):
                    dve.wait_ge(s_in[u], nth(g, u))
                    na.stats(dve, x_of(u, span(g)[0]), g, u, *span(g))

                def stats_b(g, u):
                    p, j = span(g)
                    dve.wait_ge(s_t0, g + 1)
                    nb.stats(dve, lambda n: pso[0:p, u % 2, n, F + ATT:T0W], g, u, p, j)

                def stats_c(g, u):
                    p, j = span(g)
                    dve.wait_ge(s_x1, g + 1)
                    nn.stats(dve, lambda n: t1[0:p, u % 4, n, 0:F], g, u, p, j)

                def affine(g, u):
                    p, j = span(g)
                    dve.wait_ge(nb.s_rs, g + 1)
                    reached(dve, s_x1, g - 3)
                    for n in range(j):
                        ins = dve.scalar_tensor_tensor(y[0:p, u % 4, n, :], pso[0:p, u % 2, n, F + ATT:T0W],
                                                       nb.rs[0:p, u % 4, n:n + 1], r.gamma[0:p, :], ALU.mult, ALU.mult)
                    ins.then_inc(s_y, 1)

                on = lambda step: lambda g, u: step(dve, g, u, *span(g))
                pipeline(dve, NGROUPS, [
                    (0, stats_a), (5, stats_c), (0, on(na.aggregate)), (1, on(na.inverse)),
                    (6, on(nn.inverse)), (4, on(nb.inverse)), (1, on(na.shift)), (6, on(nn.shift)), (4, affine),
                    (3, stats_b), (5, on(nn.aggregate)), (3, on(nb.aggregate))])

            @block.scalar
            def _(act):
                def relu_a(g, u):
                    p, j = span(g)
                    reached(act, s_tr, g - 1)
                    na.relu(act, lambda n: h0[0:p, u % 2, n * F:(n + 1) * F], x_of(u, p), g, u, p, j).then_inc(s_h0, 1)

                def turned(g, u):
                    act.wait_ge(s_tr, g + 1)
                    reached(act, s_mm, g - 1)
                    w = turned_width(*span(g))
                    act.activation(ht[:, u % 2, 0:w], pst[:, u % 2, 0:w], ACT.Copy).then_inc(s_ht, 1)

                def keep(g, u):
                    p, j = span(g)
                    act.wait_ge(s_mm, g + 1)
                    act.activation(t0[0:p, u, 0:j, 0:F + ATT], pso[0:p, u % 2, 0:j, 0:F + ATT], ACT.Copy).then_inc(s_t0, 1)

                def relu_c(g, u):
                    p, j = span(g)
                    nn.relu(act, lambda n: t1[0:p, u % 4, n, F:], lambda n: t1[0:p, u % 4, n, 0:F], g, u, p, j).then_inc(s_h1, 1)

                root = lambda norm: lambda g, u: norm.root(act, r, g, u, *span(g))
                pipeline(act, NGROUPS, [(1, root(na)), (6, root(nn)), (4, root(nb)), (3, keep), (2, turned), (1, relu_a),
                                        (6, relu_c)])

            @block.tensor
            def _(pe):
                def turn(g, u):
                    p, j = span(g)
                    pe.wait_ge(s_h0, g + 1)
                    reached(pe, s_ht, g - 1)
                    for n in range(j):
                        ins = pe.transpose(pst[:, u % 2, n * F:n * F + p], h0[0:p, u % 2, n * F:(n + 1) * F], r.ident[0:p, 0:p])
                    ins.then_inc(s_tr, 1)

                def product(g, u):
                    p, j = span(g)
                    pe.wait_ge(s_ht, g + 1)
                    reached(pe, s_t0, g - 1)
                    reached(pe, s_y, g - 1)
                    for n in range(j):
                        pe.matmul(pso[0:p, u % 2, n, 0:T0W], ht[:, u % 2, n * F:n * F + p], r.w0[:, :], start=True, stop=False)
                        ins = pe.matmul(pso[0:p, u % 2, n, F + ATT:T0W], r.ones3[:, 0:p], r.bias3[:, C0:B1], start=False, stop=True)
                    ins.then_inc(s_mm, 1)

                pipeline(pe, NGROUPS, [(3, product), (2, turn)])


def node_pass_2(nc, d, r, out):
    with Pass(nc, "n2") as k:
        a = k.sb("a", [P, RING, J, HPW])
        x3 = k.sb("x3", [P, RING, J, F])
        ka = k.sb("ka", [P, 2, J, F])
        ht = k.sb("ht", [P, 2, 2, J * F])
        up = k.sb("up", [P, RING, J, F])
        o = k.sb("o", [P, RING, J, F])
        pst = k.ps("pst", [P, 2, 2, 512])
        pso = k.ps("pso", [P, 2, 2, 512])
        s_in, s_x3, s_stu, s_sto = (k.ring(x) for x in ("in", "x3_", "stu", "sto"))
        s_ka, s_up, s_o = (k.sem(x) for x in ("ka", "up", "o"))
        s_tr, s_ht, s_mm = ([k.sem(f"{x}{n}") for n in range(2)] for x in ("tr", "ht", "mm"))
        grid = lambda n, u, p, j: pso[0:p, n, u % 2, 0:J * F].rearrange("p (j f) -> p j f", j=J)[:, 0:j, :]
        with nc.Block() as block:
            @block.sync
            def _(sp):
                def load(g, u):
                    p, j = span(g)
                    reached(sp, s_ka, g - RING + 1)
                    sp.dma_start(a[0:p, u, 0:j, :], node_rows(d.hp, g)).then_inc(s_in[u], 16)

                def load_x3(g, u):
                    p, j = span(g)
                    reached(sp, s_o, g - RING + 1)
                    sp.dma_start(x3[0:p, u, 0:j, :], node_rows(d.x3, g)).then_inc(s_x3[u], 16)

                def store_up(g, u):
                    p, j = span(g)
                    sp.wait_ge(s_up, g + 1)
                    sp.dma_start(node_rows(d.up, g), up[0:p, u, 0:j, :]).then_inc(s_stu[u], 16)

                def store(g, u):
                    p, j = span(g)
                    sp.wait_ge(s_o, g + 1)
                    sp.dma_start(node_rows(out, g), o[0:p, u, 0:j, :]).then_inc(s_sto[u], 16)

                pipeline(sp, NGROUPS, [(0, load), (4, load_x3), (7, store_up), (11, store)])
                drained(sp, s_stu, NGROUPS)
                drained(sp, s_sto, NGROUPS)

            @block.vector
            def _(dve):
                def keep(g, u):
                    p, j = span(g)
                    dve.wait_ge(s_in[u], nth(g, u))
                    reached(dve, s_tr[0], g - 1)
                    for n in range(j):
                        ins = dve.tensor_scalar(ka[0:p, u % 2, n, :], a[0:p, u, n, 0:F], r.keep[0:p, bass.ds(g * J + n, 1)],
                                                None, ALU.mult)
                    ins.then_inc(s_ka, 1)

                def turned(g, u):
                    w = turned_width(*span(g))
                    dve.wait_ge(s_tr[1], g + 1)
                    reached(dve, s_mm[1], g - 1)
                    dve.tensor_copy(ht[:, 1, u % 2, 0:w], pst[:, 1, u % 2, 0:w]).then_inc(s_ht[1], 1)

                def add(g, u):
                    p, j = span(g)
                    dve.wait_ge(s_mm[1], g + 1)
                    dve.wait_ge(s_x3[u], nth(g, u))
                    reached(dve, s_sto[u], nth(g, u) - 16)
                    dve.tensor_tensor(o[0:p, u, 0:j, :], x3[0:p, u, 0:j, :], grid(1, u, p, j), ALU.add).then_inc(s_o, 1)

                pipeline(dve, NGROUPS, [(0, keep), (7, add), (5, turned)])

            @block.scalar
            def _(act):
                def turned(g, u):
                    w = turned_width(*span(g))
                    act.wait_ge(s_tr[0], g + 1)
                    reached(act, s_mm[0], g - 1)
                    act.activation(ht[:, 0, u % 2, 0:w], pst[:, 0, u % 2, 0:w], ACT.Copy).then_inc(s_ht[0], 1)

                def relu(g, u):
                    p, j = span(g)
                    act.wait_ge(s_mm[0], g + 1)
                    reached(act, s_stu[u], nth(g, u) - 16)
                    act.activation(up[0:p, u, 0:j, :], grid(0, u, p, j), ACT.Relu).then_inc(s_up, 1)

                pipeline(act, NGROUPS, [(3, relu), (1, turned)])

            @block.tensor
            def _(pe):
                def turn(n):
                    def stage(g, u):
                        p, j = span(g)
                        pe.wait_ge((s_ka, s_up)[n], g + 1)
                        reached(pe, s_ht[n], g - 1)
                        for v in range(j):
                            ins = pe.transpose(pst[:, n, u % 2, v * F:v * F + p], (ka[0:p, u % 2, v, :], up[0:p, u, v, :])[n],
                                               r.ident[0:p, 0:p])
                        ins.then_inc(s_tr[n], 1)
                    return stage

                def product(n):
                    def stage(g, u):
                        p, j = span(g)
                        pe.wait_ge(s_ht[n], g + 1)
                        reached(pe, (s_up, s_o)[n], g - 1)
                        bias = B3 + (2 + n) * (F + 1)
                        for v in range(j):
                            ps = pso[0:p, n, u % 2, v * F:(v + 1) * F]
                            pe.matmul(ps, ht[:, n, u % 2, v * F:v * F + p], r.w3[:, 4 + 2 * n, 0:F], start=True, stop=False)
                            ins = pe.matmul(ps, r.ones3[:, 0:p], r.bias3[:, bias:bias + F], start=False, stop=True)
                        ins.then_inc(s_mm[n], 1)
                    return stage

                pipeline(pe, NGROUPS, [(0, turn(0)), (6, product(1)), (2, product(0)), (4, turn(1))])


def collect(nc, d, r):
    with Pass(nc, "col") as k:
        a = k.sb("a", [P, RING, J, HPW])
        logit = k.sb("logit", [P, NGROUPS, J])
        s_in = k.ring("in")
        s_z, s_turn, s_pre, s_exp, s_sum = (k.sem(x) for x in ("z", "turn", "pre", "exp", "sum"))
        with nc.Block() as block:
            @block.sync
            def _(sp):
                def load(g, u):
                    p, j = span(g)
                    reached(sp, s_z, g - RING + 1)
                    sp.dma_start(a[0:p, u, 0:j, :], node_rows(d.hp, g)).then_inc(s_in[u], 16)

                pipeline(sp, NGROUPS, [(0, load)])

            @block.vector
            def _(dve):
                dve.memset(r.z[:, :, :], -1.0).then_inc(s_pre, 1)
                dve.memset(logit[:, :, :], 0.0).then_inc(s_pre, 1)
                dve.wait_ge(s_pre, 2)

                def take(g, u):
                    p, j = span(g)
                    dve.wait_ge(s_in[u], nth(g, u))
                    dve.sem_inc(s_turn, 1)
                    dve.tensor_copy(logit[0:p, bass.ds(g, 1), 0:j], a[0:p, u, 0:j, F].unsqueeze(1)).then_inc(s_z, 1)

                pipeline(dve, NGROUPS, [(0, take)])
                dve.wait_ge(s_exp, 1)
                dve.tensor_scalar(logit[:, :, :], logit[:, :, :], 1.0, None, ALU.add).then_inc(s_sum, 1)
                dve.wait_ge(s_sum, 1)
                dve.reciprocal(r.z[:, 0:FULL, :], logit[:, 0:FULL, :])
                dve.reciprocal(r.z[0:REST, FULL, 0:1], logit[0:REST, FULL, 0:1])

            @block.scalar
            def _(act):
                act.wait_ge(s_z, NGROUPS)
                act.activation(logit[:, :, :], logit[:, :, :], ACT.Exp, scale=-1.0).then_inc(s_exp, 1)


class SegmentSum:

    def __init__(self, k, r, parts=1):
        self.r, self.parts = r, parts
        self.sf = k.sb("segf", [P, 4, P])
        self.st = k.sb("sums", [P, 4, parts, P])
        self.ps = k.ps("ps_sum", [P, 2, 512])
        self.s_sf, self.s_turn, self.s_sum, self.s_st = (k.sem(x) for x in ("sf", "sf_turn", "sum", "st"))

    def clear(self, dve):
        dve.memset(self.st[:, :, :, :], 0.0).then_inc(self.s_st, 1)

    def widen(self, act, t, u):
        reached(act, self.s_sum, t - 3)
        act.sem_inc(self.s_turn, 1)
        act.activation(self.sf[:, u % 4, :], self.r.seg[:, bass.ds(t, 1), :].rearrange("p a f -> p (a f)"), ACT.Copy)\
           .then_inc(self.s_sf, 1)

    def sum(self, pe, rows, t, u):
        pe.wait_ge(self.s_sf, t + 1)
        reached(pe, self.s_st, t)
        for n, part in enumerate(rows):
            ins = pe.matmul(self.ps[:, u % 2, n * P:(n + 1) * P], part, self.sf[:, u % 4, :], start=True, stop=True)
        ins.then_inc(self.s_sum, 1)

    def follow(self, dve, used, t, u):
        dve.wait_ge(self.s_sum, t + 1)
        dve.wait_ge(self.s_st, t + 1)
        reached(dve, used, t - 3)
        for n in range(self.parts):
            ins = dve.scalar_tensor_tensor(self.st[:, u % 4, n, :].unsqueeze(1), self.r.goes_on[:, bass.ds(t, 1), :],
                                           self.st[:, (u - 1) % 4, n, P - 1:P], self.ps[:, u % 2, n * P:(n + 1) * P].unsqueeze(1),
                                           ALU.mult, ALU.add)
        ins.then_inc(self.s_st, 1)


class Indices:

    def __init__(self, k, name, table):
        self.table = table
        self.at = k.sb(name, [P, RING], I32)
        self.s, self.s_turn, self.s_pool = k.sem(name), k.sem(f"{name}_turn"), k.sem(f"{name}_pool")

    def stage(self, dve, t, u, used):
        reached(dve, used[u], nth(t, u) - 16)
        dve.sem_inc(self.s_turn, 1)
        dve.tensor_copy(self.at[:, u:u + 1], self.table[:, bass.ds(t, 1)]).then_inc(self.s, 1)

    def gather(self, pool, dst, table, t, u, arrived):
        pool.wait_ge(self.s, t + 1)
        pool.sem_inc(self.s_pool, 1)
        pool.indirect_dma_start(dst, None, table, bass.IndirectOffsetOnAxis(ap=self.at[:, u:u + 1], axis=0))\
            .then_inc(arrived[u], 16)

    def scatter(self, pool, table, src, t, u, written):
        pool.wait_ge(self.s, t + 1)
        pool.sem_inc(self.s_pool, 1)
        pool.indirect_dma_start(table, bass.IndirectOffsetOnAxis(ap=self.at[:, u:u + 1], axis=0), src, None,
                                bounds_check=N - 1, oob_is_err=False).then_inc(written[u], 16)


def drained(eng, sems, total):
    for u in range(RING):
        eng.wait_ge(sems[u], nth(last_in(total, u), u))


def node_pass_1_edge_pass_0a(nc, d, r):
    cols = F + 1
    with Pass(nc, "n1") as k:
        J = PAIR
        t1 = k.sb("t1", [P, RING, J, T1W])
        ht = k.sb("ht", [P, 2, 3, J * F])
        x2 = k.sb("x2", [P, 4, J, F])
        h2 = k.sb("h2", [P, 4, J, F])
        g1 = k.sb("g1", [P, 4, J, F])
        o = k.sb("o", [P, 4, J, HPW])
        nn = Norm(k, "c", J)
        gs = k.sb("gs", [P, RING, T0W])
        gd = k.sb("gd", [P, RING, T0W])
        src, dst = Indices(k, "src", r.src), Indices(k, "dst", r.dstg)
        s_gs, s_gd, s_eh, s_ed = (k.ring(x) for x in ("gs", "gd", "eh", "ed"))
        s_l, s_turn = k.sem("l"), k.sem("turn")
        dr = k.sb("dr", [P, RING, 1 + P], I32)
        s_row, s_seg, s_seg_turn = k.ring("row"), k.sem("seg"), k.sem("seg_turn")
        pst = k.ps("pst", [P, 3, 512])
        pso = k.ps("pso", [P, 3, 512])
        s_t1, s_stx, s_sth, s_stg, s_sto = (k.ring(x) for x in ("t1_", "stx", "sth", "stg", "sto"))
        s_x2, s_h2, s_g, s_o, s_pre = (k.sem(x) for x in ("x2", "h2", "g", "o", "pre"))
        s_tr, s_ht, s_mm = ([k.sem(f"{x}{n}") for n in range(3)] for x in ("tr", "ht", "mm"))
        view = lambda u, p, j: pso[0:p, 2, 0:J * cols].rearrange("p (j f) -> p j f", j=J)[:, 0:j, :]
        grid = lambda n, p, j: pso[0:p, n, 0:J * F].rearrange("p (j f) -> p j f", j=J)[:, 0:j, :]
        with nc.Block() as block:
            @block.sync
            def _(sp):
                def load(g, u):
                    p, j = span(g, J)
                    reached(sp, s_x2, g - RING + 1)
                    reached(sp, s_tr[0], g - RING + 1)
                    sp.dma_start(t1[0:p, u, 0:j, :], node_rows(d.t1, g, J)).then_inc(s_t1[u], 16)

                def store(ready, table, rows, sems):
                    def stage(g, u):
                        p, j = span(g, J)
                        sp.wait_ge(ready, g + 1)
                        sp.dma_start(node_rows(table, g, J), rows[0:p, u % 4, 0:j, :]).then_inc(sems[u], 16)
                    return stage

                def keep(t, u):
                    sp.wait_ge(s_gs[u], nth(t, u))
                    sp.dma_start(edge_rows(d.eh, t), gs[:, u, 0:F]).then_inc(s_eh[u], 16)

                def destinations(t, u):
                    reached(sp, s_seg, t - RING + 1)
                    sp.dma_start(dr[:, u, :], d.dst[bass.ds(t * P, 1 + P)].rearrange("(a n) -> a n", a=1)
                                 .to_broadcast([P, 1 + P])).then_inc(s_row[u], 16)

                pipeline(sp, ET, [(0, load), (0, destinations), (3, store(s_x2, d.x3, x2, s_stx)), (3, keep), (6, store(s_h2, d.h2, h2, s_sth)),
                                  (9, store(s_g, d.g, g1, s_stg)), (12, store(s_o, d.hp, o, s_sto))])
                for sems in (s_stx, s_sth, s_stg, s_sto, s_eh):
                    drained(sp, sems, ET)

            @block.gpsimd
            def _(pool):
                def gather(t, u):
                    reached(pool, s_eh[u], nth(t, u) - 16)
                    reached(pool, s_ed[u], nth(t, u) - 16)
                    reached(pool, s_l, t - RING + 1)
                    src.gather(pool, gs[:, u, :], d.t0, t, u, s_gs)
                    dst.gather(pool, gd[:, u, :], d.t0, t, u, s_gd)

                def keep(t, u):
                    pool.wait_ge(s_gd[u], nth(t, u))
                    pool.sem_inc(s_turn, 1)
                    pool.dma_start(edge_rows(d.ed, t), gd[:, u, :]).then_inc(s_ed[u], 16)

                pipeline(pool, ET, [(0, gather), (3, keep)])
                drained(pool, s_ed, ET)

            @block.vector
            def _(dve):
                dve.memset(o[:, :, :, F:], 0.0).then_inc(s_pre, 1)
                dve.wait_ge(s_pre, 1)

                def turned(n):
                    def stage(g, u):
                        w = turned_width(*span(g, J))
                        dve.wait_ge(s_tr[n], g + 1)
                        reached(dve, s_mm[n], g - 1)
                        dve.tensor_copy(ht[:, u % 2, n, 0:w], pst[:, n, 0:w]).then_inc(s_ht[n], 1)
                    return stage

                def add(g, u):
                    p, j = span(g, J)
                    dve.wait_ge(s_mm[0], g + 1)
                    sent(dve, s_stx, g, u, 4)
                    reached(dve, s_h2, g - 3)
                    dve.tensor_tensor(x2[0:p, u % 4, 0:j, :], t1[0:p, u, 0:j, 0:F], grid(0, p, j), ALU.add).then_inc(s_x2, 1)

                def stats(g, u):
                    p, j = span(g, J)
                    dve.wait_ge(s_x2, g + 1)
                    nn.stats(dve, lambda n: x2[0:p, u % 4, n, :], g, u, p, j)

                on = lambda step: lambda g, u: step(dve, g, u, *span(g, J))
                def logits(t, u):
                    dve.wait_ge(s_gs[u], nth(t, u))
                    dve.wait_ge(s_gd[u], nth(t, u))
                    dve.tensor_tensor(r.logit[:, bass.ds(t, 1), :], gs[:, u, F:F + H0].unsqueeze(1),
                                      gd[:, u, F + H0:F + ATT].unsqueeze(1), ALU.add)
                    dve.tensor_tensor(r.self_logit[:, bass.ds(t, 1), :], gd[:, u, F:F + H0].unsqueeze(1),
                                      gd[:, u, F + H0:F + ATT].unsqueeze(1), ALU.add).then_inc(s_l, 1)

                def segments(t, u):
                    dve.wait_ge(s_row[u], nth(t, u))
                    dve.sem_inc(s_seg_turn, 1)
                    dve.tensor_scalar(r.seg[:, bass.ds(t, 1), :], dr[:, u, 1:].unsqueeze(1), r.dstf[:, bass.ds(t, 1)], None,
                                      ALU.is_equal)
                    dve.tensor_tensor(r.goes_on[:, bass.ds(t, 1), :], dr[:, u, 1:].unsqueeze(1),
                                      dr[:, u, 0:1].unsqueeze(1).to_broadcast([P, 1, P]), ALU.is_equal).then_inc(s_seg, 1)

                pipeline(dve, ET, [(3, segments), (0, lambda t, u: src.stage(dve, t, u, s_gs)), (0, lambda t, u: dst.stage(dve, t, u, s_gd)),
                                   (2, add), (4, on(nn.inverse)), (0, turned(0)), (2, stats), (4, on(nn.shift)), (9, turned(2)),
                                   (3, logits), (2, on(nn.aggregate))])

            @block.scalar
            def _(act):
                def turned(g, u):
                    w = turned_width(*span(g, J))
                    act.wait_ge(s_tr[1], g + 1)
                    reached(act, s_mm[1], g - 1)
                    act.activation(ht[:, u % 2, 1, 0:w], pst[:, 1, 0:w], ACT.Copy).then_inc(s_ht[1], 1)

                def relu_h(g, u):
                    p, j = span(g, J)
                    sent(act, s_sth, g, u, 4)
                    reached(act, s_tr[1], g - 3)
                    nn.relu(act, lambda n: h2[0:p, u % 4, n, :], lambda n: x2[0:p, u % 4, n, :], g, u, p, j).then_inc(s_h2, 1)

                def relu_g(g, u):
                    p, j = span(g, J)
                    act.wait_ge(s_mm[1], g + 1)
                    sent(act, s_stg, g, u, 4)
                    reached(act, s_tr[2], g - 3)
                    act.activation(g1[0:p, u % 4, 0:j, :], grid(1, p, j), ACT.Relu).then_inc(s_g, 1)

                def finish(g, u):
                    p, j = span(g, J)
                    act.wait_ge(s_mm[2], g + 1)
                    sent(act, s_sto, g, u, 4)
                    act.activation(o[0:p, u % 4, 0:j, 0:cols], view(u, p, j), ACT.Copy).then_inc(s_o, 1)

                act.wait_ge(s_pre, 1)
                pipeline(act, ET, [(11, finish), (8, relu_g), (3, lambda g, u: nn.root(act, r, g, u, *span(g, J))), (5, relu_h),
                                   (6, turned)])

            @block.tensor
            def _(pe):
                def turn(n):
                    def stage(g, u):
                        p, j = span(g, J)
                        if n == 0:
                            pe.wait_ge(s_t1[u], nth(g, u))
                        else:
                            pe.wait_ge((s_h2, s_g)[n - 1], g + 1)
                        reached(pe, s_ht[n], g)
                        rows = lambda v: (t1[0:p, u, v, F:], h2[0:p, u % 4, v, :], g1[0:p, u % 4, v, :])[n]
                        for v in range(j):
                            ins = pe.transpose(pst[:, n, v * F:v * F + p], rows(v), r.ident[0:p, 0:p])
                        ins.then_inc(s_tr[n], 1)
                    return stage

                def product(n):
                    def stage(g, u):
                        p, j = span(g, J)
                        w = (F, F, cols)[n]
                        pe.wait_ge(s_ht[n], g + 1)
                        reached(pe, (s_x2, s_g, s_o)[n], g)
                        weights = (r.wu[:, 0:F], r.w3[:, 0, 0:F], r.w3[:, 2, 0:cols])[n]
                        bias = (B1, B3, B3 + F + 1)[n]
                        for v in range(j):
                            ps = pso[0:p, n, v * w:(v + 1) * w]
                            pe.matmul(ps, ht[:, u % 2, n, v * F:v * F + p], weights, start=True, stop=False)
                            ins = pe.matmul(ps, r.ones3[:, 0:p], r.bias3[:, bias:bias + w], start=False, stop=True)
                        ins.then_inc(s_mm[n], 1)
                    return stage

                pipeline(pe, ET, [(0, turn(0)), (1, product(0)), (6, turn(1)), (9, turn(2)), (7, product(1)), (10, product(2))])


def softmax_weights(nc, d, r, name, own_loop):
    rows = H0 * CH
    with Pass(nc, name) as k:
        xp = k.sb("xp", [P, 2, CT, H0, CH])
        xt = k.sb("xt", [rows, CL])
        xs = k.sb("xs", [rows, CL])
        fw = k.sb("fw", [rows, CL])
        bw = k.sb("bw", [rows, CL])
        ids = k.sb("ids", [rows, 3, CL], I32)
        gate = [ids[:, 2 * n, :].bitcast(F32) for n in range(2)]
        spare = ids[:, 1, :].bitcast(F32)
        eid = k.sb("eid", [H0, 4, CH], I32)
        egate = k.sb("egate", [H0, 2, CH])
        es = k.sb("es", [H0, CH])
        ec = k.sb("ec", [H0, CH])
        cin = k.sb("cin", [rows, 1])
        ps = k.ps("ps", [P, 8, 512])
        s_ids, s_eid, s_xp, s_up, s_dn, s_x = (k.sem(x) for x in ("ids", "eid", "xp", "up", "dn", "x"))
        s_v, s_e, s_a, s_end, s_in = (k.sem(x) for x in ("v", "e", "a", "end", "in"))
        s_hop = [k.sem(f"hop{n}") for n in range(8)]
        with nc.Block() as block:
            @block.sync
            def _(sp):
                for n in range(3):
                    for h in range(H0):
                        sp.dma_start(ids[h * CH:(h + 1) * CH, n, :], d.dst[n:n + EPAD].rearrange("(c e) -> c e", c=CH))\
                          .then_inc(s_ids, 16)
                with nc.allow_non_contiguous_dma(reason="four words of each chunk"):
                    for n, at in enumerate((0, CL, CL + 1, 1)):
                        sp.dma_start(eid[:, n, :], d.dst[at:at + EPAD].rearrange("(a c e) -> a c e", a=1, e=CL)[:, :, 0]
                                     .to_broadcast([H0, CH])).then_inc(s_eid, 16)
                for n in range(4):
                    sp.wait_ge(s_end, n + 1)
                    with nc.allow_non_contiguous_dma(reason="one word a partition"):
                        sp.dma_start(d.hop[2 * n:2 * n + 1, :].rearrange("a (n b) -> (a n) b", b=1),
                                     fw[:, CL - 1:CL] if n % 2 == 0 else bw[:, 0:1]).then_inc(s_hop[2 * n], 16)
                        sp.wait_ge(s_hop[2 * n], 16)
                        sp.dma_start(es[:, :], d.hop[2 * n, :].rearrange("(h c) -> h c", c=CH)).then_inc(s_hop[2 * n], 16)
                        sp.wait_ge(s_in, n + 1)
                        sp.dma_start(d.hop[2 * n + 1, :].rearrange("(h c) -> h c", c=CH), ec[:, :]).then_inc(s_hop[2 * n + 1], 16)
                        sp.wait_ge(s_hop[2 * n + 1], 16)
                        sp.dma_start(cin[:, :], d.hop[2 * n + 1:2 * n + 2, :].rearrange("a (n b) -> (a n) b", b=1))\
                          .then_inc(s_hop[2 * n + 1], 16)

            @block.vector
            def _(dve):
                done = 0

                def link(ins):
                    nonlocal done
                    done += 1
                    ins.then_inc(s_v, 1)
                    dve.wait_ge(s_v, done)

                def carried_scans(n, op0, op1, start, back):
                    for m, (out, by, of, ends, carries) in enumerate((
                            (fw[:, :], gate[0], xt[:, :], slice(None), (ec[:, 1:CH], es[:, 0:CH - 1])),
                            (bw[:, ::-1], gate[1][:, ::-1], fw[:, ::-1], slice(None, None, -1), (ec[:, 0:CH - 1], es[:, 1:CH])))):
                        if m == 1:
                            back()
                        link(dve.tensor_tensor_scan(out, by, of, initial=start, op0=op0, op1=op1))
                        link(dve.memset(ec[:, :], start))
                        dve.sem_inc(s_end, 1)
                        dve.wait_ge(s_hop[2 * (n + m)], 32)
                        link(dve.tensor_tensor_scan(es[:, ends], egate[:, m, ends], es[:, ends], initial=start, op0=op0, op1=op1))
                        dve.tensor_copy(*carries).then_inc(s_in, 1)
                        dve.wait_ge(s_hop[2 * (n + m) + 1], 32)
                        link(dve.tensor_tensor_scan(out, by, of, initial=cin[:, :], op0=op0, op1=op1))

                if own_loop:
                    for v in (r.logit, r.self_logit):
                        ins = dve.scalar_tensor_tensor(v[:, :, :], v[:, :, :], 0.2, v[:, :, :], ALU.mult, ALU.max)
                    link(ins)
                else:
                    link(dve.memset(r.logit[:, :, H2:], 0.0))
                    link(dve.tensor_scalar(r.logit[:, :, 0:H2], r.logit[:, :, 0:H2], r.attb[:, :], None, ALU.add))
                values = (r.logit, r.self_logit) if own_loop else (r.logit,)
                turned = (xt, xs)
                for n, v in enumerate(values):
                    for h in range(H0):
                        ins = dve.tensor_copy(xp[:, n, :, h, :], v[:, :, h].rearrange("p (c j) -> p j c", j=CT))
                    ins.then_inc(s_xp, 1)
                dve.wait_ge(s_ids, 16 * 3 * H0)
                dve.tensor_tensor(gate[0], ids[:, 0, :], ids[:, 1, :], ALU.is_equal)
                link(dve.tensor_tensor(gate[1], ids[:, 2, :], ids[:, 1, :], ALU.is_equal))
                dve.wait_ge(s_eid, 16 * 4)
                dve.tensor_tensor(egate[:, 0, :], eid[:, 0, :], eid[:, 1, :], ALU.is_equal)
                dve.tensor_tensor(egate[:, 1, :], eid[:, 2, :], eid[:, 3, :], ALU.is_equal)
                for g in gate:
                    link(dve.tensor_scalar(g, g, 2 * BIG, -BIG, ALU.mult, ALU.add))
                link(dve.tensor_scalar(egate[:, :, :], egate[:, :, :], 2 * BIG, -BIG, ALU.mult, ALU.add))
                for n in range(len(values)):
                    for b in range(4):
                        w = min(4, CT - 4 * b) * P
                        dve.wait_ge(s_up, 4 * n + b + 1)
                        ins = dve.tensor_copy(turned[n][:, 4 * b * P:4 * b * P + w], ps[0:rows, 4 * n + b, 0:w])
                link(ins)
                carried_scans(0, ALU.min, ALU.max, -BIG, lambda: None)
                if own_loop:
                    link(dve.tensor_tensor(bw[:, :], bw[:, :], xs[:, :], ALU.max))
                    dve.tensor_tensor(xs[:, :], xs[:, :], bw[:, :], ALU.subtract)
                dve.tensor_tensor(xt[:, :], xt[:, :], bw[:, :], ALU.subtract).then_inc(s_e, 1)
                dve.tensor_scalar(egate[:, :, :], egate[:, :, :], 0.0, None, ALU.is_gt)
                for g in gate:
                    link(dve.tensor_scalar(g, g, 0.0, None, ALU.is_gt))
                dve.wait_ge(s_a, len(values))
                if own_loop:
                    link(dve.tensor_tensor(bw[:, :], xs[:, :], gate[0], ALU.mult))
                    link(dve.tensor_tensor(xs[:, :], xs[:, :], bw[:, :], ALU.subtract))
                    dve.tensor_copy(spare, xt[:, :])
                    link(dve.tensor_tensor(xt[:, :], xt[:, :], xs[:, :], ALU.add))

                def whole():
                    link(dve.tensor_tensor(bw[:, :], fw[:, :], gate[1], ALU.mult))
                    link(dve.tensor_tensor(fw[:, :], fw[:, :], bw[:, :], ALU.subtract))

                carried_scans(2, ALU.mult, ALU.add, 0.0, whole)
                link(dve.reciprocal(bw[:, :], bw[:, :]))
                if own_loop:
                    dve.tensor_tensor(xs[:, :], xs[:, :], bw[:, :], ALU.mult)
                    dve.tensor_tensor(xt[:, :], spare, bw[:, :], ALU.mult).then_inc(s_x, 1)
                else:
                    dve.tensor_tensor(xt[:, :], xt[:, :], bw[:, :], ALU.mult).then_inc(s_x, 1)
                for n, v in enumerate(values):
                    for b in range(4):
                        dve.wait_ge(s_dn, 4 * n + b + 1)
                        for j in range(min(4, CT - 4 * b)):
                            dve.tensor_copy(v[:, :, :].rearrange("p (c j) h -> p j h c", j=CT)[:, 4 * b + j, :, :],
                                            ps[:, 4 * n + b, j * P:j * P + rows].rearrange("p (h c) -> p h c", c=CH))

            @block.scalar
            def _(act):
                act.wait_ge(s_e, 1)
                act.activation(xt[:, :], xt[:, :], ACT.Exp).then_inc(s_a, 1)
                if own_loop:
                    act.activation(xs[:, :], xs[:, :], ACT.Exp).then_inc(s_a, 1)

            @block.tensor
            def _(pe):
                turned = (xt, xs) if own_loop else (xt,)
                for n in range(len(turned)):
                    pe.wait_ge(s_xp, n + 1)
                    for j in range(CT):
                        ins = pe.transpose(ps[0:rows, 4 * n + j // 4, j % 4 * P:(j % 4 + 1) * P],
                                           xp[:, n, j, :, :].rearrange("p h c -> p (h c)"), r.ident[:, :])
                        if j % 4 == 3 or j == CT - 1:
                            ins.then_inc(s_up, 1)
                pe.wait_ge(s_x, 1)
                for n, t in enumerate(turned):
                    for j in range(CT):
                        ins = pe.transpose(ps[:, 4 * n + j // 4, j % 4 * P:j % 4 * P + rows], t[:, j * P:(j + 1) * P],
                                           r.ident[0:rows, 0:rows])
                        if j % 4 == 3 or j == CT - 1:
                            ins.then_inc(s_dn, 1)


def edge_pass_2a(nc, a, d, r):
    with Pass(nc, "e2a") as k:
        gs = k.sb("gs", [P, RING, F])
        gd = k.sb("gd", [P, RING, F])
        ea = k.sb("ea", [P, RING, F])
        xt = k.sb("xt", [P, 4, 3 * F])
        e = k.sb("e", [P, RING, F])
        z, zc, uu, w, w2, wi, zw, zv = (k.sb(x, [P, 4, F]) for x in ("z", "zc", "uu", "w", "w2", "wi", "zw", "zv"))
        src, dst = Indices(k, "src", r.src), Indices(k, "dst", r.dstg)
        pst = k.ps("pst", [P, 4, 512])
        pso = k.ps("pso", [P, 4, 512])
        s_gs, s_gd, s_ea, s_e = (k.ring(x) for x in ("gs", "gd", "ea", "e"))
        names = ("tr", "xt", "mm", "ev", "z", "zc", "u", "w", "w2", "wi", "zw", "zv", "zz", "l")
        s_tr, s_xt, s_mm, s_ev, s_z, s_zc, s_u, s_w, s_w2, s_wi, s_zw, s_zv, s_zz, s_l = (k.sem(x) for x in names)
        with nc.Block() as block:
            @block.gpsimd
            def _(pool):
                def gather(t, u):
                    reached(pool, s_tr, t - RING + 1)
                    src.gather(pool, gs[:, u, :], d.h2, t, u, s_gs)
                    dst.gather(pool, gd[:, u, :], d.h2, t, u, s_gd)

                def weigh(t, u):
                    pool.wait_ge(s_z, t + 1)
                    reached(pool, s_zv, t - 3)
                    pool.tensor_tensor(zw[:, u % 4, :], z[:, u % 4, :], r.attw[:, :, :].rearrange("p h d -> p (h d)"), ALU.mult)\
                        .then_inc(s_zw, 1)

                pipeline(pool, ET, [(0, gather), (6, weigh)])

            @block.sync
            def _(sp):
                def load(t, u):
                    n = EREST if isinstance(t, int) and t == ET - 1 else P
                    reached(sp, s_tr, t - RING + 1)
                    sp.dma_start(ea[0:n, u, :], edge_rows(a["edge_attr_128"], t, n)).then_inc(s_ea[u], 16)

                def store(t, u):
                    sp.wait_ge(s_ev, t + 1)
                    sp.dma_start(edge_rows(d.eh, t), e[:, u, :]).then_inc(s_e[u], 16)

                pipeline(sp, ET, [(0, load), (7, store)])
                drained(sp, s_e, ET)

            @block.vector
            def _(dve):
                def add(t, u):
                    dve.wait_ge(s_ev, t + 1)
                    reached(dve, s_zw, t - 3)
                    dve.tensor_tensor(z[:, u % 4, :], e[:, u, :], pso[:, u % 4, F:2 * F], ALU.add).then_inc(s_z, 1)

                def cap(t, u):
                    dve.wait_ge(s_z, t + 1)
                    dve.tensor_scalar(zc[:, u % 4, :], z[:, u % 4, :], 20.0, None, ALU.min).then_inc(s_zc, 1)

                def square(t, u):
                    dve.wait_ge(s_u, t + 1)
                    dve.scalar_tensor_tensor(w[:, u % 4, :], uu[:, u % 4, :], 2.0, uu[:, u % 4, :], ALU.add, ALU.mult).then_inc(s_w, 1)

                def invert(t, u):
                    dve.wait_ge(s_w2, t + 1)
                    dve.reciprocal(wi[:, u % 4, :], w2[:, u % 4, :]).then_inc(s_wi, 1)

                def times_w(t, u):
                    dve.wait_ge(s_zw, t + 1)
                    dve.tensor_tensor(zv[:, u % 4, :], zw[:, u % 4, :], w[:, u % 4, :], ALU.mult).then_inc(s_zv, 1)

                def divide(t, u):
                    dve.wait_ge(s_wi, t + 1)
                    dve.wait_ge(s_zv, t + 1)
                    dve.tensor_tensor(wi[:, u % 4, :], zv[:, u % 4, :], wi[:, u % 4, :], ALU.mult).then_inc(s_zz, 1)

                def reduce(t, u):
                    dve.wait_ge(s_zz, t + 1)
                    dve.tensor_reduce(r.logit[:, bass.ds(t, 1), 0:H2].rearrange("p a h -> p (a h)"),
                                      wi[:, u % 4, :].rearrange("p (h d) -> p h d", d=D2), AX_X, ALU.add).then_inc(s_l, 1)

                pipeline(dve, ET, [
                    (0, lambda t, u: src.stage(dve, t, u, s_gs)), (0, lambda t, u: dst.stage(dve, t, u, s_gd)),
                    (5, add), (6, square), (5, cap), (7, invert), (7, times_w), (8, reduce), (7, divide)])

            @block.scalar
            def _(act):
                def turned(t, u):
                    act.wait_ge(s_tr, t + 1)
                    reached(act, s_mm, t - 3)
                    act.activation(xt[:, u % 4, :], pst[:, u % 4, 0:3 * F], ACT.Copy).then_inc(s_xt, 1)

                def keep(t, u):
                    act.wait_ge(s_mm, t + 1)
                    reached(act, s_e[u], nth(t, u) - 16)
                    reached(act, s_z, t - RING + 1)
                    act.activation(e[:, u, :], pso[:, u % 4, 0:F], ACT.Copy).then_inc(s_ev, 1)

                def exp(t, u):
                    act.wait_ge(s_zc, t + 1)
                    reached(act, s_w, t - 3)
                    act.activation(uu[:, u % 4, :], zc[:, u % 4, :], ACT.Exp).then_inc(s_u, 1)

                def plus_two(t, u):
                    act.wait_ge(s_w, t + 1)
                    reached(act, s_wi, t - 3)
                    act.activation(w2[:, u % 4, :], w[:, u % 4, :], ACT.Copy, bias=2.0).then_inc(s_w2, 1)

                pipeline(act, ET, [(2, keep), (3, exp), (4, plus_two), (0, turned)])

            @block.tensor
            def _(pe):
                def turn(t, u):
                    reached(pe, s_xt, t - 3)
                    for n, (rows, sem) in enumerate(((ea, s_ea), (gs, s_gs), (gd, s_gd))):
                        pe.wait_ge(sem[u], nth(t, u))
                        ins = pe.transpose(pst[:, u % 4, n * F:(n + 1) * F], rows[:, u, :], r.ident[:, :])
                    ins.then_inc(s_tr, 1)

                def product(t, u):
                    pe.wait_ge(s_xt, t + 1)
                    reached(pe, s_ev, t - 3)
                    reached(pe, s_z, t - 3)
                    x = lambda n: xt[:, u % 4, n * F:(n + 1) * F]
                    pe.matmul(pso[:, u % 4, 0:2 * F], r.ones3[:, :], r.bias3[:, B2:B3], start=True, stop=False)
                    pe.matmul(pso[:, u % 4, 0:F], x(0), r.we[:, :], start=False, stop=False)
                    pe.matmul(pso[:, u % 4, 0:F], x(1), r.ws[:, :], start=False, stop=False)
                    pe.matmul(pso[:, u % 4, F:2 * F], x(2), r.wr[:, :], start=False, stop=True).then_inc(s_mm, 1)

                pipeline(pe, ET, [(2, product), (0, turn)])


def edge_pass_0b(nc, d, r):
    with Pass(nc, "e0b") as k:
        hs = k.sb("hs", [P, RING, F])
        hd = k.sb("hd", [P, RING, T0W])
        own = k.sb("own", [P, 4, F])
        m = k.sb("m", [P, 4, 2, F])
        y = k.sb("y", [P, 4, 2, F])
        o = k.sb("o", [P, RING, T1W])
        seg = SegmentSum(k, r)
        nb, nn = Norm(k, "b"), Norm(k, "c")
        last = Indices(k, "last", r.last)
        px = k.ps("px", [P, 4, 512])
        s_hs, s_hd, s_w, s_st = k.ring("hs"), k.ring("hd"), k.ring("w"), k.ring("st")
        names = ("own", "m", "m2", "mm", "y", "yx", "x1", "h1")
        s_own, s_m, s_m2, s_mm, s_y, s_yx, s_x1, s_h1 = (k.sem(x) for x in names)
        heads = lambda v: v.rearrange("p (h d) -> p h d", d=D0)
        wide = lambda v: v.rearrange("p a h -> p (a h)").unsqueeze(2).to_broadcast([P, H0, D0])
        with nc.Block() as block:
            @block.sync
            def _(sp):
                def load(t, u):
                    reached(sp, s_m, t - RING + 1)
                    sp.dma_start(hs[:, u, :], edge_rows(d.eh, t)).then_inc(s_hs[u], 16)
                    reached(sp, s_yx, t - RING + 1)
                    sp.dma_start(hd[:, u, :], edge_rows(d.ed, t)).then_inc(s_hd[u], 16)

                def store(t, u):
                    sp.wait_ge(s_h1, t + 1)
                    sp.dma_start(edge_rows(d.e1, t), o[:, u, :]).then_inc(s_st[u], 16)

                pipeline(sp, ET, [(0, load), (8, store)])
                drained(sp, s_st, ET)

            @block.gpsimd
            def _(pool):
                def own_row(t, u):
                    pool.wait_ge(s_hd[u], nth(t, u))
                    reached(pool, s_m2, t - 3)
                    pool.tensor_tensor(heads(own[:, u % 4, :]), heads(hd[:, u, 0:F]), wide(r.self_logit[:, bass.ds(t, 1), :]),
                                       ALU.mult).then_inc(s_own, 1)

                def add_x(t, u):
                    pool.wait_ge(s_y, t + 1)
                    pool.tensor_tensor(y[:, u % 4, 1, :], y[:, u % 4, 0, :], hd[:, u, F + ATT:], ALU.add).then_inc(s_yx, 1)

                def scatter(t, u):
                    pool.wait_ge(s_h1, t + 1)
                    last.scatter(pool, d.t1, o[:, u, :], t, u, s_w)

                pipeline(pool, ET, [(0, own_row), (4, add_x), (8, scatter)])
                drained(pool, s_w, ET)

            @block.vector
            def _(dve):
                seg.clear(dve)

                def weigh(t, u):
                    dve.wait_ge(s_hs[u], nth(t, u))
                    reached(dve, s_m2, t - 3)
                    dve.tensor_tensor(heads(m[:, u % 4, 0, :]), heads(hs[:, u, :]), wide(r.logit[:, bass.ds(t, 1), :]),
                                      ALU.mult).then_inc(s_m, 1)

                def add_own(t, u):
                    dve.wait_ge(s_m, t + 1)
                    dve.wait_ge(s_own, t + 1)
                    reached(dve, seg.s_sum, t - 3)
                    dve.tensor_tensor(m[:, u % 4, 1, :], m[:, u % 4, 0, :], own[:, u % 4, :], ALU.add).then_inc(s_m2, 1)

                def stats_b(t, u):
                    dve.wait_ge(s_mm, t + 1)
                    nb.stats(dve, lambda n: px[:, u % 4, 0:F], t, u)

                def affine(t, u):
                    dve.wait_ge(nb.s_rs, t + 1)
                    reached(dve, s_yx, t - 3)
                    dve.scalar_tensor_tensor(y[:, u % 4, 0, :], px[:, u % 4, 0:F], nb.rs[:, u % 4, 0:1], r.gamma[:, :],
                                             ALU.mult, ALU.mult).then_inc(s_y, 1)

                def add_beta(t, u):
                    dve.wait_ge(s_yx, t + 1)
                    reached(dve, s_w[u], nth(t, u) - 16)
                    reached(dve, s_st[u], nth(t, u) - 16)
                    dve.tensor_tensor(o[:, u, 0:F], y[:, u % 4, 1, :], r.beta[:, :], ALU.add).then_inc(s_x1, 1)

                def stats_c(t, u):
                    dve.wait_ge(s_x1, t + 1)
                    nn.stats(dve, lambda n: o[:, u, 0:F], t, u)

                on = lambda step: lambda t, u: step(dve, t, u)
                pipeline(dve, ET, [
                    (1, lambda t, u: seg.follow(dve, s_mm, t, u)), (0, weigh), (3, on(nb.inverse)), (6, on(nn.inverse)),
                    (0, add_own), (5, add_beta), (3, affine), (6, on(nn.shift)), (2, stats_b), (5, stats_c),
                    (2, on(nb.aggregate)), (4, lambda t, u: last.stage(dve, t, u, s_w)), (5, on(nn.aggregate))])

            @block.scalar
            def _(act):
                def relu(t, u):
                    nn.relu(act, lambda n: o[:, u, F:], lambda n: o[:, u, 0:F], t, u).then_inc(s_h1, 1)

                pipeline(act, ET, [(3, lambda t, u: nb.root(act, r, t, u)), (6, lambda t, u: nn.root(act, r, t, u)),
                                   (0, lambda t, u: seg.widen(act, t, u)), (6, relu)])

            @block.tensor
            def _(pe):
                def sums(t, u):
                    pe.wait_ge(s_m2, t + 1)
                    seg.sum(pe, (m[:, u % 4, 1, :],), t, u)

                def project(t, u):
                    pe.wait_ge(seg.s_st, t + 2)
                    reached(pe, s_y, t - 3)
                    pe.matmul(px[:, u % 4, 0:F], seg.st[:, u % 4, 0, :], r.projc[:, :], start=True, stop=False)
                    pe.matmul(px[:, u % 4, 0:F], r.ones3[:, :], r.bias3[:, C0:C0 + F], start=False, stop=True).then_inc(s_mm, 1)

                pipeline(pe, ET, [(1, project), (0, sums)])


def edge_pass_1(nc, d, r):
    with Pass(nc, "e1") as k:
        g = k.sb("g", [P, RING, T1W])
        t1 = k.sb("t1", [P, RING, T1W])
        ht = k.sb("ht", [P, 4, F])
        dg = k.sb("dg", [P, 4])
        q = k.sb("q", [P, 4, F])
        o = k.sb("o", [P, RING, T1W])
        seg = SegmentSum(k, r, 2)
        nn = Norm(k, "c")
        src, last = Indices(k, "src", r.src), Indices(k, "last", r.last)
        pt = k.ps("pt", [P, 2, 512])
        po = k.ps("po", [P, 4, 512])
        s_g, s_t1, s_w, s_st = k.ring("g"), k.ring("t1_"), k.ring("w"), k.ring("st")
        s_tr, s_ht, s_mm, s_dg, s_q, s_x2, s_h2 = (k.sem(x) for x in ("tr", "ht", "mm", "dg", "q", "x2", "h2"))
        with nc.Block() as block:
            @block.sync
            def _(sp):
                def load(t, u):
                    reached(sp, s_tr, t - RING + 1)
                    reached(sp, s_q, t - RING + 1)
                    sp.dma_start(t1[:, u, :], edge_rows(d.e1, t)).then_inc(s_t1[u], 16)

                def store(t, u):
                    sp.wait_ge(s_h2, t + 1)
                    sp.dma_start(edge_rows(d.e2, t), o[:, u, :]).then_inc(s_st[u], 16)

                pipeline(sp, ET, [(0, load), (9, store)])
                drained(sp, s_st, ET)

            @block.gpsimd
            def _(pool):
                def gather(t, u):
                    reached(pool, seg.s_sum, t - RING + 1)
                    src.gather(pool, g[:, u, :], d.t1, t, u, s_g)

                def scatter(t, u):
                    pool.wait_ge(s_h2, t + 1)
                    last.scatter(pool, d.h2, o[:, u, F:], t, u, s_w)

                pipeline(pool, ET, [(0, gather), (9, scatter)])
                drained(pool, s_w, ET)

            @block.vector
            def _(dve):
                seg.clear(dve)

                def degree(t, u):
                    dve.wait_ge(s_mm, t + 1)
                    reached(dve, s_q, t - 3)
                    dve.tensor_copy(dg[:, u % 4:u % 4 + 1], po[:, u % 4, 3 * F:3 * F + 1]).then_inc(s_dg, 1)

                def weigh(t, u):
                    dve.wait_ge(s_dg, t + 1)
                    dve.scalar_tensor_tensor(q[:, u % 4, :], po[:, u % 4, F:2 * F], dg[:, u % 4:u % 4 + 1], t1[:, u, 0:F],
                                             ALU.mult, ALU.add)
                    dve.reciprocal(r.rdeg[:, bass.ds(t, 1)], dg[:, u % 4:u % 4 + 1]).then_inc(s_q, 1)

                def add(t, u):
                    dve.wait_ge(s_q, t + 1)
                    reached(dve, s_w[u], nth(t, u) - 16)
                    reached(dve, s_st[u], nth(t, u) - 16)
                    dve.tensor_tensor(o[:, u, 0:F], q[:, u % 4, :], po[:, u % 4, 0:F], ALU.add).then_inc(s_x2, 1)

                def stats(t, u):
                    dve.wait_ge(s_x2, t + 1)
                    nn.stats(dve, lambda n: o[:, u, 0:F], t, u)

                on = lambda step: lambda t, u: step(dve, t, u)
                pipeline(dve, ET, [
                    (6, stats), (0, lambda t, u: src.stage(dve, t, u, s_g)), (5, degree), (6, on(nn.aggregate)),
                    (3, lambda t, u: seg.follow(dve, s_mm, t, u)), (5, weigh), (7, on(nn.inverse)),
                    (5, lambda t, u: last.stage(dve, t, u, s_w)), (7, on(nn.shift)), (5, add)])

            @block.scalar
            def _(act):
                def turned(t, u):
                    act.wait_ge(s_tr, t + 1)
                    reached(act, s_mm, t - 3)
                    act.activation(ht[:, u % 4, :], pt[:, u % 2, 0:F], ACT.Copy).then_inc(s_ht, 1)

                def relu(t, u):
                    nn.relu(act, lambda n: o[:, u, F:], lambda n: o[:, u, 0:F], t, u).then_inc(s_h2, 1)

                pipeline(act, ET, [(5, lambda t, u: nn.root(act, r, t, u)), (0, lambda t, u: seg.widen(act, t, u)), (0, turned),
                                   (6, relu)])

            @block.tensor
            def _(pe):
                def turn(t, u):
                    pe.wait_ge(s_t1[u], nth(t, u))
                    reached(pe, s_ht, t - 1)
                    pe.transpose(pt[:, u % 2, 0:F], t1[:, u, F:], r.ident[:, :]).then_inc(s_tr, 1)

                def sums(t, u):
                    pe.wait_ge(s_g[u], nth(t, u))
                    seg.sum(pe, (g[:, u, F:], r.ones[:, :]), t, u)

                def product(t, u):
                    pe.wait_ge(s_ht, t + 1)
                    pe.wait_ge(seg.s_st, t + 2)
                    reached(pe, s_x2, t - 3)
                    pe.matmul(po[:, u % 4, 0:2 * F], ht[:, u % 4, :], r.wu[:, :], start=True, stop=False)
                    pe.matmul(po[:, u % 4, 0:2 * F], r.ones3[:, :], r.bias3[:, B1:B2], start=False, stop=False)
                    pe.matmul(po[:, u % 4, 0:F], seg.st[:, u % 4, 0, :], r.wa[:, :], start=False, stop=True)
                    pe.matmul(po[:, u % 4, 3 * F:3 * F + 1], seg.st[0:1, u % 4, 1, :], r.ones[0:1, 0:1], start=True, stop=True)\
                      .then_inc(s_mm, 1)

                pipeline(pe, ET, [(0, turn), (0, sums), (2, product)])


def edge_pass_2b(nc, d, r):
    with Pass(nc, "e2b") as k:
        e = k.sb("e", [P, RING, F])
        x2 = k.sb("x2", [P, RING, T1W])
        m = k.sb("m", [P, 4, F])
        o = k.sb("o", [P, RING, T1W])
        seg = SegmentSum(k, r)
        nn = Norm(k, "c")
        last = Indices(k, "last", r.last)
        px = k.ps("px", [P, 2, 512])
        s_e, s_x2, s_w, s_st = k.ring("e"), k.ring("x2_"), k.ring("w"), k.ring("st")
        s_m, s_tr, s_x3, s_h3 = (k.sem(x) for x in ("m", "tr", "x3", "h3"))
        heads = lambda v: v.rearrange("p (h d) -> p h d", d=D2)
        wide = lambda t: r.logit[:, bass.ds(t, 1), 0:H2].rearrange("p a h -> p (a h)").unsqueeze(2).to_broadcast([P, H2, D2])
        with nc.Block() as block:
            @block.sync
            def _(sp):
                def load(t, u):
                    reached(sp, s_m, t - RING + 1)
                    sp.dma_start(e[:, u, :], edge_rows(d.eh, t)).then_inc(s_e[u], 16)
                    reached(sp, s_x3, t - RING + 1)
                    sp.dma_start(x2[:, u, :], edge_rows(d.e2, t)).then_inc(s_x2[u], 16)

                def store(t, u):
                    sp.wait_ge(s_h3, t + 1)
                    sp.dma_start(edge_rows(d.e3, t), o[:, u, :]).then_inc(s_st[u], 16)

                pipeline(sp, ET, [(0, load), (7, store)])
                drained(sp, s_st, ET)

            @block.gpsimd
            def _(pool):
                def scatter(t, u):
                    pool.wait_ge(s_h3, t + 1)
                    last.scatter(pool, d.h2, o[:, u, F:], t, u, s_w)

                pipeline(pool, ET, [(0, scatter)])
                drained(pool, s_w, ET)

            @block.vector
            def _(dve):
                seg.clear(dve)

                def weigh(t, u):
                    dve.wait_ge(s_e[u], nth(t, u))
                    reached(dve, seg.s_sum, t - 3)
                    dve.tensor_tensor(heads(m[:, u % 4, :]), heads(e[:, u, :]), wide(t), ALU.mult).then_inc(s_m, 1)

                def add(t, u):
                    dve.wait_ge(s_tr, t + 1)
                    dve.wait_ge(s_x2[u], nth(t, u))
                    reached(dve, s_w[u], nth(t, u) - 16)
                    reached(dve, s_st[u], nth(t, u) - 16)
                    dve.tensor_tensor(o[:, u, 0:F], x2[:, u, 0:F], px[:, u % 2, 0:F], ALU.add).then_inc(s_x3, 1)

                def stats(t, u):
                    dve.wait_ge(s_x3, t + 1)
                    nn.stats(dve, lambda n: o[:, u, 0:F], t, u)

                on = lambda step: lambda t, u: step(dve, t, u)
                pipeline(dve, ET, [
                    (1, lambda t, u: seg.follow(dve, s_tr, t, u)), (0, weigh), (3, on(nn.inverse)), (2, add),
                    (2, lambda t, u: last.stage(dve, t, u, s_w)), (3, on(nn.shift)), (2, stats), (2, on(nn.aggregate))])

            @block.scalar
            def _(act):
                def relu(t, u):
                    nn.relu(act, lambda n: o[:, u, F:], lambda n: o[:, u, 0:F], t, u).then_inc(s_h3, 1)

                pipeline(act, ET, [(3, lambda t, u: nn.root(act, r, t, u)), (0, lambda t, u: seg.widen(act, t, u)), (3, relu)])

            @block.tensor
            def _(pe):
                def sums(t, u):
                    pe.wait_ge(s_m, t + 1)
                    seg.sum(pe, (m[:, u % 4, :],), t, u)

                def turn(t, u):
                    pe.wait_ge(seg.s_st, t + 2)
                    reached(pe, s_x3, t - 1)
                    pe.transpose(px[:, u % 2, 0:F], seg.st[:, u % 4, 0, :], r.ident[:, :]).then_inc(s_tr, 1)

                pipeline(pe, ET, [(1, turn), (0, sums)])


def edge_conv(nc, d, r, name, gather, own, wn, bias, out, own_at=0, out_own=None, score=False, masked=False, add=None):
    cols = F + 1 if score else F
    relu = not score and add is None
    with Pass(nc, name) as k:
        gw, ow = gather.shape[1], own.shape[1]
        ga = k.sb("ga", [P, RING, 2, max(gw, ow)])
        x3 = k.sb("x3", [P, RING, F]) if add is not None else None
        km = k.sb("km", [P, 4, 2, 2]) if masked else None
        m = k.sb("m", [P, 4, 2, F]) if masked else None
        ht = k.sb("ht", [P, 4, F])
        q = k.sb("q", [P, 4, 2, cols])
        y = k.sb("y", [P, 4, F]) if not score else None
        z = k.sb("z", [P, 4, 3, 2]) if masked else None
        o = k.sb("o", [P, RING, out.shape[1]])
        seg = SegmentSum(k, r)
        src, last = Indices(k, "src", r.src), Indices(k, "last", r.last)
        pt = k.ps("pt", [P, 2, 512])
        po = k.ps("po", [P, 2, 512])
        s_g, s_a, s_x3, s_w, s_st = k.ring("g"), k.ring("a"), k.ring("x3_"), k.ring("w"), k.ring("st")
        names = ("pre", "k0", "k1", "m", "tr", "ht", "mm", "q", "y", "ex", "e1", "z", "out")
        s_pre, s_k0, s_k1, s_m, s_tr, s_ht, s_mm, s_q, s_y, s_ex, s_e1, s_z, s_out = (k.sem(x) for x in names)
        with nc.Block() as block:
            @block.sync
            def _(sp):
                def load(t, u):
                    reached(sp, s_m if masked else s_tr, t - RING + 1)
                    sp.dma_start(ga[:, u, 1, 0:ow], edge_rows(own, t)).then_inc(s_a[u], 16)
                    if add is not None:
                        reached(sp, s_out, t - RING + 1)
                        sp.dma_start(x3[:, u, :], edge_rows(add, t)[:, 0:F]).then_inc(s_x3[u], 16)

                def store(t, u):
                    sp.wait_ge(s_out, t + 1)
                    sp.dma_start(edge_rows(out_own, t), o[:, u, :]).then_inc(s_st[u], 16)

                pipeline(sp, ET, [(0, load)] + ([(9 if masked else 8, store)] if out_own is not None else []))
                if out_own is not None:
                    drained(sp, s_st, ET)

            @block.gpsimd
            def _(pool):
                def fetch(t, u):
                    reached(pool, s_m if masked else seg.s_sum, t - RING + 1)
                    src.gather(pool, ga[:, u, 0, 0:gw], gather, t, u, s_g)

                def scatter(t, u):
                    pool.wait_ge(s_out, t + 1)
                    last.scatter(pool, out, o[:, u, :], t, u, s_w)

                pipeline(pool, ET, [(0, fetch), (10 if masked else 8, scatter)])
                drained(pool, s_w, ET)

            @block.vector
            def _(dve):
                seg.clear(dve)
                if score:
                    dve.memset(o[:, :, F:], 0.0).then_inc(s_pre, 1)
                    dve.wait_ge(s_pre, 1)

                def mask(t, u):
                    dve.wait_ge(s_z, t + 1)
                    dve.scalar_tensor_tensor(km[:, u % 4, 0, :].unsqueeze(1), z[:, u % 4, 2:3, :], r.thr[:, 0:1],
                                             r.below[:, bass.ds(t, 1), :], ALU.is_equal, ALU.mult).then_inc(s_k0, 1)

                def mask_too(t, u):
                    dve.wait_ge(s_k0, t + 1)
                    dve.scalar_tensor_tensor(km[:, u % 4, 1, :], z[:, u % 4, 2, :], r.thr[:, 0:1], km[:, u % 4, 0, :],
                                             ALU.is_gt, ALU.add).then_inc(s_k1, 1)

                def kept(t, u):
                    dve.wait_ge(s_k1, t + 1)
                    reached(dve, seg.s_sum, t - 3)
                    reached(dve, s_tr, t - 3)
                    for n in range(2):
                        ins = dve.tensor_scalar(m[:, u % 4, n, :], ga[:, u, n, 0:F], km[:, u % 4, 1, n:n + 1], None, ALU.mult)
                    ins.then_inc(s_m, 1)

                def weigh(t, u):
                    dve.wait_ge(s_mm, t + 1)
                    dve.tensor_scalar(q[:, u % 4, 0, :], po[:, u % 2, 256:256 + cols], r.rdeg[:, bass.ds(t, 1)], None, ALU.mult)\
                       .then_inc(s_q, 1)

                def combine(t, u):
                    dve.wait_ge(s_q, t + 1)
                    if score:
                        reached(dve, s_w[u], nth(t, u) - 16)
                        reached(dve, s_st[u], nth(t, u) - 16)
                    else:
                        reached(dve, s_out, t - 3)
                    dve.tensor_tensor(o[:, u, 0:cols] if score else y[:, u % 4, :], q[:, u % 4, 0, :], po[:, u % 2, 0:cols],
                                      ALU.add).then_inc(s_out if score else s_y, 1)

                def plus_x3(t, u):
                    dve.wait_ge(s_y, t + 1)
                    dve.wait_ge(s_x3[u], nth(t, u))
                    reached(dve, s_w[u], nth(t, u) - 16)
                    dve.tensor_tensor(o[:, u, :], y[:, u % 4, :], x3[:, u, :], ALU.add).then_inc(s_out, 1)

                def plus_one(t, u):
                    dve.wait_ge(s_ex, t + 1)
                    dve.tensor_scalar(z[:, u % 4, 1, :], z[:, u % 4, 0, :], 1.0, None, ALU.add).then_inc(s_e1, 1)

                def sigmoid(t, u):
                    dve.wait_ge(s_e1, t + 1)
                    dve.reciprocal(z[:, u % 4, 2, :], z[:, u % 4, 1, :]).then_inc(s_z, 1)

                convolve = [(lambda t, u: seg.follow(dve, s_mm, t, u)), combine, lambda t, u: last.stage(dve, t, u, s_w)]
                stages = [(0, lambda t, u: src.stage(dve, t, u, s_g))]
                if masked:
                    stages += [(4, plus_one), (9, weigh), (4, sigmoid), (7, convolve[0]), (5, mask), (9, convolve[1]),
                               (5, mask_too), (9, convolve[2]), (5, kept)]
                else:
                    stages += [(6, weigh), (4, convolve[0]), (6, convolve[1]), (6, convolve[2])]
                if add is not None:
                    stages += [(7, plus_x3)]
                pipeline(dve, ET, stages)

            @block.scalar
            def _(act):
                def turned(t, u):
                    act.wait_ge(s_tr, t + 1)
                    reached(act, s_mm, t - 3)
                    act.activation(ht[:, u % 4, :], pt[:, u % 2, 0:F], ACT.Copy).then_inc(s_ht, 1)

                def finish(t, u):
                    act.wait_ge(s_y, t + 1)
                    reached(act, s_w[u], nth(t, u) - 16)
                    reached(act, s_st[u], nth(t, u) - 16)
                    act.activation(o[:, u, :], y[:, u % 4, :], ACT.Relu).then_inc(s_out, 1)

                def exp(t, u):
                    act.wait_ge(s_g[u], nth(t, u))
                    act.wait_ge(s_a[u], nth(t, u))
                    reached(act, s_m, t - 3)
                    act.activation(z[:, u % 4, 0, :], ga[:, u, :, F], ACT.Exp, scale=-1.0).then_inc(s_ex, 1)

                widen = lambda t, u: seg.widen(act, t, u)
                if masked:
                    pipeline(act, ET, [(8, finish), (0, exp), (0, widen), (2, turned)])
                else:
                    pipeline(act, ET, ([(5, finish)] if relu else []) + [(0, widen), (0, turned)])

            @block.tensor
            def _(pe):
                def turn(t, u):
                    if masked:
                        pe.wait_ge(s_m, t + 1)
                    else:
                        pe.wait_ge(s_a[u], nth(t, u))
                    reached(pe, s_ht, t - 1)
                    pe.transpose(pt[:, u % 2, 0:F], m[:, u % 4, 1, :] if masked else ga[:, u, 1, own_at:own_at + F], r.ident[:, :])\
                      .then_inc(s_tr, 1)

                def sums(t, u):
                    if not masked:
                        pe.wait_ge(s_g[u], nth(t, u))
                    seg.sum(pe, (m[:, u % 4, 0, :] if masked else ga[:, u, 0, 0:F],), t, u)

                def product(t, u):
                    pe.wait_ge(s_ht, t + 1)
                    pe.wait_ge(seg.s_st, t + 2)
                    reached(pe, s_out if score else s_y, t - 1)
                    at = B3 + bias * (F + 1)
                    pe.matmul(po[:, u % 2, 0:cols], ht[:, u % 4, :], r.w3[:, wn, 0:cols], start=True, stop=False)
                    pe.matmul(po[:, u % 2, 0:cols], r.ones3[:, :], r.bias3[:, at:at + cols], start=False, stop=True)
                    pe.matmul(po[:, u % 2, 256:256 + cols], seg.st[:, u % 4, 0, :], r.w3[:, wn + 1, 0:cols], start=True, stop=True)\
                      .then_inc(s_mm, 1)

                pipeline(pe, ET, [(0, turn), (0, sums), (2, product)])


def choose(nc, d, r):
    with Pass(nc, "top") as k:
        zf = r.z[:, :, :].rearrange("p g j -> p (g j)")
        n = NGROUPS * J
        ids = k.sb("ids", [P, n], I32)
        idt = k.sb("idt", [P, 1], I32)
        idf = k.sb("idf", [P, n])
        junk = k.sb("junk", [P, 3, n])
        far = k.sb("far", [P, n])
        bit = k.sb("bit", [P, 2, 3], I32)
        cand = k.sb("cand", [P, 3], I32)
        yes = k.sb("yes", [P, 3], I32)
        cnt = k.sb("cnt", [P, 3])
        need = k.sb("need", [P, 1])
        step = k.sb("step", [P, 1])
        bound = k.sb("bound", [P, 1])
        fit = k.sb("fit", [P, 1])
        tot = k.ps("tot", [P, 512])
        thr = r.thr[:, 0:1]
        thr_bits = thr.bitcast(I32)
        s_id, s_cnt, s_tot, s_v = (k.sem(x) for x in ("id", "cnt", "tot", "v"))
        VALUE_BITS, INDEX_BITS = 30, 17
        with nc.Block() as block:
            @block.gpsimd
            def _(pool):
                pool.iota(ids[:, :], pattern=[[GROUP, NGROUPS], [1, J]], base=0, channel_multiplier=J).then_inc(s_id, 1)
                pool.iota(idt[:, :], pattern=[[0, 1]], base=FULL * GROUP, channel_multiplier=1).then_inc(s_id, 1)

            @block.tensor
            def _(pe):
                with pe.Fori(0, VALUE_BITS // 2 + 1 + INDEX_BITS) as i:
                    pe.wait_ge(s_cnt, i + 1)
                    pe.matmul(tot[:, 0:3], r.ones[:, :], cnt[:, :], start=True, stop=True).then_inc(s_tot, 1)

            @block.vector
            def _(dve):
                FIRST, EACH, SECOND = 2, 6, 7

                def link(ins, value):
                    ins.then_inc(s_v, 1)
                    dve.wait_ge(s_v, value)

                dve.memset(thr, 0.0)
                dve.memset(cnt[:, :], 0.0)
                low = 1 << (VALUE_BITS - 2)
                for n, v in enumerate((1, 2, 3, 1, 3, 1)):
                    ins = dve.memset(bit[:, n // 3, n % 3:n % 3 + 1], v * low)
                link(ins, 1)
                dve.wait_ge(s_id, 2)
                dve.tensor_copy(idf[:, :], ids[:, :])
                link(dve.tensor_copy(junk[:, 0, 0:1], idt[:, :]), 2)
                with dve.Fori(0, VALUE_BITS // 2) as i:
                    at = FIRST + i * EACH
                    link(dve.tensor_tensor(cand[:, :], thr_bits.to_broadcast([P, 3]), bit[:, 0, :], ALU.bitwise_or), at + 1)
                    for n in range(3):
                        ins = dve.tensor_scalar(junk[:, n, :], zf, cand[:, n:n + 1].bitcast(F32), 0.0, ALU.is_ge, ALU.add,
                                                accum_out=cnt[:, n:n + 1])
                    link(ins, at + 2)
                    dve.sem_inc(s_cnt, 1)
                    dve.wait_ge(s_tot, i + 1)
                    link(dve.tensor_scalar(yes[:, :], tot[:, 0:3], float(KEEP), -1.0, ALU.is_ge, ALU.mult), at + 3)
                    link(dve.tensor_tensor(yes[:, :], yes[:, :], bit[:, 1, :], ALU.bitwise_and), at + 4)
                    dve.tensor_tensor(thr_bits, thr_bits, yes[:, 0:1], ALU.bitwise_xor)
                    link(dve.tensor_tensor(yes[:, 1:2], yes[:, 1:2], yes[:, 2:3], ALU.bitwise_xor), at + 5)
                    dve.tensor_tensor(thr_bits, thr_bits, yes[:, 1:2], ALU.bitwise_xor)
                    link(dve.tensor_scalar(bit[:, :, :], bit[:, :, :], 2, None, ALU.logical_shift_right), at + 6)
                at = FIRST + VALUE_BITS // 2 * EACH
                link(dve.tensor_scalar(junk[:, 0, :], zf, thr, 0.0, ALU.is_gt, ALU.add, accum_out=cnt[:, 0:1]), at + 1)
                dve.sem_inc(s_cnt, 1)
                dve.wait_ge(s_tot, VALUE_BITS // 2 + 1)
                dve.tensor_scalar(need[:, :], tot[:, 0:1], -1.0, float(KEEP), ALU.mult, ALU.add)
                dve.memset(bound[:, :], 0.0)
                dve.memset(step[:, :], float(1 << (INDEX_BITS - 1)))
                link(dve.tensor_scalar(far[:, :], zf, thr, float(1 << 20), ALU.not_equal, ALU.mult), at + 2)
                link(dve.tensor_copy(idf[0:REST, FULL * J:FULL * J + 1], idt[0:REST, :]), at + 3)
                link(dve.tensor_tensor(far[:, :], far[:, :], idf[:, :], ALU.add), at + 4)
                at += 4
                with dve.Fori(0, INDEX_BITS) as i:
                    v = at + i * SECOND
                    link(dve.tensor_tensor(cand[:, 0:1].bitcast(F32), bound[:, :], step[:, :], ALU.add), v + 1)
                    link(dve.tensor_scalar(junk[:, 0, :], far[:, :], cand[:, 0:1].bitcast(F32), 0.0, ALU.is_lt, ALU.add,
                                           accum_out=cnt[:, 0:1]), v + 2)
                    dve.sem_inc(s_cnt, 1)
                    dve.wait_ge(s_tot, i + (VALUE_BITS // 2 + 2))
                    link(dve.tensor_tensor(fit[:, :], tot[:, 0:1], need[:, :], ALU.is_le), v + 3)
                    link(dve.tensor_tensor(fit[:, :], fit[:, :], step[:, :], ALU.mult), v + 4)
                    link(dve.tensor_tensor(bound[:, :], bound[:, :], fit[:, :], ALU.add), v + 5)
                    link(dve.tensor_scalar(step[:, :], step[:, :], 0.5, None, ALU.mult), v + 6)
                    link(dve.tensor_copy(fit[:, :], bound[:, :]), v + 7)
                at += INDEX_BITS * SECOND
                link(dve.tensor_scalar(far[:, :], far[:, :], bound[:, :], None, ALU.is_lt), at + 1)
                dve.scalar_tensor_tensor(r.keep[:, :], zf, thr, far[:, :], ALU.is_gt, ALU.add)
                dve.tensor_scalar(r.below[:, :, 0], r.srcf[:, :], bound[:, :], None, ALU.is_lt)
                dve.tensor_scalar(r.below[:, :, 1], r.dstf[:, :], bound[:, :], None, ALU.is_lt)




def main(nc, a, out):
    with ExitStack() as ctx:
        def sb(name, shape, dt=F32):
            return ctx.enter_context(nc.sbuf_tensor(name, shape, dt))
        d, r = Resident(), Resident()
        dram = lambda n, s, dt=F32: nc.dram_tensor(n, s, dt, kind="Internal").ap()
        d.dst = dram("dst_padded", (EPAD + CL + 2,), I32)
        d.hop = dram("chunk_values", (8, H0 * CH))
        d.src = dram("src_padded", (EPAD,), I32)
        d.t0 = dram("table0", (N, T0W))
        d.t1 = dram("table1", (N, T1W))
        d.x3 = dram("x3", (N, F))
        d.h2 = dram("h2", (N, F))
        d.g = dram("g_conv1", (N, F))
        d.hp = dram("h_scored", (N, HPW))
        d.up = dram("up_conv1", (N, F))
        d.parts = dram("bias_parts_list", (3, BIASES), BF16)
        d.e1 = dram("edge_x1_h1", (EPAD, T1W))
        d.e2 = dram("edge_x2_h2", (EPAD, T1W))
        d.e3 = dram("edge_x3_h3", (EPAD, T1W))
        d.eg = dram("edge_g", (EPAD, F))
        d.ehp = dram("edge_scored", (EPAD, HPW))
        d.eup = dram("edge_up", (EPAD, F))
        d.eh = dram("edge_source_rows", (EPAD, F))
        d.ed = dram("edge_target_rows", (EPAD, T0W))
        r.ident = sb("ident", [P, P])
        r.ones = sb("ones", [P, P])
        r.eps = sb("eps", [P, 1])
        r.src = sb("src_index", [P, ET], I32)
        r.dstg = sb("dst_index", [P, ET], I32)
        r.last = sb("last_index", [P, ET], I32)
        r.srcf = sb("src_float", [P, ET])
        r.dstf = sb("dst_float", [P, ET])
        r.rdeg = sb("degree_inverse", [P, ET])
        r.seg = sb("segments", [P, ET, P], BF16)
        r.goes_on = sb("goes_on", [P, ET, P], BF16)
        r.projc = sb("projc", [P, F])
        r.w0 = sb("w0", [P, T0W])
        r.bias = sb("bias", [1, BIASES])
        r.bias3 = sb("bias_parts", [3, BIASES], BF16)
        r.ones3 = sb("ones_parts", [3, P], BF16)
        r.c0, r.b1, r.b2 = r.bias[:, C0:B1], r.bias[:, B1:B2], r.bias[:, B2:B3]
        r.b3 = r.bias[:, B3:BIASES].rearrange("a (n f) -> a n f", n=4)
        r.gamma = sb("gamma", [P, F])
        r.beta = sb("beta", [P, F])
        r.wu = sb("wu", [P, 2 * F])
        r.wa = sb("wa", [P, F])
        r.ws = sb("ws", [P, F])
        r.wr = sb("wr", [P, F])
        r.we = sb("we", [P, F])
        r.attw = sb("attw", [P, H2, D2])
        r.attb = sb("attb", [P, 1])
        r.w3 = sb("w3", [P, 8, F + 1])
        r.logit = sb("logit", [P, ET, H0])
        r.self_logit = sb("self_logit", [P, ET, H0])
        r.z = sb("score", [P, FULL + 1, J])
        r.thr = sb("threshold", [P, 2])
        r.keep = sb("keep", [P, NGROUPS * J])
        r.below = sb("below", [P, ET, 2])
        passes(nc, a, d, r, out)


def passes(nc, a, d, r, out):
    setup(nc, a, d, r)
    node_pass_0(nc, a, d, r)
    node_pass_1_edge_pass_0a(nc, d, r)
    softmax_weights(nc, d, r, "sm0", own_loop=True)
    edge_pass_0b(nc, d, r)
    edge_pass_1(nc, d, r)
    edge_pass_2a(nc, a, d, r)
    softmax_weights(nc, d, r, "sm2", own_loop=False)
    edge_pass_2b(nc, d, r)
    edge_conv(nc, d, r, "e3", gather=d.h2, own=d.e3, own_at=F, wn=0, bias=0, out=d.g, out_own=d.eg)
    edge_conv(nc, d, r, "e4", gather=d.g, own=d.eg, wn=2, bias=1, out=d.hp, out_own=d.ehp, score=True)
    collect(nc, d, r)
    choose(nc, d, r)
    node_pass_2(nc, d, r, out)
    edge_conv(nc, d, r, "e5", gather=d.hp, own=d.ehp, wn=4, bias=2, out=d.up, out_own=d.eup, masked=True)
    edge_conv(nc, d, r, "e6", gather=d.up, own=d.eup, wn=6, bias=3, out=out, add=d.e3)


_OUTS = [((N, F), 'float32')]


def kernel(**inputs):
    import numpy as _np
    import concourse.bacc as _bacc
    from concourse import mybir as _mybir
    from concourse.bass_utils import run_bass_kernel_spmd as _run

    nc = _bacc.Bacc("TRN2", target_bir_lowering=False, num_devices=1)
    arrays, args = {}, {}
    for name, value in inputs.items():
        v = _np.ascontiguousarray(value)
        arrays[f"in_{name}"] = v
        args[name] = nc.dram_tensor(f"in_{name}", v.shape, _mybir.dt.from_np(v.dtype), kind="ExternalInput").ap()
    out = nc.dram_tensor("out_x", (N, F), _mybir.dt.float32, kind="ExternalOutput").ap()
    main(nc, args, out)
    got = _run(nc, [arrays], core_ids=[0])
    return got.results[0]["out_x"]
```
